# Optimizing a Trainium2 kernel written in Bass

```python
import numpy as np
import jax
import jax.numpy as jnp

def _softmax(x, axis=-1):
    return jax.nn.softmax(x, axis=axis)

def _gelu(x):
    return jax.nn.gelu(x, approximate=True)

def _silu(x):
    return jax.nn.silu(x)

def _sigmoid(x):
    return jax.nn.sigmoid(x)

def _layernorm(x, axis=-1, eps=1e-05):
    m = jnp.mean(x, axis=axis, keepdims=True)
    v = jnp.var(x, axis=axis, keepdims=True)
    return (x - m) / jnp.sqrt(v + eps)

def _scatter_add(tgt, idx, src, axis=0):
    return tgt.at[idx].add(src)

def _segment_sum(src, seg, n):
    return jax.ops.segment_sum(src, seg, n)
kernel_name = 'mk_sandwich_d1_jaxref_r8_5503b9'

def setup_inputs(seed: int=0):
    np.random.seed(seed)
    _w = jnp.asarray

    def _L0_attn_setup():
        import jax, jax.numpy as jnp
        import numpy as np
        from jax import lax
        BLOCK_LEN = 128
        NEG_INF = -1000000000.0
        key = jax.random.key(seed)
        ks = jax.random.split(key, 8)
        N, L, Dm = (2, 1024, 512)
        W, H, dh = (128, 16, 64)
        s = lambda fan: 1.0 / np.sqrt(fan)
        return {'inputs': jax.random.normal(ks[0], (N, L, Dm), jnp.float32), 'conv_w': jax.random.normal(ks[1], (3, Dm, 3 * W), jnp.float32) * s(3 * Dm), 'conv_b': jnp.zeros((3 * W,), jnp.float32), 'wq': jax.random.normal(ks[2], (W, H, dh), jnp.float32) * s(W), 'bq': jnp.zeros((H, dh), jnp.float32), 'wk': jax.random.normal(ks[3], (W, H, dh), jnp.float32) * s(W), 'bk': jnp.zeros((H, dh), jnp.float32), 'wv': jax.random.normal(ks[4], (W, H, dh), jnp.float32) * s(W), 'bv': jnp.zeros((H, dh), jnp.float32), 'wo': jax.random.normal(ks[5], (H, dh, W), jnp.float32) * s(H * dh), 'bo': jnp.zeros((W,), jnp.float32), 'proj_w': jax.random.normal(ks[6], (W, Dm), jnp.float32) * s(W), 'proj_b': jnp.zeros((Dm,), jnp.float32)}
    _L0_attn_in = _L0_attn_setup()

    def _L0_ffn_setup():
        import jax, jax.numpy as jnp
        import numpy as np
        IMAGE_START_POS = 34
        Q_START = IMAGE_START_POS + 72 + 1
        Q_END = -1
        LORA_ALPHA = 32
        LORA_RANK = 16
        SCALING = LORA_ALPHA / LORA_RANK
        key = jax.random.key(seed)
        ks = jax.random.split(key, 7)
        B_, S, D, O, E, R = (4, 256, 512, 512, 8, LORA_RANK)
        s = 0.02
        return {'x': jax.random.normal(ks[0], (B_, S, D), jnp.float32), 'W': jax.random.normal(ks[1], (O, D), jnp.float32) * s, 'b': jax.random.normal(ks[2], (O,), jnp.float32) * s, 'A': jax.random.normal(ks[3], (E, R, D), jnp.float32) * s, 'B': jax.random.normal(ks[4], (E, O, R), jnp.float32) * s, 'router_W': jax.random.normal(ks[5], (E, D), jnp.float32) * s, 'router_b': jax.random.normal(ks[6], (E,), jnp.float32) * s}
    _L0_ffn_in = _L0_ffn_setup()
    _d = {'L0_attn_inputs': _L0_attn_in['inputs'], 'L0_attn_conv_w': _L0_attn_in['conv_w'], 'L0_attn_conv_b': _L0_attn_in['conv_b'], 'L0_attn_wq': _L0_attn_in['wq'], 'L0_attn_bq': _L0_attn_in['bq'], 'L0_attn_wk': _L0_attn_in['wk'], 'L0_attn_bk': _L0_attn_in['bk'], 'L0_attn_wv': _L0_attn_in['wv'], 'L0_attn_bv': _L0_attn_in['bv'], 'L0_attn_wo': _L0_attn_in['wo'], 'L0_attn_bo': _L0_attn_in['bo'], 'L0_attn_proj_w': _L0_attn_in['proj_w'], 'L0_attn_proj_b': _L0_attn_in['proj_b'], 'L0_ffn_W': _L0_ffn_in['W'], 'L0_ffn_b': _L0_ffn_in['b'], 'L0_ffn_A': _L0_ffn_in['A'], 'L0_ffn_B': _L0_ffn_in['B'], 'L0_ffn_router_W': _L0_ffn_in['router_W'], 'L0_ffn_router_b': _L0_ffn_in['router_b']}
    _x0 = _d['L0_attn_inputs']
    _d['L0_attn_inputs'] = jax.random.normal(jax.random.fold_in(jax.random.key(seed), 1), (1, 2048, 512), dtype=_x0.dtype)
    del _x0
    return _d

def reference(L0_attn_inputs, L0_attn_conv_w, L0_attn_conv_b, L0_attn_wq, L0_attn_bq, L0_attn_wk, L0_attn_bk, L0_attn_wv, L0_attn_bv, L0_attn_wo, L0_attn_bo, L0_attn_proj_w, L0_attn_proj_b, L0_ffn_W, L0_ffn_b, L0_ffn_A, L0_ffn_B, L0_ffn_router_W, L0_ffn_router_b):

    def _L0_attn_ref(inputs, conv_w, conv_b, wq, bq, wk, bk, wv, bv, wo, bo, proj_w, proj_b):
        import jax, jax.numpy as jnp
        import numpy as np
        from jax import lax
        BLOCK_LEN = 128
        NEG_INF = -1000000000.0
        N, L, Dm = inputs.shape
        x = lax.conv_general_dilated(inputs, conv_w, window_strides=(1,), padding='SAME', dimension_numbers=('NWC', 'WIO', 'NWC')) + conv_b
        q, k, v = jnp.split(x, 3, axis=-1)
        W_ = q.shape[-1]
        nb = L // BLOCK_LEN
        q = q.reshape(N * nb, BLOCK_LEN, W_)
        k = k.reshape(N * nb, BLOCK_LEN, W_)
        v = v.reshape(N * nb, BLOCK_LEN, W_)
        dh = wq.shape[-1]
        qh = jnp.einsum('btd,dhe->bthe', q, wq) + bq
        kh = jnp.einsum('btd,dhe->bthe', k, wk) + bk
        vh = jnp.einsum('btd,dhe->bthe', v, wv) + bv
        scale = 1.0 / jnp.sqrt(jnp.asarray(dh, qh.dtype))
        scores = jnp.einsum('bqhe,bkhe->bhqk', qh * scale, kh)
        causal = jnp.tril(jnp.ones((BLOCK_LEN, BLOCK_LEN), bool))
        scores = jnp.where(causal, scores, NEG_INF)
        p = jax.nn.softmax(scores, axis=-1)
        o = jnp.einsum('bhqk,bkhe->bqhe', p, vh)
        o = jnp.einsum('bqhe,hed->bqd', o, wo) + bo
        o = o.reshape(N, L, W_)
        return o @ proj_w + proj_b

    def _L0_ffn_ref(x, W, b, A, B, router_W, router_b):
        import jax, jax.numpy as jnp
        import numpy as np
        IMAGE_START_POS = 34
        Q_START = IMAGE_START_POS + 72 + 1
        Q_END = -1
        LORA_ALPHA = 32
        LORA_RANK = 16
        SCALING = LORA_ALPHA / LORA_RANK
        x_q = x[:, Q_START:Q_END, :]
        q = x_q.mean(axis=1)
        logits = q @ router_W.T + router_b
        routing = jax.nn.softmax(logits, axis=-1)
        base = x @ W.T + b
        t = jnp.einsum('bsd,erd->bser', x, A)
        lora = jnp.einsum('bser,eor,be->bso', t, B, routing) * SCALING
        return base + lora
    x = L0_attn_inputs
    x = x + _layernorm(_L0_attn_ref(_layernorm(x, axis=-1), L0_attn_conv_w, L0_attn_conv_b, L0_attn_wq, L0_attn_bq, L0_attn_wk, L0_attn_bk, L0_attn_wv, L0_attn_bv, L0_attn_wo, L0_attn_bo, L0_attn_proj_w, L0_attn_proj_b), axis=-1)
    x = x + _layernorm(_L0_ffn_ref(_layernorm(x, axis=-1), L0_ffn_W, L0_ffn_b, L0_ffn_A, L0_ffn_B, L0_ffn_router_W, L0_ffn_router_b), axis=-1)
    return x

_drawn_inputs = setup_inputs


def setup_inputs(seed=0):
    import zlib

    import numpy as np

    out = dict(_drawn_inputs(seed))
    spreads = {'L0_attn_conv_b': (0.0, 0.1),
     'L0_attn_bq': (0.0, 0.1),
     'L0_attn_bk': (0.0, 2.0),
     'L0_attn_bv': (0.0, 0.1),
     'L0_attn_bo': (0.0, 0.1),
     'L0_attn_proj_b': (0.0, 0.1)}
    factors = {'L0_ffn_router_W': 8.0, 'L0_ffn_router_b': 64.0}
    for name, (base, spread) in spreads.items():
        noise = np.random.default_rng([zlib.crc32(name.encode()), seed]).standard_normal(out[name].shape)
        drawn = base * np.exp(spread * noise) if base else spread * noise
        out[name] = jnp.asarray(drawn.astype(out[name].dtype))
    for name, factor in factors.items():
        out[name] = (out[name] * factor).astype(out[name].dtype)
    return out
```

```python
from contextlib import ExitStack

import concourse.bass as bass
from concourse import mybir

F32 = mybir.dt.float32
F32R = mybir.dt.float32r
BF16 = mybir.dt.bfloat16
ALU = mybir.AluOpType
ACT = mybir.ActivationFunctionType
AX_X = mybir.AxisListType.X

P = 128
EPS = 1e-5
MASKED = -1e9
LORA_SCALING = 2.0
Q_START, Q_END = 107, -1


def attention_ffn_sandwich(
    nc: bass.Bass, x: bass.AP, conv_w: bass.AP, conv_b: bass.AP,
    wq: bass.AP, bq: bass.AP, wk: bass.AP, bk: bass.AP, wv: bass.AP, bv: bass.AP,
    wo: bass.AP, bo: bass.AP, proj_w: bass.AP, proj_b: bass.AP,
    ffn_w: bass.AP, ffn_b: bass.AP, lora_a: bass.AP, lora_b: bass.AP,
    router_w: bass.AP, router_b: bass.AP, out: bass.AP,
):
    _, L, D = x.shape
    C, H, E = wq.shape
    TAPS = conv_w.shape[0]
    NE, R = lora_a.shape[:2]
    KT = D // P
    NBLK = L // P
    GB = 4
    GT = GB * P
    NG = NBLK // GB
    NP = H // 2
    NK = TAPS * KT
    NH = NK // 2
    SCALE = float(E) ** -0.5
    assert D == 512 and C == P and 2 * E == P and TAPS == 3 and NE * R == P and GT == 512

    xd = x.rearrange("a (g b p) d -> g p (a b) d", p=P, b=GB)
    xrow = x.rearrange("a l d -> (a l) d")
    outd = out.rearrange("a (n p) d -> n p (a d)", p=P)
    convd = conv_w.rearrange("j c n -> (j c) n").rearrange("(i t p) n -> i p t n", p=P, t=2)

    with ExitStack() as ctx:
        def sb(name, shape, dt=F32, scope=ctx):
            return scope.enter_context(nc.sbuf_tensor(name, shape, dt))

        def bank(name):
            return ctx.enter_context(nc.psum_tensor(name, [P, 512], F32))

        def sem(name):
            return ctx.enter_context(nc.semaphore(name))

        x1 = sb("x1", [P, NBLK, D])
        rows = sb("rows", [P, GB, D])
        ident = sb("ident", [P, P])
        stats2 = sb("stats2", [P, NBLK, 2])
        bn_raw = sb("bn_raw", [P, GB, 6])
        bn_mv = sb("bn_mv", [P, GB, 2])
        var_eps = sb("var_eps", [P, GB])
        rstd = sb("rstd", [P, GB])
        neg_half, eps_sb = sb("neg_half", [P, GB]), sb("eps_sb", [P, GB])
        rowmask = sb("rowmask", [P, NBLK])
        mrstd = sb("mrstd", [P, GB])
        acc = sb("acc", [P, D])
        ones = sb("ones", [P, P])

        ph1 = ExitStack()
        cw_hi = sb("cw_hi", [P, NK, 3 * C], F32R, ph1)
        cw_lo = sb("cw_lo", [P, NK, 3 * C], F32R, ph1)
        ph1.close()
        ph2 = ExitStack()
        w_raw = sb("w_raw", [P, KT, D], F32, ph2)
        a_raw = sb("a_raw", [P, D], F32, ph2)
        b_raw = sb("b_raw", [P, KT, NE, R], F32, ph2)
        r_raw = sb("r_raw", [NE, D], F32, ph2)
        r_bias = sb("r_bias", [P, NE], F32, ph2)
        y_bias = sb("y_bias", [P, D], F32, ph2)
        wT = sb("wT", [P, KT, D], F32, ph2)
        bT = sb("bT", [P, D], F32, ph2)
        rT = sb("rT", [P, KT, NE], F32, ph2)
        expert = sb("expert", [P, NE], F32, ph2)
        colmean = sb("colmean", [P, KT, P], F32, ph2)
        logit = sb("logit", [P, NE], F32, ph2)
        nlmax = sb("nlmax", [P, 1], F32, ph2)
        lsum = sb("lsum", [P, 1], F32, ph2)
        lrec = sb("lrec", [P, 1], F32, ph2)
        lexp = sb("lexp", [P, NE], F32, ph2)
        lpick = sb("lpick", [P, NE], F32, ph2)
        route = sb("route", [P, 1], F32, ph2)
        route2 = sb("route2", [P, 1], F32, ph2)
        we_hi = sb("we_hi", [P, KT, D], F32R, ph2)
        we_lo = sb("we_lo", [P, KT, D], F32R, ph2)
        ph2.close()
        hold = sb("hold", [P, 2 * NK * 3 * C])

        wq_hi, wq_lo = sb("wq_hi", [P, H * E], F32R), sb("wq_lo", [P, H * E], F32R)
        wk_hi, wk_lo = sb("wk_hi", [P, H * E], F32R), sb("wk_lo", [P, H * E], F32R)
        wv_hi, wv_lo = sb("wv_hi", [P, H * E], F32R), sb("wv_lo", [P, H * E], F32R)
        wo_hi, wo_lo = sb("wo_hi", [P, NP, C], F32R), sb("wo_lo", [P, NP, C], F32R)
        pj_hi, pj_lo = sb("pj_hi", [P, D], F32R), sb("pj_lo", [P, D], F32R)
        NB = 3 * NP + 3 + 1
        bias_rows, biases, bq_sc = sb("bias_rows", [NB, P]), sb("biases", [P, NB]), sb("bq_sc", [P, NP])
        bk_sb, bv_sb = biases[:, NP:2 * NP], biases[:, 2 * NP:3 * NP]
        conv_bias, bo_sb = biases[:, 3 * NP:3 * NP + 3], biases[:, 3 * NP + 3:NB]
        pb_sb = sb("pb_sb", [P, D])
        ident16 = sb("ident16", [P, P], BF16)
        mask16 = sb("mask16", [P, 4 * P], BF16)
        edge = sb("edge", [2 * NG, D])
        edge_bn, edge_mv = sb("edge_bn", [2 * NG, 6]), sb("edge_mv", [2 * NG, 2])
        edge_hi, edge_lo = sb("edge_hi", [P, KT, 2 * NG], F32R), sb("edge_lo", [P, KT, 2 * NG], F32R)
        xt_hi, xt_lo = sb("xt_hi", [P, KT, GT + 2], F32R), sb("xt_lo", [P, KT, GT + 2], F32R)
        qkv_hi, qkv_lo = sb("qkv_hi", [P, 3, GT], F32R), sb("qkv_lo", [P, 3, GT], F32R)
        vh = sb("vh", [P, GB, H * E])
        q_hi, q_lo = sb("q_hi", [P, GT], F32R), sb("q_lo", [P, GT], F32R)
        k_hi, k_lo = sb("k_hi", [P, GB, 2, P], F32R), sb("k_lo", [P, GB, 2, P], F32R)
        nmax = sb("nmax", [P, 2, 8])
        rsum = sb("rsum", [P, 2, 8])
        rinv = sb("rinv", [P, 2, 8])
        probs = sb("probs", [P, 2, 8, P])
        pT = sb("pT", [P, 8, P])
        ctx_hi, ctx_lo = sb("ctx_hi", [P, 2, GT], F32R), sb("ctx_lo", [P, 2, GT], F32R)
        o_hi, o_lo = sb("o_hi", [P, GT], F32R), sb("o_lo", [P, GT], F32R)

        S_BANK = [bank("scores0"), bank("scores1")]
        Q_BANK, K_BANK = bank("proj_q"), bank("proj_k")
        T_BANK = [bank("trans0"), bank("trans1")]
        V_BANK = bank("context")
        O_BANK = bank("attn_out")
        CONV_BANK = [T_BANK[0], T_BANK[1], V_BANK]
        PJ_BANK = [Q_BANK, K_BANK]

        x_first, x_rest, edge_in, small_in = sem("x_first"), sem("x_rest"), sem("edge_in"), sem("small_in")
        w_in = [sem(f"w_in{i}") for i in range(4)]
        ffn_in = sem("ffn_in")
        out_done = [sem(f"out_done{i}") for i in range(GB)]
        pool_const, dve_const, bias_done = sem("pool_const"), sem("dve_const"), sem("bias_done")
        bias_full = sem("bias_full")
        w_hi_done, w_split = sem("w_hi_done"), sem("w_split")
        edge_zero, edge_step, edge_n, edge_full = sem("edge_zero"), sem("edge_step"), sem("edge_n"), sem("edge_full")
        edge_hi_done, edge_split = sem("edge_hi_done"), sem("edge_split")
        edge_var, edge_rstd = sem("edge_var"), sem("edge_rstd")
        ln1_raw, ln1_stats, ln1_var, ln1_rstd = sem("ln1_raw"), sem("ln1_stats"), sem("ln1_var"), sem("ln1_rstd")
        xn_ready, xt_full, xt_hi_done, xt_split = sem("xn_ready"), sem("xt_full"), sem("xt_hi_done"), sem("xt_split")
        halo_done, conv_full, qkv_hi_done, qkv_split = sem("halo_done"), sem("conv_full"), sem("qkv_hi_done"), sem("qkv_split")
        v_full, vh_ready = sem("v_full"), sem("vh_ready")
        q_full, k_full, q_hi_done, k_hi_done = sem("q_full"), sem("k_full"), sem("q_hi_done"), sem("k_hi_done")
        q_split, k_split = sem("q_split"), sem("k_split")
        s_full, nmax_ready, exp_done, rinv_ready = sem("s_full"), sem("nmax_ready"), sem("exp_done"), sem("rinv_ready")
        pn_ready, t_full = sem("pn_ready"), sem("t_full")
        ptA_ready, ptB_ready = sem("ptA_ready"), sem("ptB_ready")
        pv_full, ctx_hi_done, ctx_split, o_used = sem("pv_full"), sem("ctx_hi_done"), sem("ctx_split"), sem("o_used")
        oacc_full, o_hi_done, o_split, pj_full, pj_evac = sem("oacc_full"), sem("o_hi_done"), sem("o_split"), sem("pj_full"), sem("pj_evac")
        lno_raw, lno_stats, lno_var, lno_rstd = sem("lno_raw"), sem("lno_stats"), sem("lno_var"), sem("lno_rstd")
        on_ready, x1_ready = sem("on_ready"), sem("x1_ready")
        ln2_raw, ln2_stats, ln2_var, ln2_rstd, ln2_kept = sem("ln2_raw"), sem("ln2_stats"), sem("ln2_var"), sem("ln2_rstd"), sem("ln2_kept")
        xm_ready, acc_done = sem("xm_ready"), sem("acc_done")
        exp_mark, expert_ready = sem("exp_mark"), sem("expert_ready")
        wT_full, wT_ready = sem("wT_full"), sem("wT_ready")
        bT_full, bT_ready, rT_ready = sem("bT_full"), sem("bT_ready"), sem("rT_ready")
        sum_full, mean_ready, logit_full, route_step, lexp_ready = sem("sum_full"), sem("mean_ready"), sem("logit_full"), sem("route_step"), sem("lexp_ready")
        bs_ready, lora_full, we_ready, we_hi_done, we_split = sem("bs_ready"), sem("lora_full"), sem("we_ready"), sem("we_hi_done"), sem("we_split")
        x2_ready, x2_full, x2_hi_done, x2_split = sem("x2_ready"), sem("x2_full"), sem("x2_hi_done"), sem("x2_split")
        y_full, y_ready, y_raw, y_stats, y_var, y_rstd = sem("y_full"), sem("y_ready"), sem("y_raw"), sem("y_stats"), sem("y_var"), sem("y_rstd")
        yn_ready, res_ready = sem("yn_ready"), sem("res_ready")

        x2T_hi = xt_hi[:, :, 0:2 * P].rearrange("p k (s t) -> p s k t", s=2)
        x2T_lo = xt_lo[:, :, 0:2 * P].rearrange("p k (s t) -> p s k t", s=2)
        x2n = probs[:, 0, :, :].rearrange("p a k -> p (a k)").rearrange("p (s d) -> p s d", s=2)
        X2_BANK, Y_BANK = [T_BANK[0], T_BANK[1]], [Q_BANK, K_BANK]
        NY = GB
        Y_AHEAD = 1

        def flat(t):
            return t[:, :, :].rearrange("p a n -> p (a n)")

        splits = [(flat(cw_hi)[:, i * 768:(i + 1) * 768], flat(cw_lo)[:, i * 768:(i + 1) * 768], 768, 1.0)
                  for i in range(NH)]
        splits += [(wq_hi[:, :], wq_lo[:, :], H * E, SCALE), (wk_hi[:, :], wk_lo[:, :], H * E, 1.0),
                   (wv_hi[:, :], wv_lo[:, :], H * E, 1.0), (flat(wo_hi), flat(wo_lo), NP * C, 1.0),
                   (pj_hi[:, :], pj_lo[:, :], D, 1.0)]
        sources = [(convd[i], "p t n") for i in range(NH)]
        sources += [(wq.rearrange("c h e -> c (h e)"), ""), (wk.rearrange("c h e -> c (h e)"), ""),
                    (wv.rearrange("c h e -> c (h e)"), ""),
                    (wo.rearrange("(p two) e w -> (two e) p w", two=2), "p t n"), (proj_w, "")]
        NW = len(splits)

        def landing(i):
            return vh[:, i % 4, 0:splits[i][2]]

        CH = [2, 0, 1]
        X_SLOTS = [3, 4, 5, 6]
        LORA_BANK = [T_BANK[0], T_BANK[1], V_BANK, S_BANK[1]]
        N_SMALL = 6
        N_FFN = KT + 5
        block = ctx.enter_context(nc.Block())

        @block.sync
        def _(sp):
            for b in range(GB):
                sp.dma_start(x1[:, b, :], xd[0, :, b, :]).then_inc(x_first, 16)
            sp.wait_ge(edge_zero, 1)
            for g in range(NG):
                if g > 0:
                    sp.dma_start(edge[2 * g:2 * g + 1, :], xrow[g * GT - 1:g * GT, :]).then_inc(edge_in, 16)
                if g < NG - 1:
                    sp.dma_start(edge[2 * g + 1:2 * g + 2, :], xrow[(g + 1) * GT:(g + 1) * GT + 1, :]).then_inc(edge_in, 16)
            for i in range(NW):
                if i >= 4:
                    sp.wait_ge(w_split, i - 3)
                src, kind = sources[i]
                dst = landing(i)
                if kind:
                    dst = dst.rearrange("p (t n) -> p t n", n=src.shape[2])
                sp.dma_start(dst, src).then_inc(w_in[i % 4], 16)
            for g in range(1, NG):
                sp.dma_start(x1[:, g * GB:(g + 1) * GB, :], xd[g]).then_inc(x_rest, 16)
            sp.wait_ge(conv_full, 3 * NG)
            sp.dma_start(w_raw[:, :, :], ffn_w.rearrange("(t p) d -> p t d", p=P)).then_inc(ffn_in, 16)
            for t in range(KT):
                sp.dma_start(b_raw[:, t, :, :], lora_b[:, t * P:(t + 1) * P, :].rearrange("e p r -> p e r")).then_inc(ffn_in, 16)
            sp.dma_start(a_raw[:, :], lora_a.rearrange("e r d -> (e r) d")).then_inc(ffn_in, 16)
            sp.dma_start(r_raw[:, :], router_w).then_inc(ffn_in, 16)
            sp.dma_start(r_bias[:, :], router_b.rearrange("(a e) -> a e", a=1).broadcast_to([P, NE])).then_inc(ffn_in, 16)
            sp.dma_start(y_bias[:, :], ffn_b.rearrange("(a e) -> a e", a=1).broadcast_to([P, D])).then_inc(ffn_in, 16)

            with sp.Fori(0, NBLK // NY) as i:
                for s in range(NY):
                    sp.wait_ge(res_ready, NY * i + (s + 1))
                    sp.dma_start(outd[bass.ds(NY * i + s, 1)].rearrange("n p d -> p (n d)"), rows[:, s, :]).then_inc(out_done[s], 16)
            for s in range(NY):
                sp.wait_ge(out_done[s], 16 * (NBLK // NY))

        def rsqrt_chain(pool, n, stats_sem, var_sem, done_sem, count, mv, ve, rs, half):
            pool.wait_ge(stats_sem, count)
            nc.gpsimd.tensor_tensor(ve, mv, eps_sb[0:ve.shape[0], 0:n], ALU.add).then_inc(var_sem, 1)
            pool.wait_ge(var_sem, count)
            nc.gpsimd.tensor_tensor(rs, ve, half, ALU.pow).then_inc(done_sem, 1)

        @block.gpsimd
        def _(pool):
            nc.gpsimd.memset(edge[:, :], 0.0).then_inc(edge_zero, 1)
            nc.gpsimd.memset(ident[:, :], 0.0).then_inc(pool_const, 1)
            nc.gpsimd.memset(neg_half[:, :], -0.5).then_inc(pool_const, 1)
            nc.gpsimd.memset(eps_sb[:, :], EPS).then_inc(pool_const, 1)
            pool.wait_ge(pool_const, 3)
            nc.gpsimd.affine_select(out=ident[:, :], in_=ident[:, :], compare_op=ALU.not_equal, fill=1.0,
                                    base=0, pattern=[[-1, P]], channel_multiplier=1).then_inc(pool_const, 1)
            rsqrt_chain(pool, GB, ln1_stats, ln1_var, ln1_rstd, 1, bn_mv[:, :, 1], var_eps[:, :], rstd[:, :], neg_half[:, :])
            rsqrt_chain(pool, 1, edge_n, edge_var, edge_rstd, 1, edge_mv[:, 1:2], edge_bn[:, 0:1], edge_bn[:, 1:2],
                        neg_half[0:2 * NG, 0:1])
            pool.wait_ge(pool_const, 4)
            nc.gpsimd.tensor_copy(ident16[:, :], ident[:, :]).then_inc(pool_const, 1)
            nc.gpsimd.memset(mask16[:, :], 0.0).then_inc(pool_const, 1)
            nc.gpsimd.memset(rowmask[:, :], 1.0).then_inc(pool_const, 1)
            nc.gpsimd.memset(acc[:, :], 0.0).then_inc(pool_const, 1)
            nc.gpsimd.memset(ones[:, :], 1.0).then_inc(pool_const, 1)
            pool.wait_ge(pool_const, 9)
            nc.gpsimd.affine_select(out=mask16[:, :].rearrange("p (a k) -> p a k", k=P),
                                    in_=mask16[:, :].rearrange("p (a k) -> p a k", k=P),
                                    compare_op=ALU.is_ge, fill=MASKED, base=0,
                                    pattern=[[0, 4], [-1, P]], channel_multiplier=1).then_inc(pool_const, 1)
            nc.gpsimd.affine_select(out=rowmask[:, 0:1], in_=rowmask[:, 0:1], compare_op=ALU.is_ge, fill=0.0,
                                    base=-Q_START, pattern=[[0, 1]], channel_multiplier=1).then_inc(pool_const, 1)
            nc.gpsimd.affine_select(out=rowmask[:, NBLK - 1:NBLK], in_=rowmask[:, NBLK - 1:NBLK],
                                    compare_op=ALU.is_ge, fill=0.0, base=P - 1 + Q_END, pattern=[[0, 1]],
                                    channel_multiplier=-1).then_inc(pool_const, 1)

            def halo(g, at_edge):
                pool.wait_ge(edge_split, 1)
                for dst, src in ((xt_hi, edge_hi), (xt_lo, edge_lo)):
                    nc.gpsimd.tensor_copy(dst[:, :, 0:GT + 2:GT + 1], src[:, :, at_edge]).then_inc(halo_done, 1)

            halo(0, slice(0, 2))

            def group(g, last):
                if not last:
                    rsqrt_chain(pool, GB, ln1_stats, ln1_var, ln1_rstd, g + 2, bn_mv[:, :, 1], var_eps[:, :],
                                rstd[:, :], neg_half[:, :])
                    pool.wait_ge(conv_full, 3 * g + 3)
                    halo(g + 1, bass.ds(2 * g + 2, 2))
                for p in range(NP):
                    for h in range(2):
                        pool.wait_ge(rinv_ready, 16 * g + (2 * p + h + 1))
                        part = probs[:, p % 2, 4 * h:4 * h + 4, :]
                        nc.gpsimd.tensor_tensor(
                            part, part, rinv[:, p % 2, 4 * h:4 * h + 4].unsqueeze(2).broadcast_to([P, 4, P]),
                            ALU.mult).then_inc(pn_ready, 1)
                rsqrt_chain(pool, GB, lno_stats, lno_var, lno_rstd, g + 1, bn_mv[:, :, 1], var_eps[:, :],
                            rstd[:, :], neg_half[:, :])
                for b in range(GB):
                    pool.wait_ge(on_ready, 4 * g + (b + 1))
                    xb = x1[:, bass.ds(4 * g + b, 1), :].rearrange("p a d -> p (a d)")
                    nc.gpsimd.tensor_tensor(xb, xb, rows[:, b, :], ALU.add).then_inc(x1_ready, 1)
                rsqrt_chain(pool, GB, ln2_stats, ln2_var, ln2_rstd, g + 1, bn_mv[:, :, 1], var_eps[:, :],
                            rstd[:, :], neg_half[:, :])
                pool.wait_ge(ln2_rstd, g + 1)
                nc.gpsimd.tensor_tensor(mrstd[:, :], rstd[:, :], rowmask[:, bass.ds(4 * g, 4)], ALU.mult).then_inc(ln2_kept, 1)
                nc.gpsimd.tensor_copy(stats2[:, bass.ds(4 * g, 4), 0], bn_mv[:, :, 0]).then_inc(ln2_kept, 1)
                nc.gpsimd.tensor_copy(stats2[:, bass.ds(4 * g, 4), 1], rstd[:, :]).then_inc(ln2_kept, 1)
                for b in range(GB):
                    pool.wait_ge(xm_ready, 4 * g + (b + 1))
                    if b > 0:
                        pool.wait_ge(acc_done, 4 * g + b)
                    nc.gpsimd.tensor_tensor(acc[:, :], acc[:, :], rows[:, b, :], ALU.add).then_inc(acc_done, 1)

            with pool.Fori(0, NG - 1) as g:
                group(g, False)
            group(NG - 1, True)

            pool.wait_ge(conv_full, 3 * NG)
            nc.gpsimd.memset(expert[:, :], 1.0).then_inc(exp_mark, 1)
            pool.wait_ge(exp_mark, 1)
            nc.gpsimd.affine_select(out=expert[:, :], in_=expert[:, :], compare_op=ALU.is_ge, fill=0.0, base=0,
                                    pattern=[[-R, NE]], channel_multiplier=1).then_inc(exp_mark, 1)
            pool.wait_ge(exp_mark, 2)
            nc.gpsimd.affine_select(out=expert[:, :], in_=expert[:, :], compare_op=ALU.is_ge, fill=0.0, base=R - 1,
                                    pattern=[[R, NE]], channel_multiplier=-1).then_inc(expert_ready, 1)

            with pool.Fori(0, NBLK // NY) as i:
                n0 = NY * i
                for s in range(NY):
                    pool.wait_ge(y_stats, n0 + (s + 1))
                    nc.gpsimd.tensor_tensor(var_eps[:, s:s + 1], bn_mv[:, s, 1:2], eps_sb[:, 0:1], ALU.add).then_inc(y_var, 1)
                    pool.wait_ge(y_var, n0 + (s + 1))
                    nc.gpsimd.tensor_tensor(rstd[:, s:s + 1], var_eps[:, s:s + 1], neg_half[:, s:s + 1], ALU.pow).then_inc(y_rstd, 1)
                    pool.wait_ge(yn_ready, n0 + (s + 1))
                    xb = x1[:, bass.ds(n0 + s, 1), :].rearrange("p a d -> p (a d)")
                    nc.gpsimd.tensor_tensor(rows[:, s, :], rows[:, s, :], xb, ALU.add).then_inc(res_ready, 1)

        @block.scalar
        def _(act):
            for n, src in enumerate((bq, bk, bv)):
                act.dma_start(bias_rows[n * NP:(n + 1) * NP, :], src.rearrange("(p two) e -> p (two e)", two=2)).then_inc(small_in, 16)
            act.dma_start(bias_rows[3 * NP:3 * NP + 3, :], conv_b.rearrange("(m p) -> m p", p=P)).then_inc(small_in, 16)
            act.dma_start(bias_rows[3 * NP + 3:NB, :], bo.rearrange("(a p) -> a p", a=1)).then_inc(small_in, 16)
            act.dma_start(pb_sb[:, :], proj_b.rearrange("(a e) -> a e", a=1).broadcast_to([P, D])).then_inc(small_in, 16)

            def split_hi(i):
                act.wait_ge(w_in[i % 4], 16 * (i // 4 + 1))
                nc.scalar.activation(splits[i][0], landing(i), ACT.Copy, scale=splits[i][3]).then_inc(w_hi_done, 1)

            def xt_hi_part(n, b, bk):
                act.wait_ge(xt_full, n)
                nc.scalar.activation(xt_hi[:, :, 1 + b * P:1 + (b + 1) * P],
                                     bk[:, :].rearrange("p (k t) -> p k t", k=KT), ACT.Copy).then_inc(xt_hi_done, 1)

            for b in range(GB):
                xt_hi_part(b + 1, b, T_BANK[b % 2])
                split_hi(b)
            act.wait_ge(edge_full, 1)
            nc.scalar.activation(edge_hi[:, :, :], V_BANK[:, 0:KT * 2 * NG].rearrange("p (k t) -> p k t", k=KT),
                                 ACT.Copy).then_inc(edge_hi_done, 1)
            act.wait_ge(bias_full, 1)
            nc.scalar.activation(biases[:, :], S_BANK[0][:, 0:NB], ACT.Copy).then_inc(bias_done, 1)
            nc.scalar.activation(bq_sc[:, :], S_BANK[0][:, 0:NP], ACT.Copy, scale=SCALE).then_inc(bias_done, 1)
            for i in range(GB, NW):
                split_hi(i)
            act.wait_ge(bias_done, 2)

            def evac_q(g, p):
                act.wait_ge(q_full, 8 * g + (p + 1))
                nc.scalar.activation(q_hi[:, :], Q_BANK[:, :], ACT.Identity, bias=bq_sc[:, p:p + 1]).then_inc(q_hi_done, 1)

            def evac_k(g, p):
                act.wait_ge(k_full, 8 * g + (p + 1))
                for h in range(2):
                    r = slice(E * h, E * h + E)
                    nc.scalar.activation(k_hi[r, :, h, :], K_BANK[r, :].rearrange("p (b k) -> p b k", b=GB),
                                         ACT.Identity, bias=bk_sb[r, p:p + 1]).then_inc(k_hi_done, 1)

            def exps(g, p, h):
                act.wait_ge(nmax_ready, 16 * g + (2 * p + h + 1))
                if p >= 2:
                    act.wait_ge(t_full, 16 * g + (2 * (p - 2) + h + 1))
                for j in range(4):
                    c = 4 * h + j
                    last = nc.scalar.activation(probs[:, p % 2, c, :], S_BANK[h][:, j * P:(j + 1) * P], ACT.Exp,
                                                bias=nmax[:, p % 2, c:c + 1], accum_out=rsum[:, p % 2, c:c + 1])
                last.then_inc(exp_done, 1)

            def group(g, last):
                for m in range(3):
                    act.wait_ge(conv_full, 3 * g + (m + 1))
                    nc.scalar.activation(qkv_hi[:, m, :], CONV_BANK[m][:, :], ACT.Identity,
                                         bias=conv_bias[:, CH[m]:CH[m] + 1]).then_inc(qkv_hi_done, 1)
                evac_q(g, 0)
                evac_k(g, 0)
                for u in range(2 * GB):
                    act.wait_ge(v_full, 8 * g + (u + 1))
                    nc.scalar.activation(vh[:, u // 2, (u % 2) * 512:(u % 2) * 512 + 512], T_BANK[u % 2][:, :],
                                         ACT.Copy).then_inc(vh_ready, 1)
                for p in range(NP + 1):
                    if p < NP:
                        exps(g, p, 0)
                    if p + 1 < NP:
                        evac_q(g, p + 1)
                    if p >= 1:
                        act.wait_ge(t_full, 16 * g + 2 * p)
                        nc.scalar.activation(pT[:, 4:8, :], T_BANK[1][:, :].rearrange("p (a k) -> p a k", a=4),
                                             ACT.Copy).then_inc(ptB_ready, 1)
                    if p + 1 < NP:
                        evac_k(g, p + 1)
                    if p < NP:
                        exps(g, p, 1)
                    if p >= 1:
                        act.wait_ge(pv_full, 8 * g + p)
                        if p >= 3:
                            act.wait_ge(o_used, (NP - 1) * g + (p - 2))
                        nc.scalar.activation(ctx_hi[:, (p - 1) % 2, :], V_BANK[:, :], ACT.Identity,
                                             bias=bv_sb[:, p - 1:p]).then_inc(ctx_hi_done, 1)
                    if not last and p in X_SLOTS:
                        b = X_SLOTS.index(p)
                        xt_hi_part(4 * g + (GB + b + 1), b, T_BANK[0])
                act.wait_ge(oacc_full, g + 1)
                nc.scalar.activation(o_hi[:, :], O_BANK[:, :], ACT.Identity, bias=bo_sb[:, 0:1]).then_inc(o_hi_done, 1)

            with act.Fori(0, NG - 1) as g:
                group(g, False)
            group(NG - 1, True)

            for k in range(KT):
                act.wait_ge(wT_full, k + 1)
                nc.scalar.activation(wT[:, k, :], T_BANK[k % 2][:, :], ACT.Copy).then_inc(wT_ready, 1)
            act.wait_ge(bT_full, 1)
            nc.scalar.activation(bT[:, :], V_BANK[:, :], ACT.Copy).then_inc(bT_ready, 1)
            act.wait_ge(bT_full, 2)
            nc.scalar.activation(rT[:, :, :], S_BANK[0][:, 0:KT * NE].rearrange("p (k e) -> p k e", k=KT),
                                 ACT.Copy).then_inc(rT_ready, 1)
            act.wait_ge(sum_full, 1)
            nc.scalar.activation(colmean[:, :, :], O_BANK[:, :].rearrange("p (k t) -> p k t", k=KT), ACT.Copy,
                                 scale=1.0 / (L + Q_END - Q_START)).then_inc(mean_ready, 1)
            act.wait_ge(route_step, 2)
            nc.scalar.activation(lexp[:, :], logit[:, :], ACT.Exp, bias=nlmax[:, 0:1],
                                 accum_out=lsum[:, 0:1]).then_inc(lexp_ready, 1)
            for k in range(KT):
                act.wait_ge(we_ready, k + 1)
                nc.scalar.activation(we_hi[:, k, :], wT[:, k, :], ACT.Copy).then_inc(we_hi_done, 1)

            def x2_hi(n, s):
                act.wait_ge(x2_full, n)
                nc.scalar.activation(x2T_hi[:, s], X2_BANK[s][:, :].rearrange("p (k t) -> p k t", k=KT),
                                     ACT.Copy).then_inc(x2_hi_done, 1)

            with act.Fori(0, NBLK // 2) as i:
                n0 = 2 * i
                for s in range(2):
                    x2_hi(n0 + (s + 1), s)

        @block.vector
        def _(dve):
            nc.vector.memset(k_hi[:, :, :, :].bitcast(F32), 0.0).then_inc(dve_const, 1)
            nc.vector.memset(k_lo[:, :, :, :].bitcast(F32), 0.0).then_inc(dve_const, 1)

            def raw_waited(raw, count):
                count = count if type(count) is int else dve.to_reg(count)
                dve.wait_ge(dve_const, 2)
                dve.wait_ge(raw, count)

            def x_block(n):
                if type(n) is int:
                    return x1[:, n, :]
                return x1[:, bass.ds(n, 1), :].rearrange("p a d -> p (a d)")

            def ln1_statistics(gg):
                for b in range(GB):
                    nc.vector.bn_stats(bn_raw[:, b, :], x_block(4 * gg + b)).then_inc(ln1_raw, 1)
                raw_waited(ln1_raw, 4 * gg + GB)
                for b in range(GB):
                    last = nc.vector.bn_aggr(bn_mv[:, b, :], bn_raw[:, b, :])
                last.then_inc(ln1_stats, 1)

            def normed(gg, b):
                dve.wait_ge(ln1_rstd, gg + 1)
                nc.vector.tensor_scalar(rows[:, b, :], x_block(4 * gg + b), bn_mv[:, b, 0:1], rstd[:, b:b + 1],
                                        ALU.subtract, ALU.mult).then_inc(xn_ready, 1)

            def xt_lo_part(n, b, bk):
                dve.wait_ge(xt_hi_done, n)
                nc.vector.tensor_tensor(xt_lo[:, :, 1 + b * P:1 + (b + 1) * P], bk[:, :].rearrange("p (k t) -> p k t", k=KT),
                                        xt_hi[:, :, 1 + b * P:1 + (b + 1) * P].bitcast(F32), ALU.subtract).then_inc(xt_split, 1)

            def split_lo(i):
                dve.wait_ge(w_hi_done, i + 1)
                nc.vector.scalar_tensor_tensor(out=splits[i][1], in0=landing(i), scalar=splits[i][3],
                                               in1=splits[i][0].bitcast(F32), op0=ALU.mult,
                                               op1=ALU.subtract).then_inc(w_split, 1)

            dve.wait_ge(x_first, 16 * GB)
            ln1_statistics(0)
            dve.wait_ge(edge_in, 16 * (2 * NG - 2))
            nc.vector.bn_stats(edge_bn[:, :], edge[:, :]).then_inc(edge_step, 1)
            dve.wait_ge(edge_step, 1)
            nc.vector.bn_aggr(edge_mv[:, :], edge_bn[:, :]).then_inc(edge_n, 1)
            for b in range(GB):
                normed(0, b)
            dve.wait_ge(edge_rstd, 1)
            nc.vector.tensor_scalar(edge[:, :], edge[:, :], edge_mv[:, 0:1], edge_bn[:, 1:2],
                                    ALU.subtract, ALU.mult).then_inc(edge_step, 1)
            for b in range(GB):
                xt_lo_part(b + 1, b, T_BANK[b % 2])
                split_lo(b)
            dve.wait_ge(edge_hi_done, 1)
            nc.vector.tensor_tensor(edge_lo[:, :, :], V_BANK[:, 0:KT * 2 * NG].rearrange("p (k t) -> p k t", k=KT),
                                    edge_hi[:, :, :].bitcast(F32), ALU.subtract).then_inc(edge_split, 1)
            for i in range(GB, NW):
                split_lo(i)
            dve.wait_ge(small_in, 16 * N_SMALL)
            dve.wait_ge(bias_done, 2)
            dve.wait_ge(x_rest, 16 * (NG - 1))

            def lo_q(g, p):
                dve.wait_ge(q_hi_done, 8 * g + (p + 1))
                nc.vector.scalar_tensor_tensor(out=q_lo[:, :], in0=Q_BANK[:, :], scalar=bq_sc[:, p:p + 1],
                                               in1=q_hi[:, :].bitcast(F32), op0=ALU.add, op1=ALU.subtract).then_inc(q_split, 1)

            def lo_k(g, p):
                for h in range(2):
                    r = slice(E * h, E * h + E)
                    dve.wait_ge(k_hi_done, 16 * g + (2 * p + h + 1))
                    nc.vector.scalar_tensor_tensor(
                        out=k_lo[r, :, h, :], in0=K_BANK[r, :].rearrange("p (b k) -> p b k", b=GB),
                        scalar=bk_sb[r, p:p + 1], in1=k_hi[r, :, h, :].bitcast(F32),
                        op0=ALU.add, op1=ALU.subtract).then_inc(k_split, 1)

            def row_max(g, p, h):
                dve.wait_ge(s_full, 16 * g + (2 * p + h + 1))
                nc.vector.tensor_reduce(nmax[:, p % 2, 4 * h:4 * h + 4], S_BANK[h][:, :].rearrange("p (a k) -> p a k", a=4),
                                        op=ALU.max, axis=AX_X, negate=True).then_inc(nmax_ready, 1)

            def row_inv(g, p, h):
                dve.wait_ge(exp_done, 16 * g + (2 * p + h + 1))
                nc.vector.reciprocal(rinv[:, p % 2, 4 * h:4 * h + 4], rsum[:, p % 2, 4 * h:4 * h + 4]).then_inc(rinv_ready, 1)

            def group(g, first, last):
                for m in range(3):
                    dve.wait_ge(qkv_hi_done, 3 * g + (m + 1))
                    nc.vector.scalar_tensor_tensor(
                        out=qkv_lo[:, m, :], in0=CONV_BANK[m][:, :], scalar=conv_bias[:, CH[m]:CH[m] + 1],
                        in1=qkv_hi[:, m, :].bitcast(F32), op0=ALU.add, op1=ALU.subtract).then_inc(qkv_split, 1)
                lo_q(g, 0)
                lo_k(g, 0)
                if not first and not last:
                    dve.wait_ge(ln2_kept, 3 * g)
                    dve.wait_ge(acc_done, 4 * g)
                if not last:
                    ln1_statistics(g + 1)
                for p in range(NP + 1):
                    if p < NP:
                        row_max(g, p, 0)
                    if 1 <= p:
                        row_inv(g, p - 1, 1)
                    if p >= 2:
                        ctx_lo_part(g, p - 2)
                    if p < NP:
                        row_max(g, p, 1)
                    if p >= 1:
                        dve.wait_ge(t_full, 16 * g + (2 * p - 1))
                        nc.vector.tensor_copy(pT[:, 0:4, :], T_BANK[0][:, :].rearrange("p (a k) -> p a k", a=4)).then_inc(ptA_ready, 1)
                    if p + 1 < NP:
                        lo_q(g, p + 1)
                    if p < NP:
                        row_inv(g, p, 0)
                    if p + 1 < NP:
                        lo_k(g, p + 1)
                    if not last and p + 1 in X_SLOTS:
                        normed(g + 1, X_SLOTS.index(p + 1))
                    if not last and p in X_SLOTS:
                        b = X_SLOTS.index(p)
                        xt_lo_part(4 * g + (GB + b + 1), b, T_BANK[0])
                ctx_lo_part(g, NP - 1)
                dve.wait_ge(o_hi_done, g + 1)
                nc.vector.scalar_tensor_tensor(out=o_lo[:, :], in0=O_BANK[:, :], scalar=bo_sb[:, 0:1],
                                               in1=o_hi[:, :].bitcast(F32), op0=ALU.add, op1=ALU.subtract).then_inc(o_split, 1)
                for b in range(GB):
                    dve.wait_ge(pj_full, 4 * g + (b + 1))
                    nc.vector.tensor_tensor(rows[:, b, :], PJ_BANK[b % 2][:, :], pb_sb[:, :], ALU.add).then_inc(pj_evac, 1)
                for b in range(GB):
                    dve.wait_ge(pj_evac, 4 * g + (b + 1))
                    nc.vector.bn_stats(bn_raw[:, b, :], rows[:, b, :]).then_inc(lno_raw, 1)
                raw_waited(lno_raw, 4 * g + GB)
                for b in range(GB):
                    done = nc.vector.bn_aggr(bn_mv[:, b, :], bn_raw[:, b, :])
                done.then_inc(lno_stats, 1)
                dve.wait_ge(lno_rstd, g + 1)
                for b in range(GB):
                    nc.vector.tensor_scalar(rows[:, b, :], rows[:, b, :], bn_mv[:, b, 0:1], rstd[:, b:b + 1],
                                            ALU.subtract, ALU.mult).then_inc(on_ready, 1)
                for b in range(GB):
                    dve.wait_ge(x1_ready, 4 * g + (b + 1))
                    nc.vector.bn_stats(bn_raw[:, b, :], x_block(4 * g + b)).then_inc(ln2_raw, 1)
                raw_waited(ln2_raw, 4 * g + GB)
                for b in range(GB):
                    done = nc.vector.bn_aggr(bn_mv[:, b, :], bn_raw[:, b, :])
                done.then_inc(ln2_stats, 1)
                dve.wait_ge(ln2_kept, 3 * g + 1)
                for b in range(GB):
                    nc.vector.tensor_scalar(rows[:, b, :], x_block(4 * g + b), bn_mv[:, b, 0:1], mrstd[:, b:b + 1],
                                            ALU.subtract, ALU.mult).then_inc(xm_ready, 1)

            def ctx_lo_part(g, p):
                dve.wait_ge(ctx_hi_done, 8 * g + (p + 1))
                nc.vector.scalar_tensor_tensor(out=ctx_lo[:, p % 2, :], in0=V_BANK[:, :], scalar=bv_sb[:, p:p + 1],
                                               in1=ctx_hi[:, p % 2, :].bitcast(F32), op0=ALU.add,
                                               op1=ALU.subtract).then_inc(ctx_split, 1)

            group(0, True, False)
            with dve.Fori(1, NG - 1) as g:
                group(g, False, False)
            group(NG - 1, False, True)

            def x2_norm(n, s):
                nc.vector.tensor_scalar(x2n[:, s, :], x_block(n), stat(n, 0), stat(n, 1),
                                        ALU.subtract, ALU.mult).then_inc(x2_ready, 1)

            def stat(n, c):
                if type(n) is int:
                    return stats2[:, n, c:c + 1]
                return stats2[:, bass.ds(n, 1), c:c + 1].rearrange("p a c -> p (a c)")

            dve.wait_ge(ln2_kept, 3 * NG)
            dve.wait_ge(acc_done, 4 * NG)
            x2_norm(0, 0)
            x2_norm(1, 1)
            dve.wait_ge(logit_full, 1)
            dve.wait_ge(ffn_in, 16 * N_FFN)
            nc.vector.tensor_tensor(logit[:, :], O_BANK[:, 0:NE], r_bias[:, :], ALU.add).then_inc(route_step, 1)
            dve.wait_ge(route_step, 1)
            nc.vector.tensor_reduce(nlmax[:, :], logit[:, :], op=ALU.max, axis=AX_X, negate=True).then_inc(route_step, 1)
            dve.wait_ge(lexp_ready, 1)
            nc.vector.reciprocal(lrec[:, :], lsum[:, :]).then_inc(route_step, 1)
            dve.wait_ge(expert_ready, 1)
            nc.vector.tensor_tensor(lpick[:, :], lexp[:, :], expert[:, :], ALU.mult).then_inc(route_step, 1)
            dve.wait_ge(route_step, 4)
            nc.vector.tensor_reduce(route[:, :], lpick[:, :], op=ALU.add, axis=AX_X).then_inc(route_step, 1)
            dve.wait_ge(route_step, 5)
            nc.vector.tensor_scalar(route2[:, :], route[:, :], lrec[:, 0:1], LORA_SCALING, ALU.mult, ALU.mult).then_inc(route_step, 1)
            dve.wait_ge(route_step, 6)
            dve.wait_ge(bT_ready, 1)
            nc.vector.tensor_scalar(bT[:, :], bT[:, :], route2[:, 0:1], None, ALU.mult).then_inc(bs_ready, 1)
            for k in range(KT):
                dve.wait_ge(lora_full, k + 1)
                dve.wait_ge(wT_ready, k + 1)
                nc.vector.tensor_tensor(wT[:, k, :], LORA_BANK[k][:, :], wT[:, k, :], ALU.add).then_inc(we_ready, 1)
            for k in range(KT):
                dve.wait_ge(we_hi_done, k + 1)
                nc.vector.tensor_tensor(we_lo[:, k, :], wT[:, k, :], we_hi[:, k, :].bitcast(F32), ALU.subtract).then_inc(we_split, 1)

            def x2_lo(n, s):
                dve.wait_ge(x2_hi_done, n)
                nc.vector.tensor_tensor(x2T_lo[:, s], X2_BANK[s][:, :].rearrange("p (k t) -> p k t", k=KT),
                                        x2T_hi[:, s].bitcast(F32), ALU.subtract).then_inc(x2_split, 1)

            def y_statistics(n, s, n_done):
                dve.wait_ge(y_full, n + 1)
                if n_done is not None:
                    dve.wait_ge(out_done[s], n_done)
                nc.vector.tensor_tensor(rows[:, s, :], Y_BANK[s % 2][:, :], y_bias[:, :], ALU.add).then_inc(y_ready, 1)
                dve.wait_ge(y_ready, n + 1)
                nc.vector.bn_stats(bn_raw[:, s, :], rows[:, s, :]).then_inc(y_raw, 1)
                raw_waited(y_raw, n + 1)
                nc.vector.bn_aggr(bn_mv[:, s, :], bn_raw[:, s, :]).then_inc(y_stats, 1)

            def y_norm(n, s):
                dve.wait_ge(y_rstd, n + 1)
                nc.vector.tensor_scalar(rows[:, s, :], rows[:, s, :], bn_mv[:, s, 0:1], rstd[:, s:s + 1],
                                        ALU.subtract, ALU.mult).then_inc(yn_ready, 1)

            x2_lo(1, 0)

            def ffn_rows(n0, rounds, first, last):
                for s in range(NY):
                    tail = last and s >= NY - 2
                    if not tail:
                        dve.wait_ge(x2_full, n0 + (s + 1))
                        x2_norm(n0 + (s + 2), s % 2)
                    if not (last and s == NY - 1):
                        x2_lo(n0 + (s + 2), (s + 1) % 2)
                    if not (first and s == 0):
                        y_norm(n0 + (s - 1), (s - 1) % NY)
                    y_statistics(n0 + s, s, None if first else 16 * rounds)

            ffn_rows(0, 0, True, False)
            with dve.Fori(1, NBLK // NY - 1) as i:
                ffn_rows(NY * i, i, False, False)
            ffn_rows(NBLK - NY, NBLK // NY - 1, False, True)
            y_norm(NBLK - 1, NY - 1)

        @block.tensor
        def _(pe):
            def three(bank_ap, lhs_hi, lhs_lo, rhs_hi, rhs_lo, start, stop):
                nc.tensor.matmul(bank_ap, lhs_hi, rhs_hi, start=start, stop=False)
                nc.tensor.matmul(bank_ap, lhs_hi, rhs_lo, start=False, stop=False)
                return nc.tensor.matmul(bank_ap, lhs_lo, rhs_hi, start=False, stop=stop)

            def x_transposes(bk, b):
                for k in range(KT):
                    last = nc.tensor.transpose(bk[:, k * P:(k + 1) * P], rows[:, b, k * P:(k + 1) * P], ident[:, :])
                last.then_inc(xt_full, 1)

            pe.wait_ge(pool_const, 4)
            for b in range(GB):
                pe.wait_ge(xn_ready, b + 1)
                if b >= 2:
                    pe.wait_ge(xt_split, b - 1)
                x_transposes(T_BANK[b % 2], b)
            pe.wait_ge(edge_step, 2)
            for k in range(KT):
                last = nc.tensor.transpose(V_BANK[:, k * 2 * NG:(k + 1) * 2 * NG], edge[:, k * P:(k + 1) * P],
                                           ident[0:2 * NG, 0:2 * NG])
            last.then_inc(edge_full, 1)
            pe.wait_ge(small_in, 16 * N_SMALL)
            nc.tensor.transpose(S_BANK[0][:, 0:NB], bias_rows[:, :], ident[0:NB, 0:NB]).then_inc(bias_full, 1)
            pe.wait_ge(bias_done, 2)
            pe.wait_ge(w_split, NH)
            pe.wait_ge(edge_split, 1)
            pe.wait_ge(dve_const, 2)
            pe.wait_ge(pool_const, 12)

            def project_qk(g, p, w_wait):
                if w_wait:
                    pe.wait_ge(w_split, w_wait)
                if p > 0:
                    pe.wait_ge(q_split, 8 * g + p)
                    pe.wait_ge(k_split, 16 * g + 2 * p)
                c = slice(p * P, (p + 1) * P)
                three(Q_BANK[:, :], wq_hi[:, c], wq_lo[:, c], qkv_hi[:, 1, :], qkv_lo[:, 1, :], True, True).then_inc(q_full, 1)
                three(K_BANK[:, :], wk_hi[:, c], wk_lo[:, c], qkv_hi[:, 2, :], qkv_lo[:, 2, :], True, True).then_inc(k_full, 1)

            def scores(g, p, first):
                pe.wait_ge(q_split, 8 * g + (p + 1))
                pe.wait_ge(k_split, 16 * g + (2 * p + 2))
                for h in range(2):
                    if p > 0 or not first:
                        pe.wait_ge(exp_done, 16 * g + (2 * p + h - 1 if p > 0 else 0))
                    nc.tensor.matmul(S_BANK[h][:, :], ident16[:, :], mask16[:, :], start=True, stop=False)
                    for b in range(2 * h, 2 * h + 2):
                        t = slice(b * P, (b + 1) * P)
                        last = three(S_BANK[h][:, (b % 2) * 256:(b % 2) * 256 + 256], q_hi[:, t], q_lo[:, t],
                                     k_hi[:, b, :, :].rearrange("p h k -> p (h k)"),
                                     k_lo[:, b, :, :].rearrange("p h k -> p (h k)"), False, b % 2 == 1)
                    last.then_inc(s_full, 1)

            def transpose_probs(g, p):
                for h in range(2):
                    pe.wait_ge(pn_ready, 16 * g + (2 * p + h + 1))
                    if h == 0 and p > 0:
                        pe.wait_ge(ptA_ready, 8 * g + p)
                    if h == 1 and p > 0:
                        pe.wait_ge(ptB_ready, 8 * g + p)
                    for j in range(4):
                        last = nc.tensor.transpose(T_BANK[h][:, j * P:(j + 1) * P], probs[:, p % 2, 4 * h + j, :], ident[:, :])
                    last.then_inc(t_full, 1)

            def context(g, p, first):
                if p > 0 or not first:
                    pe.wait_ge(ctx_split, 8 * g + p)
                for b in range(GB):
                    if b == 0:
                        pe.wait_ge(ptA_ready, 8 * g + (p + 1))
                    if b == 2:
                        pe.wait_ge(ptB_ready, 8 * g + (p + 1))
                    for h in range(2):
                        last = nc.tensor.matmul(V_BANK[E * h:E * h + E, b * P:(b + 1) * P],
                                                vh[:, b, (2 * p + h) * E:(2 * p + h + 1) * E],
                                                pT[:, 2 * b + h, :], start=True, stop=True)
                last.then_inc(pv_full, 1)

            def project_out(g, p, first):
                pe.wait_ge(ctx_split, 8 * g + (p + 1))
                if p == 0 and not first:
                    pe.wait_ge(o_split, g)
                last = three(O_BANK[:, :], wo_hi[:, p, :], wo_lo[:, p, :], ctx_hi[:, p % 2, :], ctx_lo[:, p % 2, :],
                             p == 0, p == NP - 1)
                last.then_inc(o_used if p < NP - 1 else oacc_full, 1)

            def group(g, first, last):
                pe.wait_ge(xt_split, 4 * g + GB)
                pe.wait_ge(halo_done, 2 * g + 2)
                for m in range(3):
                    for k in range(NK):
                        c = slice(CH[m] * P, (CH[m] + 1) * P)
                        t = slice(k // KT, k // KT + GT)
                        done = three(CONV_BANK[m][:, :], cw_hi[:, k, c], cw_lo[:, k, c], xt_hi[:, k % KT, t],
                                     xt_lo[:, k % KT, t], k == 0, k == NK - 1)
                    done.then_inc(conv_full, 1)
                pe.wait_ge(qkv_split, 3 * g + 3)
                if not first:
                    pe.wait_ge(pj_evac, 4 * g)
                project_qk(g, 0, NW)
                for u in range(2 * GB):
                    if u >= 2:
                        pe.wait_ge(vh_ready, 8 * g + (u - 1))
                    t = slice((u // 2) * P, (u // 2 + 1) * P)
                    c = slice((u % 2) * 512, (u % 2) * 512 + 512)
                    three(T_BANK[u % 2][:, :], qkv_hi[:, 0, t], qkv_lo[:, 0, t], wv_hi[:, c], wv_lo[:, c],
                          True, True).then_inc(v_full, 1)
                for p in range(NP + 2):
                    if p < NP:
                        scores(g, p, first)
                    if p + 1 < NP:
                        project_qk(g, p + 1, 0)
                    if p == 1:
                        pe.wait_ge(vh_ready, 8 * g + 8)
                    if not last and p - 1 in X_SLOTS:
                        pe.wait_ge(xt_split, 4 * g + (GB + X_SLOTS.index(p - 1) + 1))
                    if 1 <= p <= NP:
                        transpose_probs(g, p - 1)
                        context(g, p - 1, first)
                    if p >= 2:
                        project_out(g, p - 2, first)
                    if not last and p in X_SLOTS:
                        b = X_SLOTS.index(p)
                        pe.wait_ge(xn_ready, 4 * g + (GB + b + 1))
                        x_transposes(T_BANK[0], b)
                pe.wait_ge(o_split, g + 1)
                for b in range(GB):
                    if b >= 2:
                        pe.wait_ge(pj_evac, 4 * g + (b - 1))
                    t = slice(b * P, (b + 1) * P)
                    three(PJ_BANK[b % 2][:, :], o_hi[:, t], o_lo[:, t], pj_hi[:, :], pj_lo[:, :], True, True).then_inc(pj_full, 1)

            group(0, True, False)
            with pe.Fori(1, NG - 1) as g:
                group(g, False, False)
            group(NG - 1, False, True)

            pe.wait_ge(ffn_in, 16 * N_FFN)
            for k in range(KT):
                if k >= 2:
                    pe.wait_ge(wT_ready, k - 1)
                for t in range(KT):
                    last = nc.tensor.transpose(T_BANK[k % 2][:, t * P:(t + 1) * P], w_raw[:, t, k * P:(k + 1) * P], ident[:, :])
                last.then_inc(wT_full, 1)
            for t in range(KT):
                last = nc.tensor.transpose(V_BANK[:, t * P:(t + 1) * P], b_raw[:, t, :, :].rearrange("p e r -> p (e r)"), ident[:, :])
            last.then_inc(bT_full, 1)
            for k in range(KT):
                last = nc.tensor.transpose(S_BANK[0][:, k * NE:(k + 1) * NE], r_raw[:, k * P:(k + 1) * P], ident[0:NE, 0:NE])
            last.then_inc(bT_full, 1)
            pe.wait_ge(acc_done, NBLK)
            for k in range(KT):
                last = nc.tensor.matmul(O_BANK[:, k * P:(k + 1) * P], acc[:, k * P:(k + 1) * P], ones[:, :], start=True, stop=True)
            last.then_inc(sum_full, 1)
            pe.wait_ge(mean_ready, 1)
            pe.wait_ge(rT_ready, 1)
            for k in range(KT):
                last = nc.tensor.matmul(O_BANK[:, 0:NE], colmean[:, k, :], rT[:, k, :], start=k == 0, stop=k == KT - 1)
            last.then_inc(logit_full, 1)
            pe.wait_ge(wT_ready, KT)
            pe.wait_ge(bs_ready, 1)
            for k in range(KT):
                nc.tensor.matmul(LORA_BANK[k][:, :], a_raw[:, k * P:(k + 1) * P], bT[:, :], start=True, stop=True).then_inc(lora_full, 1)

            def x2_transposes(n, s):
                pe.wait_ge(x2_ready, n)
                for k in range(KT):
                    last = nc.tensor.transpose(X2_BANK[s][:, k * P:(k + 1) * P], x2n[:, s, k * P:(k + 1) * P], ident[:, :])
                last.then_inc(x2_full, 1)

            def ffn(n, s, next_too, x2_free):
                if next_too:
                    if x2_free is not None:
                        pe.wait_ge(x2_split, x2_free)
                    x2_transposes(n + 2, 1 - s)
                pe.wait_ge(x2_split, n + 1)
                for k in range(KT):
                    last = three(Y_BANK[s][:, :], x2T_hi[:, s, k, :], x2T_lo[:, s, k, :], we_hi[:, k, :], we_lo[:, k, :],
                                 k == 0, k == KT - 1)
                last.then_inc(y_full, 1)

            pe.wait_ge(we_ready, 2)
            x2_transposes(1, 0)
            pe.wait_ge(we_split, KT)
            ffn(0, 0, True, None)
            ffn(1, 1, True, 1)
            with pe.Fori(1, NBLK // 2 - 1) as i:
                n0 = 2 * i
                for s in range(2):
                    pe.wait_ge(y_ready, n0 + (s - 1))
                    ffn(n0 + s, s, True, n0 + s)
            for n in (NBLK - 2, NBLK - 1):
                pe.wait_ge(y_ready, n - 1)
                ffn(n, n % 2, n == NBLK - 2, n)


_INS = ['L0_attn_inputs', 'L0_attn_conv_w', 'L0_attn_conv_b', 'L0_attn_wq', 'L0_attn_bq', 'L0_attn_wk', 'L0_attn_bk',
        'L0_attn_wv', 'L0_attn_bv', 'L0_attn_wo', 'L0_attn_bo', 'L0_attn_proj_w', 'L0_attn_proj_b', 'L0_ffn_W',
        'L0_ffn_b', 'L0_ffn_A', 'L0_ffn_B', 'L0_ffn_router_W', 'L0_ffn_router_b']
_OUTS = [((1, 2048, 512), 'float32')]


def kernel(**inputs):
    import numpy as _np
    import concourse.bacc as _bacc
    from concourse import mybir as _mybir
    from concourse.bass_utils import run_bass_kernel_spmd as _run

    nc = _bacc.Bacc("TRN2", target_bir_lowering=False, num_devices=1)
    arrays, args = {}, []
    for name in _INS:
        a = _np.ascontiguousarray(inputs[name])
        arrays[f"in_{name}_dram"] = a
        args.append(nc.dram_tensor(f"in_{name}_dram", a.shape, _mybir.dt.from_np(a.dtype), kind="ExternalInput").ap())
    for i, (shape, dtype) in enumerate(_OUTS):
        dt = _mybir.dt.from_np(_np.dtype(dtype))
        args.append(nc.dram_tensor(f"out_{i}_dram", shape, dt, kind="ExternalOutput").ap())
    attention_ffn_sandwich(nc, *args)
    r = _run(nc, [arrays], core_ids=[0])
    return r.results[0]["out_0_dram"]
```

```python
from contextlib import ExitStack

import concourse.bass as bass
from concourse import mybir

F32 = mybir.dt.float32
F32R = mybir.dt.float32r
BF16 = mybir.dt.bfloat16
ALU = mybir.AluOpType
ACT = mybir.ActivationFunctionType
AX_X = mybir.AxisListType.X

P = 128
EPS = 1e-5
MASKED = -1e9
LORA_SCALING = 2.0
Q_START, Q_END = 107, -1


def attention_ffn_sandwich(
    nc: bass.Bass, x: bass.AP, conv_w: bass.AP, conv_b: bass.AP,
    wq: bass.AP, bq: bass.AP, wk: bass.AP, bk: bass.AP, wv: bass.AP, bv: bass.AP,
    wo: bass.AP, bo: bass.AP, proj_w: bass.AP, proj_b: bass.AP,
    ffn_w: bass.AP, ffn_b: bass.AP, lora_a: bass.AP, lora_b: bass.AP,
    router_w: bass.AP, router_b: bass.AP, out: bass.AP,
):
    _, L, D = x.shape
    C, H, E = wq.shape
    TAPS = conv_w.shape[0]
    NE, R = lora_a.shape[:2]
    KT = D // P
    NBLK = L // P
    GB = 4
    GT = GB * P
    NG = NBLK // GB
    NP = H // 2
    NK = TAPS * KT
    NH = NK // 2
    SCALE = float(E) ** -0.5
    assert D == 512 and C == P and 2 * E == P and TAPS == 3 and NE * R == P and GT == 512

    xd = x.rearrange("a (g b p) d -> g p (a b) d", p=P, b=GB)
    xrow = x.rearrange("a l d -> (a l) d")
    outd = out.rearrange("a (n p) d -> n p (a d)", p=P)
    convd = conv_w.rearrange("j c n -> (j c) n").rearrange("(i t p) n -> i p t n", p=P, t=2)

    with ExitStack() as ctx:
        def sb(name, shape, dt=F32, scope=ctx):
            return scope.enter_context(nc.sbuf_tensor(name, shape, dt))

        def bank(name):
            return ctx.enter_context(nc.psum_tensor(name, [P, 512], F32))

        def sem(name):
            return ctx.enter_context(nc.semaphore(name))

        x1 = sb("x1", [P, NBLK, D])
        rows = sb("rows", [P, GB, D])
        ident = sb("ident", [P, P])
        stats2 = sb("stats2", [P, NBLK, 2])
        def norm_set(name, n=GB):
            return (sb(f"{name}_raw_sb", [P, n, 6]), sb(f"{name}_mv", [P, n, 2]), sb(f"{name}_ve", [P, n]),
                    sb(f"{name}_rs", [P, n]))

        raw_1, mv_1, ve_1, rs_1 = norm_set("in", NBLK)
        raw_o, mv_o, ve_o, rs_o = norm_set("attn")
        raw_2, mv_2, ve_2, rs_2 = norm_set("mid")
        neg_half, eps_sb = sb("neg_half", [P, NBLK]), sb("eps_sb", [P, NBLK])
        rowmask = sb("rowmask", [P, NBLK])
        avg_w = sb("avg_w", [P, NBLK])
        avg_m = sb("avg_m", [P, NBLK])
        avg_ms = sb("avg_ms", [P, 1])
        acc = sb("acc", [P, D])
        ones = sb("ones", [P, P])

        ph1 = ExitStack()
        cw_hi = sb("cw_hi", [P, NK, 3 * C], F32R, ph1)
        cw_lo = sb("cw_lo", [P, NK, 3 * C], F32R, ph1)
        ph1.close()
        ph2 = ExitStack()
        w_raw = sb("w_raw", [P, KT, D], F32, ph2)
        a_raw = sb("a_raw", [P, D], F32, ph2)
        b_raw = sb("b_raw", [P, KT, NE, R], F32, ph2)
        r_raw = sb("r_raw", [NE, D], F32, ph2)
        y_bias = sb("y_bias", [P, D], F32, ph2)
        wT_hi, wT_lo = sb("wT_hi", [P, KT, D], F32R, ph2), sb("wT_lo", [P, KT, D], F32R, ph2)
        bT = sb("bT", [P, D], F32, ph2)
        ph2.close()
        hold = sb("hold", [P, 2 * NK * 3 * C])

        r_bias = sb("r_bias", [P, NE])
        rT = sb("rT", [P, KT, NE])
        expert = sb("expert", [P, NE])
        logit, lexp, lpick = sb("logit", [P, NE]), sb("lexp", [P, NE]), sb("lpick", [P, NE])
        nlmax, lsum, lrec = sb("nlmax", [P, 1]), sb("lsum", [P, 1]), sb("lrec", [P, 1])
        route, route2 = sb("route", [P, 1]), sb("route2", [P, 1])
        y_nmr = sb("y_nmr", [P, GB])

        wqk = sb("wqk", [P, 4, H * E], F32R)
        wq_hi, wq_lo, wk_hi, wk_lo = wqk[:, 0, :], wqk[:, 1, :], wqk[:, 2, :], wqk[:, 3, :]
        wv_hi, wv_lo = sb("wv_hi", [P, H * E], F32R), sb("wv_lo", [P, H * E], F32R)
        wo_hi, wo_lo = sb("wo_hi", [P, NP, C], F32R), sb("wo_lo", [P, NP, C], F32R)
        pj_hi, pj_lo = sb("pj_hi", [P, D], F32R), sb("pj_lo", [P, D], F32R)
        NB = 3 * NP + 3 + 1
        bias_rows, biases, bq_sc = sb("bias_rows", [NB, P]), sb("biases", [P, NB]), sb("bq_sc", [P, NP])
        bk_sb, bv_sb = biases[:, NP:2 * NP], biases[:, 2 * NP:3 * NP]
        conv_bias, bo_sb = biases[:, 3 * NP:3 * NP + 3], biases[:, 3 * NP + 3:NB]
        pb_sb = sb("pb_sb", [P, D])
        ident16 = sb("ident16", [P, P], BF16)
        mask16 = sb("mask16", [P, 4 * P], BF16)
        edge = sb("edge", [2 * NG, D])
        edge_bn, edge_mv = sb("edge_bn", [2 * NG, 6]), sb("edge_mv", [2 * NG, 2])
        edge_hi, edge_lo = sb("edge_hi", [P, KT, 2 * NG], F32R), sb("edge_lo", [P, KT, 2 * NG], F32R)
        xn = sb("xn", [P, 2, D])
        xt_hi, xt_lo = sb("xt_hi", [P, KT, GT + 2], F32R), sb("xt_lo", [P, KT, GT + 2], F32R)
        qkv_hi, qkv_lo = sb("qkv_hi", [P, 3, GT], F32R), sb("qkv_lo", [P, 3, GT], F32R)
        work = sb("work", [P, NBLK, D])
        vh = work[:, 0:8, :].rearrange("p (b u) n -> p b (u n)", u=2)
        probs = work[:, 8:12, :].rearrange("p a n -> p (a n)").rearrange("p (s c k) -> p s c k", s=2, k=P)
        qT, kT = work[:, 12:14, :], work[:, 14:16, :]
        nmax = sb("nmax", [P, 2, 8])
        rsum = sb("rsum", [P, 2, 8])
        rinv = sb("rinv", [P, 2, 8])
        pT = sb("pT", [P, 8, P])
        ctx_hi, ctx_lo = sb("ctx_hi", [P, 2, GT], F32R), sb("ctx_lo", [P, 2, GT], F32R)
        o_hi, o_lo = sb("o_hi", [P, GT], F32R), sb("o_lo", [P, GT], F32R)

        S_BANK = [bank("scores0"), bank("scores1")]
        Q_BANK, K_BANK = bank("proj_q"), bank("proj_k")
        T_BANK = [bank("trans0"), bank("trans1")]
        V_BANK = bank("context")
        O_BANK = bank("attn_out")
        CONV_BANK = [Q_BANK, K_BANK, V_BANK]
        VH_BANK = [T_BANK[0], T_BANK[1], V_BANK]
        PJ_BANK = [S_BANK[0], S_BANK[1], O_BANK]

        x_first = [sem(f"x_first{b}") for b in range(GB)]
        x_rest, edge_in, small_in = sem("x_rest"), sem("edge_in"), sem("small_in")
        w_in = [sem(f"w_in{i}") for i in range(4)]
        ffn_in = sem("ffn_in")
        out_done = sem("out_done")
        pool_const, dve_const, bias_done = sem("pool_const"), sem("dve_const"), sem("bias_done")
        bias_full = sem("bias_full")
        w_hi_done, w_split = sem("w_hi_done"), sem("w_split")
        edge_zero, edge_step, edge_n, edge_full = sem("edge_zero"), sem("edge_step"), sem("edge_n"), sem("edge_full")
        edge_hi_done, edge_split = sem("edge_hi_done"), sem("edge_split")
        edge_var, edge_rstd = sem("edge_var"), sem("edge_rstd")
        ln1_raw, ln1_stats, ln1_var, ln1_rstd = sem("ln1_raw"), sem("ln1_stats"), sem("ln1_var"), sem("ln1_rstd")
        xn_ready, xt_full, xt_hi_done, xt_split = sem("xn_ready"), sem("xt_full"), sem("xt_hi_done"), sem("xt_split")
        halo_done, conv_full, qkv_hi_done, qkv_split = sem("halo_done"), sem("conv_full"), sem("qkv_hi_done"), sem("qkv_split")
        v_full, vh_act, vh_dve = sem("v_full"), sem("vh_act"), sem("vh_dve")
        q_full, k_full, q_ready, k_ready = sem("q_full"), sem("k_full"), sem("q_ready"), sem("k_ready")
        s_full, nmax_ready, exp_done, rinv_ready = sem("s_full"), sem("nmax_ready"), sem("exp_done"), sem("rinv_ready")
        pn_ready, t_full = sem("pn_ready"), sem("t_full")
        ptA_ready, ptB_ready = sem("ptA_ready"), sem("ptB_ready")
        pv_full, ctx_hi_done, ctx_split, o_used = sem("pv_full"), sem("ctx_hi_done"), sem("ctx_split"), sem("o_used")
        oacc_full, o_hi_done, o_split, pj_full, pj_evac = sem("oacc_full"), sem("o_hi_done"), sem("o_split"), sem("pj_full"), sem("pj_evac")
        lno_raw, lno_stats, lno_var, lno_rstd = sem("lno_raw"), sem("lno_stats"), sem("lno_var"), sem("lno_rstd")
        on_ready, x1_ready = sem("on_ready"), sem("x1_ready")
        ln2_raw, ln2_stats, ln2_var, ln2_rstd, ln2_kept = sem("ln2_raw"), sem("ln2_stats"), sem("ln2_var"), sem("ln2_rstd"), sem("ln2_kept")
        acc_done = sem("acc_done")
        exp_mark, expert_ready = sem("exp_mark"), sem("expert_ready")
        wT_full, wT_hi_done = sem("wT_full"), sem("wT_hi_done")
        aT_full, aT_hi_done = sem("aT_full"), sem("aT_hi_done")
        bT_full, bT_ready, rT_full, rT_ready = sem("bT_full"), sem("bT_ready"), sem("rT_full"), sem("rT_ready")
        avg_step = sem("avg_step")
        sum_full, mean_ready, logit_full, route_step, lexp_ready = sem("sum_full"), sem("mean_ready"), sem("logit_full"), sem("route_step"), sem("lexp_ready")
        bs_ready, bs_hi_done, bs_split = sem("bs_ready"), sem("bs_hi_done"), sem("bs_split")
        x2_ready, x2_full, x2_hi_done, x2_split = sem("x2_ready"), sem("x2_full"), sem("x2_hi_done"), sem("x2_split")
        base_full, tt_full, tt_hi_done = sem("base_full"), sem("tt_full"), sem("tt_hi_done")
        base_free = sem("base_free")
        tt_split = sem("tt_split")
        y_scaled = sem("y_scaled")
        y_full, y_ready, y_raw, y_stats, y_var, y_rstd = sem("y_full"), sem("y_ready"), sem("y_raw"), sem("y_stats"), sem("y_var"), sem("y_rstd")
        last_yn, last_res = sem("last_yn"), sem("last_res")
        yn_ready, res_ready = sem("yn_ready"), sem("res_ready")

        x2T_hi = xt_hi[:, :, 0:GT].rearrange("p k (s t) -> p s k t", s=2)
        x2T_lo = xt_lo[:, :, 0:GT].rearrange("p k (s t) -> p s k t", s=2)
        x2n = xn
        base = work
        tT_hi = wqk[:, 0:2, :].rearrange("p a n -> p (a n)")
        tT_lo = wqk[:, 2:4, :].rearrange("p a n -> p (a n)")
        aT_hi = ctx_hi[:, 0, :].rearrange("p (k c) -> p k c", k=KT)
        aT_lo = ctx_lo[:, 0, :].rearrange("p (k c) -> p k c", k=KT)
        bS_hi, bS_lo = ctx_hi[:, 1, :], ctx_lo[:, 1, :]
        colmean = pT[:, 0:KT, :]
        X2_BANK, BASE_BANK, TT_BANK, Y_BANK = T_BANK, [Q_BANK, K_BANK], V_BANK, S_BANK
        NJ = NBLK // 2
        FREE = NJ // 2
        FINISH = [(0, 0, 0, 2), (1, 1, 1, 1), (1, 1, 1, 2), (1, 1, 1, 2)]
        NY = GB
        ON_POOL = NBLK - 2

        def finish(j, place):
            done = sum(sum(f) for f in FINISH[:j - FREE]) + sum(FINISH[j - FREE][:place])
            return range(done, done + FINISH[j - FREE][place])

        CHUNKS = [2, 3, 0, 1, 4, 5]
        CONV_ORDER = [k for i in CHUNKS for k in (2 * i, 2 * i + 1)]
        def flat(t):
            return t[:, :, :].rearrange("p a n -> p (a n)")

        splits = [(flat(cw_hi)[:, i * 768:(i + 1) * 768], flat(cw_lo)[:, i * 768:(i + 1) * 768], 768, 1.0)
                  for i in CHUNKS]
        splits += [(wq_hi[:, :], wq_lo[:, :], H * E, SCALE), (wk_hi[:, :], wk_lo[:, :], H * E, 1.0),
                   (wv_hi[:, :], wv_lo[:, :], H * E, 1.0), (flat(wo_hi), flat(wo_lo), NP * C, 1.0),
                   (pj_hi[:, :], pj_lo[:, :], D, 1.0)]
        sources = [(convd[i], "p t n") for i in CHUNKS]
        sources += [(wq.rearrange("c h e -> c (h e)"), ""), (wk.rearrange("c h e -> c (h e)"), ""),
                    (wv.rearrange("c h e -> c (h e)"), ""),
                    (wo.rearrange("(p two) e w -> (two e) p w", two=2), "p t n"), (proj_w, "")]
        NW = len(splits)

        def landing(i):
            return vh[:, i % 4, 0:splits[i][2]]

        CH = [2, 0, 1]
        X_SLOTS = [3, 4, 6, 6]
        X_BANK = [T_BANK[0], T_BANK[0], Q_BANK, K_BANK]
        QK_AFTER = [0, 2]
        S_AFTER = 3
        CONV_PARTS = [range(0, 4), range(4, 8), range(8, 12)]
        N_SMALL = 6
        N_FFN = KT + 5
        block = ctx.enter_context(nc.Block())

        @block.sync
        def _(sp):
            for b in range(GB):
                sp.dma_start(x1[:, b, :], xd[0, :, b, :]).then_inc(x_first[b], 16)
            sp.wait_ge(edge_zero, 1)
            for g in range(NG):
                if g > 0:
                    sp.dma_start(edge[2 * g:2 * g + 1, :], xrow[g * GT - 1:g * GT, :]).then_inc(edge_in, 16)
                if g < NG - 1:
                    sp.dma_start(edge[2 * g + 1:2 * g + 2, :], xrow[(g + 1) * GT:(g + 1) * GT + 1, :]).then_inc(edge_in, 16)
            for i in range(NW):
                if i >= 4:
                    sp.wait_ge(w_split, i - 3)
                src, kind = sources[i]
                dst = landing(i)
                if kind:
                    dst = dst.rearrange("p (t n) -> p t n", n=src.shape[2])
                sp.dma_start(dst, src).then_inc(w_in[i % 4], 16)
            for g in range(1, NG):
                sp.dma_start(x1[:, g * GB:(g + 1) * GB, :], xd[g]).then_inc(x_rest, 16)
            sp.wait_ge(conv_full, 3 * NG)
            sp.dma_start(w_raw[:, :, :], ffn_w.rearrange("(t p) d -> p t d", p=P)).then_inc(ffn_in, 16)
            for t in range(KT):
                sp.dma_start(b_raw[:, t, :, :], lora_b[:, t * P:(t + 1) * P, :].rearrange("e p r -> p e r")).then_inc(ffn_in, 16)
            sp.dma_start(a_raw[:, :], lora_a.rearrange("e r d -> (e r) d")).then_inc(ffn_in, 16)
            sp.dma_start(r_raw[:, :], router_w).then_inc(ffn_in, 16)
            sp.dma_start(r_bias[:, :], router_b.rearrange("(a e) -> a e", a=1).broadcast_to([P, NE])).then_inc(ffn_in, 16)
            sp.dma_start(y_bias[:, :], ffn_b.rearrange("(a e) -> a e", a=1).broadcast_to([P, D])).then_inc(ffn_in, 16)

            def store(n):
                sp.dma_start(outd[n], base[:, n, :]).then_inc(out_done, 16)

            for n in range(ON_POOL):
                sp.wait_ge(res_ready, n + 1)
                store(n)
            for n in range(ON_POOL, NBLK):
                sp.wait_ge(last_res, n - ON_POOL + 1)
                store(n)
            sp.wait_ge(out_done, 16 * NBLK)

        def rsqrt_chain(pool, n, stats_sem, var_sem, done_sem, count, mv, ve, rs, half):
            pool.wait_ge(stats_sem, count)
            nc.gpsimd.tensor_tensor(ve, mv, eps_sb[0:ve.shape[0], 0:n], ALU.add).then_inc(var_sem, 1)
            pool.wait_ge(var_sem, count)
            nc.gpsimd.tensor_tensor(rs, ve, half, ALU.pow).then_inc(done_sem, 1)

        @block.gpsimd
        def _(pool):
            nc.gpsimd.memset(edge[:, :], 0.0).then_inc(edge_zero, 1)
            nc.gpsimd.memset(ident[:, :], 0.0).then_inc(pool_const, 1)
            nc.gpsimd.memset(neg_half[:, :], -0.5).then_inc(pool_const, 1)
            nc.gpsimd.memset(eps_sb[:, :], EPS).then_inc(pool_const, 1)
            pool.wait_ge(pool_const, 3)
            nc.gpsimd.affine_select(out=ident[:, :], in_=ident[:, :], compare_op=ALU.not_equal, fill=1.0,
                                    base=0, pattern=[[-1, P]], channel_multiplier=1).then_inc(pool_const, 1)
            def x_scales(b0, b1, n):
                rsqrt_chain(pool, b1 - b0, ln1_stats, ln1_var, ln1_rstd, n, mv_1[:, b0:b1, 1], ve_1[:, b0:b1],
                            rs_1[:, b0:b1], neg_half[:, b0:b1])

            x_scales(0, GB, 1)
            rsqrt_chain(pool, 1, edge_n, edge_var, edge_rstd, 1, edge_mv[:, 1:2], edge_bn[:, 0:1], edge_bn[:, 1:2],
                        neg_half[0:2 * NG, 0:1])
            pool.wait_ge(pool_const, 4)
            nc.gpsimd.tensor_copy(ident16[:, :], ident[:, :]).then_inc(pool_const, 1)
            nc.gpsimd.memset(mask16[:, :], 0.0).then_inc(pool_const, 1)
            nc.gpsimd.memset(rowmask[:, :], 1.0).then_inc(pool_const, 1)
            pool.wait_ge(pool_const, 7)
            nc.gpsimd.affine_select(out=mask16[:, :].rearrange("p (a k) -> p a k", k=P),
                                    in_=mask16[:, :].rearrange("p (a k) -> p a k", k=P),
                                    compare_op=ALU.is_ge, fill=MASKED, base=0,
                                    pattern=[[0, 4], [-1, P]], channel_multiplier=1).then_inc(pool_const, 1)
            nc.gpsimd.affine_select(out=rowmask[:, 0:1], in_=rowmask[:, 0:1], compare_op=ALU.is_ge, fill=0.0,
                                    base=-Q_START, pattern=[[0, 1]], channel_multiplier=1).then_inc(pool_const, 1)
            nc.gpsimd.affine_select(out=rowmask[:, NBLK - 1:NBLK], in_=rowmask[:, NBLK - 1:NBLK],
                                    compare_op=ALU.is_ge, fill=0.0, base=P - 1 + Q_END, pattern=[[0, 1]],
                                    channel_multiplier=-1).then_inc(pool_const, 1)

            def halo(g, at_edge):
                pool.wait_ge(edge_split, 1)
                for dst, src in ((xt_hi, edge_hi), (xt_lo, edge_lo)):
                    nc.gpsimd.tensor_copy(dst[:, :, 0:GT + 2:GT + 1], src[:, :, at_edge]).then_inc(halo_done, 1)

            halo(0, slice(0, 2))

            x_scales(GB, NBLK, 2)

            def x1_sums(g1, before, blocks=range(GB)):
                for b in blocks:
                    pool.wait_ge(on_ready, before + (b + 1))
                    xb = x1[:, bass.ds(4 * g1 + b, 1), :].rearrange("p a d -> p (a d)")
                    nc.gpsimd.tensor_tensor(xb, xb, rows[:, b, :], ALU.add).then_inc(x1_ready, 1)

            def x1_scales(g1, n):
                rsqrt_chain(pool, GB, ln2_stats, ln2_var, ln2_rstd, n, mv_2[:, :, 1], ve_2[:, :],
                            rs_2[:, :], neg_half[:, 0:GB])
                pool.wait_ge(ln2_rstd, n)
                nc.gpsimd.tensor_tensor(avg_w[:, bass.ds(4 * g1, 4)], rs_2[:, :], rowmask[:, bass.ds(4 * g1, 4)],
                                        ALU.mult).then_inc(ln2_kept, 1)
                nc.gpsimd.tensor_copy(stats2[:, bass.ds(4 * g1, 4), 0], mv_2[:, :, 0]).then_inc(ln2_kept, 1)
                nc.gpsimd.tensor_copy(stats2[:, bass.ds(4 * g1, 4), 1], rs_2[:, :]).then_inc(ln2_kept, 1)

            def attn_scales(n):
                rsqrt_chain(pool, GB, lno_stats, lno_var, lno_rstd, n, mv_o[:, :, 1], ve_o[:, :],
                            rs_o[:, :], neg_half[:, 0:GB])

            def group(g, first, last):
                if not last:
                    pool.wait_ge(conv_full, 3 * g + 3)
                    halo(g + 1, bass.ds(2 * g + 2, 2))
                if not first:
                    attn_scales(g)
                for p in range(NP):
                    for h in range(2):
                        pool.wait_ge(rinv_ready, 16 * g + (2 * p + h + 1))
                        part = probs[:, p % 2, 4 * h:4 * h + 4, :]
                        nc.gpsimd.tensor_tensor(
                            part, part, rinv[:, p % 2, 4 * h:4 * h + 4].unsqueeze(2).broadcast_to([P, 4, P]),
                            ALU.mult).then_inc(pn_ready, 1)
                    if p == 0 and not first:
                        x1_sums(g - 1, 4 * g - 4, range(0, 2))
                    if p == 1 and not first:
                        x1_sums(g - 1, 4 * g - 4, range(2, 4))
                    if p == 2 and not first:
                        x1_scales(g - 1, g)

            group(0, True, False)
            with pool.Fori(1, NG - 1) as g:
                group(g, False, False)
            group(NG - 1, False, True)
            attn_scales(NG)
            x1_sums(NG - 1, 4 * NG - 4)
            x1_scales(NG - 1, NG)
            pool.wait_ge(ln2_kept, 3 * NG)
            nc.gpsimd.tensor_tensor(avg_m[:, :], avg_w[:, :], stats2[:, :, 0], ALU.mult).then_inc(avg_step, 1)

            nc.gpsimd.memset(expert[:, :], 1.0).then_inc(exp_mark, 1)
            pool.wait_ge(exp_mark, 1)
            nc.gpsimd.affine_select(out=expert[:, :], in_=expert[:, :], compare_op=ALU.is_ge, fill=0.0, base=0,
                                    pattern=[[-R, NE]], channel_multiplier=1).then_inc(exp_mark, 1)
            pool.wait_ge(exp_mark, 2)
            nc.gpsimd.affine_select(out=expert[:, :], in_=expert[:, :], compare_op=ALU.is_ge, fill=0.0, base=R - 1,
                                    pattern=[[R, NE]], channel_multiplier=-1).then_inc(expert_ready, 1)

            def residual(n):
                pool.wait_ge(yn_ready, n + 1)
                nc.gpsimd.tensor_tensor(base[:, n, :], base[:, n, :], x1[:, n, :], ALU.add).then_inc(res_ready, 1)

            for n in range(NBLK):
                s = n % NY
                pool.wait_ge(y_stats, n + 1)
                nc.gpsimd.tensor_tensor(ve_o[:, s:s + 1], mv_o[:, s, 1:2], eps_sb[:, 0:1], ALU.add).then_inc(y_var, 1)
                pool.wait_ge(y_var, n + 1)
                nc.gpsimd.tensor_tensor(rs_o[:, s:s + 1], ve_o[:, s:s + 1], neg_half[:, s:s + 1], ALU.pow).then_inc(y_rstd, 1)
                if 2 <= n < ON_POOL + 2:
                    residual(n - 2)

        @block.scalar
        def _(act):
            for n, src in enumerate((bq, bk, bv)):
                act.dma_start(bias_rows[n * NP:(n + 1) * NP, :], src.rearrange("(p two) e -> p (two e)", two=2)).then_inc(small_in, 16)
            act.dma_start(bias_rows[3 * NP:3 * NP + 3, :], conv_b.rearrange("(m p) -> m p", p=P)).then_inc(small_in, 16)
            act.dma_start(bias_rows[3 * NP + 3:NB, :], bo.rearrange("(a p) -> a p", a=1)).then_inc(small_in, 16)
            act.dma_start(pb_sb[:, :], proj_b.rearrange("(a e) -> a e", a=1).broadcast_to([P, D])).then_inc(small_in, 16)

            def split_hi(i):
                act.wait_ge(w_in[i % 4], 16 * (i // 4 + 1))
                nc.scalar.activation(splits[i][0], landing(i), ACT.Copy, scale=splits[i][3]).then_inc(w_hi_done, 1)

            def xt_hi_part(n, b, bk):
                act.wait_ge(xt_full, n)
                nc.scalar.activation(xt_hi[:, :, 1 + b * P:1 + (b + 1) * P],
                                     bk[:, :].rearrange("p (k t) -> p k t", k=KT), ACT.Copy).then_inc(xt_hi_done, 1)

            for b in range(GB):
                xt_hi_part(b + 1, b, T_BANK[b % 2])
                if b == 2:
                    split_hi(0)
            act.wait_ge(edge_full, 1)
            nc.scalar.activation(edge_hi[:, :, :], V_BANK[:, 0:KT * 2 * NG].rearrange("p (k t) -> p k t", k=KT),
                                 ACT.Copy).then_inc(edge_hi_done, 1)
            for i in range(1, GB):
                split_hi(i)
            act.wait_ge(bias_full, 1)
            nc.scalar.activation(biases[:, :], S_BANK[0][:, 0:NB], ACT.Copy).then_inc(bias_done, 1)
            nc.scalar.activation(bq_sc[:, :], S_BANK[0][:, 0:NP], ACT.Copy, scale=SCALE).then_inc(bias_done, 1)
            for i in range(GB, NW):
                split_hi(i)
            act.wait_ge(bias_done, 2)

            def evac_qk(g, p):
                act.wait_ge(q_full, 8 * g + (p + 1))
                nc.scalar.activation(qT[:, p % 2, :], Q_BANK[:, :], ACT.Identity, bias=bq_sc[:, p:p + 1]).then_inc(q_ready, 1)
                act.wait_ge(k_full, 8 * g + (p + 1))
                nc.scalar.activation(kT[:, p % 2, :], K_BANK[:, :], ACT.Identity, bias=bk_sb[:, p:p + 1]).then_inc(k_ready, 1)

            def exps(g, p, h):
                act.wait_ge(nmax_ready, 16 * g + (2 * p + h + 1))
                if p >= 2:
                    act.wait_ge(t_full, 16 * g + (2 * (p - 2) + h + 1))
                for b in range(GB):
                    c = 4 * h + b
                    last = nc.scalar.activation(probs[:, p % 2, c, :], S_BANK[h][:, b * P:(b + 1) * P], ACT.Exp,
                                                bias=nmax[:, p % 2, c:c + 1], accum_out=rsum[:, p % 2, c:c + 1])
                last.then_inc(exp_done, 1)

            def conv_hi(m, n):
                act.wait_ge(conv_full, n)
                nc.scalar.activation(qkv_hi[:, m, :], CONV_BANK[m][:, :], ACT.Identity,
                                     bias=conv_bias[:, CH[m]:CH[m] + 1]).then_inc(qkv_hi_done, 1)

            def context_hi(g, p):
                act.wait_ge(pv_full, 8 * g + (p + 1))
                if p >= 2:
                    act.wait_ge(o_used, (NP - 1) * g + (p - 1))
                nc.scalar.activation(ctx_hi[:, p % 2, :], V_BANK[:, :], ACT.Identity,
                                     bias=bv_sb[:, p:p + 1]).then_inc(ctx_hi_done, 1)

            def wT_hi_part(k):
                act.wait_ge(wT_full, k + 1)
                nc.scalar.activation(wT_hi[:, k, :], BASE_BANK[k % 2][:, :], ACT.Copy).then_inc(wT_hi_done, 1)

            def group(g, last):
                for u in range(2 * GB):
                    if u == S_AFTER + 2:
                        exps(g, 0, 0)
                        exps(g, 0, 1)
                    if u % 2 == 0:
                        act.wait_ge(v_full, 8 * g + (u + 1))
                        nc.scalar.activation(vh[:, u // 2, 0:512], VH_BANK[u % 3][:, :], ACT.Copy).then_inc(vh_act, 1)
                    if u in QK_AFTER:
                        evac_qk(g, QK_AFTER.index(u))
                for p in range(NP):
                    if p > 0:
                        exps(g, p, 0)
                        exps(g, p, 1)
                    if p + 2 < NP:
                        evac_qk(g, p + 2)
                    if p >= 1:
                        context_hi(g, p - 1)
                    for b in range(GB):
                        if not last and X_SLOTS[b] == p:
                            xt_hi_part(4 * g + (GB + b + 1), b, X_BANK[b])
                if not last:
                    conv_hi(0, 3 * g + 4)
                else:
                    for k in range(KT):
                        wT_hi_part(k)
                context_hi(g, NP - 1)
                if not last:
                    conv_hi(1, 3 * g + 5)
                else:
                    act.wait_ge(bT_full, 1)
                    nc.scalar.activation(bT[:, :], T_BANK[0][:, :], ACT.Copy).then_inc(bT_ready, 1)
                    act.wait_ge(rT_full, 1)
                    nc.scalar.activation(rT[:, :, :], T_BANK[1][:, 0:KT * NE].rearrange("p (k e) -> p k e", k=KT),
                                         ACT.Copy).then_inc(rT_ready, 1)
                act.wait_ge(oacc_full, g + 1)
                nc.scalar.activation(o_hi[:, :], O_BANK[:, :], ACT.Identity, bias=bo_sb[:, 0:1]).then_inc(o_hi_done, 1)
                if not last:
                    conv_hi(2, 3 * g + 6)

            for m in range(3):
                conv_hi(m, m + 1)
            with act.Fori(0, NG - 1) as g:
                group(g, False)
            group(NG - 1, True)

            act.wait_ge(aT_full, 1)
            nc.scalar.activation(aT_hi[:, :, :], TT_BANK[:, :].rearrange("p (k c) -> p k c", k=KT), ACT.Copy).then_inc(aT_hi_done, 1)

            def x2_hi(j, b):
                act.wait_ge(x2_full, 2 * j + b + 1)
                nc.scalar.activation(x2T_hi[:, j % 2, :, b * P:(b + 1) * P],
                                     X2_BANK[b][:, :].rearrange("p (k t) -> p k t", k=KT), ACT.Copy).then_inc(x2_hi_done, 1)

            def x2_hi_pair(j):
                if j >= 2:
                    act.wait_ge(tt_full, j - 1)
                x2_hi(j, 0)
                x2_hi(j, 1)

            def tt_hi(j):
                act.wait_ge(tt_full, j + 1)
                nc.scalar.activation(tT_hi[:, 2 * j * P:2 * (j + 1) * P], TT_BANK[:, 0:2 * P], ACT.Copy).then_inc(tt_hi_done, 1)

            def y_norm(n):
                act.wait_ge(y_scaled, n + 1)
                nc.scalar.activation(base[:, n, :], base[:, n, :], ACT.Identity, bias=y_nmr[:, n % NY:n % NY + 1],
                                     scale=rs_o[:, n % NY:n % NY + 1]).then_inc(yn_ready, 1)

            x2_hi_pair(0)
            for j in range(NJ):
                if j < NJ - 1:
                    x2_hi_pair(j + 1)
                if j == FREE - 1:
                    tt_hi(j)
                    act.wait_ge(sum_full, 1)
                    nc.scalar.activation(colmean, O_BANK[:, :].rearrange("p (k t) -> p k t", k=KT), ACT.Copy,
                                         scale=1.0 / (L + Q_END - Q_START)).then_inc(mean_ready, 1)
                if j == FREE:
                    act.wait_ge(route_step, 2)
                    nc.scalar.activation(lexp[:, :], logit[:, :], ACT.Exp, bias=nlmax[:, 0:1],
                                         accum_out=lsum[:, 0:1]).then_inc(lexp_ready, 1)
                    act.wait_ge(bs_ready, 1)
                    nc.scalar.activation(bS_hi, bT[:, :], ACT.Copy).then_inc(bs_hi_done, 1)
                for place in range(4):
                    if place == 3 and j != FREE - 1:
                        tt_hi(j)
                    if j >= FREE:
                        for n in finish(j, place):
                            if n >= 2:
                                y_norm(n - 2)

        @block.vector
        def _(dve):
            nc.vector.memset(acc[:, :], 0.0).then_inc(acc_done, 1)
            nc.vector.memset(ones[:, :], 1.0).then_inc(dve_const, 1)

            def raw_waited(raw, count):
                count = count if type(count) is int else dve.to_reg(count)
                dve.wait_ge(dve_const, 1)
                dve.wait_ge(raw, count)

            def x_block(n):
                if type(n) is int:
                    return x1[:, n, :]
                return x1[:, bass.ds(n, 1), :].rearrange("p a d -> p (a d)")

            def aggregate(raw, mv, raw_sem, count, done):
                raw_waited(raw_sem, count)
                for b in range(GB):
                    last = nc.vector.bn_aggr(mv[:, b, :], raw[:, b, :])
                last.then_inc(done, 1)

            def ln1_statistics(b0, b1, n):
                for b in range(b0, b1):
                    if b < GB:
                        dve.wait_ge(x_first[b], 16)
                    nc.vector.bn_stats(raw_1[:, b, :], x1[:, b, :]).then_inc(ln1_raw, 1)
                raw_waited(ln1_raw, b1)
                for b in range(b0, b1):
                    last = nc.vector.bn_aggr(mv_1[:, b, :], raw_1[:, b, :])
                last.then_inc(ln1_stats, 1)

            def normed(gg, b, n_free):
                dve.wait_ge(ln1_rstd, 1 if type(gg) is int else 2)
                n = 4 * gg + b
                if type(gg) is int:
                    mean, rstd = mv_1[:, n, 0:1], rs_1[:, n:n + 1]
                else:
                    mean, rstd = mv_1[:, bass.ds(n, 1), 0:1].rearrange("p a c -> p (a c)"), rs_1[:, bass.ds(n, 1)]
                if n_free is not None:
                    dve.wait_ge(xt_full, n_free)
                nc.vector.tensor_scalar(xn[:, b % 2, :], x_block(n), mean, rstd,
                                        ALU.subtract, ALU.mult).then_inc(xn_ready, 1)

            def xt_lo_part(n, b, bk):
                dve.wait_ge(xt_hi_done, n)
                nc.vector.tensor_tensor(xt_lo[:, :, 1 + b * P:1 + (b + 1) * P], bk[:, :].rearrange("p (k t) -> p k t", k=KT),
                                        xt_hi[:, :, 1 + b * P:1 + (b + 1) * P].bitcast(F32), ALU.subtract).then_inc(xt_split, 1)

            def split_lo(i):
                dve.wait_ge(w_hi_done, i + 1)
                nc.vector.scalar_tensor_tensor(out=splits[i][1], in0=landing(i), scalar=splits[i][3],
                                               in1=splits[i][0].bitcast(F32), op0=ALU.mult,
                                               op1=ALU.subtract).then_inc(w_split, 1)

            ln1_statistics(0, GB, 1)
            for b in range(2):
                normed(0, b, None)
            dve.wait_ge(edge_in, 16 * (2 * NG - 2))
            nc.vector.bn_stats(edge_bn[:, :], edge[:, :]).then_inc(edge_step, 1)
            xt_lo_part(1, 0, T_BANK[0])
            normed(0, 2, 1)
            dve.wait_ge(edge_step, 1)
            nc.vector.bn_aggr(edge_mv[:, :], edge_bn[:, :]).then_inc(edge_n, 1)
            xt_lo_part(2, 1, T_BANK[1])
            normed(0, 3, 2)
            xt_lo_part(3, 2, T_BANK[0])
            dve.wait_ge(edge_rstd, 1)
            nc.vector.tensor_scalar(edge[:, :], edge[:, :], edge_mv[:, 0:1], edge_bn[:, 1:2],
                                    ALU.subtract, ALU.mult).then_inc(edge_step, 1)
            split_lo(0)
            xt_lo_part(4, 3, T_BANK[1])
            dve.wait_ge(edge_hi_done, 1)
            nc.vector.tensor_tensor(edge_lo[:, :, :], V_BANK[:, 0:KT * 2 * NG].rearrange("p (k t) -> p k t", k=KT),
                                    edge_hi[:, :, :].bitcast(F32), ALU.subtract).then_inc(edge_split, 1)
            for i in range(1, GB):
                split_lo(i)
            for i in range(GB, NW):
                split_lo(i)
            dve.wait_ge(small_in, 16 * N_SMALL)
            dve.wait_ge(bias_done, 2)

            def conv_lo(m, n):
                dve.wait_ge(qkv_hi_done, n)
                nc.vector.scalar_tensor_tensor(
                    out=qkv_lo[:, m, :], in0=CONV_BANK[m][:, :], scalar=conv_bias[:, CH[m]:CH[m] + 1],
                    in1=qkv_hi[:, m, :].bitcast(F32), op0=ALU.add, op1=ALU.subtract).then_inc(qkv_split, 1)

            def row_max(g, p, h):
                dve.wait_ge(s_full, 16 * g + (2 * p + h + 1))
                nc.vector.tensor_reduce(nmax[:, p % 2, 4 * h:4 * h + 4], S_BANK[h][:, :].rearrange("p (a k) -> p a k", a=4),
                                        op=ALU.max, axis=AX_X, negate=True).then_inc(nmax_ready, 1)

            def values_out(g, u):
                dve.wait_ge(v_full, 8 * g + (u + 1))
                nc.vector.tensor_copy(vh[:, u // 2, 512:1024], VH_BANK[u % 3][:, :]).then_inc(vh_dve, 1)

            def row_inv(g, p, h):
                dve.wait_ge(exp_done, 16 * g + (2 * p + h + 1))
                nc.vector.reciprocal(rinv[:, p % 2, 4 * h:4 * h + 4], rsum[:, p % 2, 4 * h:4 * h + 4]).then_inc(rinv_ready, 1)

            def probs_back(g, p, h):
                dve.wait_ge(t_full, 16 * g + (2 * p + h + 1))
                nc.vector.tensor_copy(pT[:, 4 * h:4 * h + 4, :], T_BANK[h][:, :].rearrange("p (a k) -> p a k", a=4)
                                      ).then_inc(ptA_ready if h == 0 else ptB_ready, 1)

            def context_lo(g, p):
                dve.wait_ge(ctx_hi_done, 8 * g + (p + 1))
                nc.vector.scalar_tensor_tensor(out=ctx_lo[:, p % 2, :], in0=V_BANK[:, :], scalar=bv_sb[:, p:p + 1],
                                               in1=ctx_hi[:, p % 2, :].bitcast(F32), op0=ALU.add,
                                               op1=ALU.subtract).then_inc(ctx_split, 1)

            def attn_row_statistics(b):
                nc.vector.bn_stats(raw_o[:, b, :], rows[:, b, :]).then_inc(lno_raw, 1)

            def attn_statistics(n):
                for b in range(GB):
                    attn_row_statistics(b)
                aggregate(raw_o, mv_o, lno_raw, 4 * n, lno_stats)

            def attn_norm(n):
                dve.wait_ge(lno_rstd, n)
                for b in range(GB):
                    nc.vector.tensor_scalar(rows[:, b, :], rows[:, b, :], mv_o[:, b, 0:1], rs_o[:, b:b + 1],
                                            ALU.subtract, ALU.mult).then_inc(on_ready, 1)

            def x1_statistics(n, before):
                for b in range(GB):
                    dve.wait_ge(x1_ready, before + (b + 1))
                    nc.vector.bn_stats(raw_2[:, b, :], x_block(before + b)).then_inc(ln2_raw, 1)
                aggregate(raw_2, mv_2, ln2_raw, 4 * n, ln2_stats)

            def x1_averaged(n, before, blocks=range(GB)):
                dve.wait_ge(ln2_kept, 3 * n)
                for b in blocks:
                    dve.wait_ge(acc_done, before + (b + 1))
                    nc.vector.scalar_tensor_tensor(out=acc[:, :], in0=x_block(before + b), scalar=row_weight(before + b),
                                                   in1=acc[:, :], op0=ALU.mult, op1=ALU.add).then_inc(acc_done, 1)

            def row_weight(n):
                if type(n) is int:
                    return avg_w[:, n:n + 1]
                return avg_w[:, bass.ds(n, 1)]

            def wT_lo_part(k):
                dve.wait_ge(wT_hi_done, k + 1)
                nc.vector.tensor_tensor(wT_lo[:, k, :], BASE_BANK[k % 2][:, :], wT_hi[:, k, :].bitcast(F32),
                                        ALU.subtract).then_inc(base_free, 1)

            def group(g, first, last):
                for p in range(NP):
                    if p >= 1:
                        row_inv(g, p - 1, 1)
                    for b in range(GB):
                        if not last and X_SLOTS[b] == p - 1:
                            xt_lo_part(4 * g + (GB + b + 1), b, X_BANK[b])
                    if p >= 2:
                        context_lo(g, p - 2)
                    if p == 0:
                        values_out(g, 1)
                        if not first:
                            attn_statistics(g)
                        values_out(g, 3)
                    row_max(g, p, 0)
                    row_max(g, p, 1)
                    if p == 0:
                        values_out(g, 5)
                        values_out(g, 7)
                    if p >= 1:
                        probs_back(g, p - 1, 0)
                        probs_back(g, p - 1, 1)
                    row_inv(g, p, 0)
                    if p == 0 and not first:
                        attn_norm(g)
                    if p == 2 and not first:
                        x1_statistics(g, 4 * g - 4)
                    if p == 3 and not first:
                        x1_averaged(g, 4 * g - 4, range(0, 2))
                    if p == 4 and not first:
                        x1_averaged(g, 4 * g - 4, range(2, 4))
                    for b in range(GB):
                        if not last and X_SLOTS[b] == p + 1:
                            normed(g + 1, b, 4 * g + (b + 3))
                if last:
                    x2_norm(0)
                    x2_norm(1)
                row_inv(g, NP - 1, 1)
                context_lo(g, NP - 2)
                probs_back(g, NP - 1, 0)
                probs_back(g, NP - 1, 1)
                if not last:
                    conv_lo(0, 3 * g + 4)
                else:
                    for k in range(KT):
                        wT_lo_part(k)
                context_lo(g, NP - 1)
                if not last:
                    conv_lo(1, 3 * g + 5)
                dve.wait_ge(o_hi_done, g + 1)
                nc.vector.scalar_tensor_tensor(out=o_lo[:, :], in0=O_BANK[:, :], scalar=bo_sb[:, 0:1],
                                               in1=o_hi[:, :].bitcast(F32), op0=ALU.add, op1=ALU.subtract).then_inc(o_split, 1)
                if not last:
                    conv_lo(2, 3 * g + 6)
                if last:
                    x2_lo(0, 0)
                    x2_lo(0, 1)
                    x2_norm(2)
                    x2_norm(3)
                    dve.wait_ge(aT_hi_done, 1)
                    nc.vector.tensor_tensor(aT_lo[:, :, :], TT_BANK[:, :].rearrange("p (k c) -> p k c", k=KT),
                                            aT_hi[:, :, :].bitcast(F32), ALU.subtract).then_inc(tt_split, 1)
                if not first:
                    dve.wait_ge(x1_ready, 4 * g)
                for b in range(GB):
                    dve.wait_ge(pj_full, 4 * g + (b + 1))
                    nc.vector.tensor_tensor(rows[:, b, :], PJ_BANK[b % 3][:, :], pb_sb[:, :], ALU.add).then_inc(pj_evac, 1)
                dve.wait_ge(pj_evac, 4 * g + GB)

            def x2_lo(j, b):
                dve.wait_ge(x2_hi_done, 2 * j + b + 1)
                nc.vector.tensor_tensor(x2T_lo[:, j % 2, :, b * P:(b + 1) * P], X2_BANK[b][:, :].rearrange("p (k t) -> p k t", k=KT),
                                        x2T_hi[:, j % 2, :, b * P:(b + 1) * P].bitcast(F32), ALU.subtract).then_inc(x2_split, 1)

            def x2_norm(n):
                dve.wait_ge(ln2_kept, 3 * (n // GB + 1))
                if n >= 2:
                    dve.wait_ge(x2_full, n - 1)
                nc.vector.tensor_scalar(x2n[:, n % 2, :], x1[:, n, :], stats2[:, n, 0:1], stats2[:, n, 1:2],
                                        ALU.subtract, ALU.mult).then_inc(x2_ready, 1)

            conv_lo(0, 1)
            conv_lo(1, 2)
            dve.wait_ge(x_rest, 16 * (NG - 1))
            ln1_statistics(GB, NBLK, 2)
            conv_lo(2, 3)
            group(0, True, False)
            with dve.Fori(1, NG - 1) as g:
                group(g, False, False)
            group(NG - 1, False, True)
            dve.wait_ge(ffn_in, 16 * N_FFN)

            def base_out(n):
                dve.wait_ge(base_full, n + 1)
                nc.vector.tensor_tensor(base[:, n, :], BASE_BANK[n % 2][:, :], y_bias[:, :], ALU.add).then_inc(base_free, 1)

            def tt_lo(j):
                dve.wait_ge(tt_hi_done, j + 1)
                t = slice(2 * j * P, 2 * (j + 1) * P)
                nc.vector.tensor_tensor(tT_lo[:, t], TT_BANK[:, 0:2 * P], tT_hi[:, t].bitcast(F32), ALU.subtract).then_inc(tt_split, 1)

            def y_sum(n):
                dve.wait_ge(y_full, n + 1)
                nc.vector.tensor_tensor(base[:, n, :], Y_BANK[n % 2][:, :], base[:, n, :], ALU.add).then_inc(y_ready, 1)

            def y_statistics(n):
                dve.wait_ge(y_ready, n + 1)
                nc.vector.bn_stats(raw_o[:, n % NY, :], base[:, n, :]).then_inc(y_raw, 1)

            def y_aggregate(n):
                raw_waited(y_raw, n + 1)
                nc.vector.bn_aggr(mv_o[:, n % NY, :], raw_o[:, n % NY, :]).then_inc(y_stats, 1)

            def y_scale(n):
                s = n % NY
                dve.wait_ge(y_rstd, n + 1)
                nc.vector.scalar_tensor_tensor(out=y_nmr[:, s:s + 1], in0=mv_o[:, s, 0:1], scalar=-1.0, in1=rs_o[:, s:s + 1],
                                               op0=ALU.mult, op1=ALU.mult).then_inc(y_scaled, 1)

            def router_sum():
                dve.wait_ge(avg_step, 1)
                nc.vector.tensor_reduce(avg_ms[:, :], avg_m[:, :], op=ALU.add, axis=AX_X).then_inc(avg_step, 1)
                dve.wait_ge(avg_step, 2)
                dve.wait_ge(acc_done, NBLK + 1)
                nc.vector.tensor_scalar(acc[:, :], acc[:, :], avg_ms[:, 0:1], None, ALU.subtract).then_inc(avg_step, 1)

            def router_softmax():
                dve.wait_ge(logit_full, 1)
                nc.vector.tensor_tensor(logit[:, :], O_BANK[:, 0:NE], r_bias[:, :], ALU.add).then_inc(route_step, 1)
                dve.wait_ge(route_step, 1)
                nc.vector.tensor_reduce(nlmax[:, :], logit[:, :], op=ALU.max, axis=AX_X, negate=True).then_inc(route_step, 1)
                dve.wait_ge(lexp_ready, 1)
                nc.vector.reciprocal(lrec[:, :], lsum[:, :]).then_inc(route_step, 1)
                dve.wait_ge(expert_ready, 1)
                nc.vector.tensor_tensor(lpick[:, :], lexp[:, :], expert[:, :], ALU.mult).then_inc(route_step, 1)
                dve.wait_ge(route_step, 4)
                nc.vector.tensor_reduce(route[:, :], lpick[:, :], op=ALU.add, axis=AX_X).then_inc(route_step, 1)
                dve.wait_ge(route_step, 5)
                nc.vector.tensor_scalar(route2[:, :], route[:, :], lrec[:, 0:1], LORA_SCALING, ALU.mult, ALU.mult).then_inc(route_step, 1)
                dve.wait_ge(route_step, 6)
                dve.wait_ge(bT_ready, 1)
                nc.vector.tensor_scalar(bT[:, :], bT[:, :], route2[:, 0:1], None, ALU.mult).then_inc(bs_ready, 1)
                dve.wait_ge(bs_hi_done, 1)
                nc.vector.tensor_tensor(bS_lo, bT[:, :], bS_hi.bitcast(F32), ALU.subtract).then_inc(bs_split, 1)

            attn_statistics(NG)
            for j in range(NJ):
                if j < NJ - 1:
                    x2_lo(j + 1, 0)
                    x2_lo(j + 1, 1)
                if j < NJ - 2:
                    x2_norm(2 * j + 4)
                    x2_norm(2 * j + 5)
                if j == 0:
                    attn_norm(NG)
                if j == 1:
                    x1_statistics(NG, 4 * NG - 4)
                if j == 2:
                    x1_averaged(NG, 4 * NG - 4)
                    router_sum()
                if j == FREE:
                    router_softmax()
                for place in range(4):
                    if place in (1, 2):
                        base_out(2 * j + place - 1)
                    if place == 3:
                        tt_lo(j)
                    if j >= FREE:
                        for n in finish(j, place):
                            if n >= 2:
                                y_scale(n - 2)
                            y_sum(n)
                            if n >= 1:
                                y_aggregate(n - 1)
                            y_statistics(n)
            y_aggregate(NBLK - 1)
            for i, n in enumerate(range(ON_POOL, NBLK)):
                dve.wait_ge(y_rstd, n + 1)
                nc.vector.tensor_scalar(base[:, n, :], base[:, n, :], mv_o[:, n % NY, 0:1], rs_o[:, n % NY:n % NY + 1],
                                        ALU.subtract, ALU.mult).then_inc(last_yn, 1)
                dve.wait_ge(last_yn, i + 1)
                nc.vector.tensor_tensor(base[:, n, :], base[:, n, :], x1[:, n, :], ALU.add).then_inc(last_res, 1)

        @block.tensor
        def _(pe):
            def three(bank_ap, lhs_hi, lhs_lo, rhs_hi, rhs_lo, start, stop):
                nc.tensor.matmul(bank_ap, lhs_hi, rhs_hi, start=start, stop=False)
                nc.tensor.matmul(bank_ap, lhs_hi, rhs_lo, start=False, stop=False)
                return nc.tensor.matmul(bank_ap, lhs_lo, rhs_hi, start=False, stop=stop)

            def x_transposes(bk, b):
                for k in range(KT):
                    last = nc.tensor.transpose(bk[:, k * P:(k + 1) * P], xn[:, b % 2, k * P:(k + 1) * P], ident[:, :])
                last.then_inc(xt_full, 1)

            pe.wait_ge(pool_const, 4)
            for b in range(GB):
                pe.wait_ge(xn_ready, b + 1)
                if b >= 2:
                    pe.wait_ge(xt_split, b - 1)
                x_transposes(T_BANK[b % 2], b)
            pe.wait_ge(edge_step, 2)
            for k in range(KT):
                last = nc.tensor.transpose(V_BANK[:, k * 2 * NG:(k + 1) * 2 * NG], edge[:, k * P:(k + 1) * P],
                                           ident[0:2 * NG, 0:2 * NG])
            last.then_inc(edge_full, 1)
            pe.wait_ge(small_in, 16 * N_SMALL)
            nc.tensor.transpose(S_BANK[0][:, 0:NB], bias_rows[:, :], ident[0:NB, 0:NB]).then_inc(bias_full, 1)

            def convolve(m, gg, before, part=range(NK)):
                if m == 0 and part[0] == 0:
                    pe.wait_ge(xt_split, 4 * gg + GB)
                if before is not None and part[0] == 0:
                    pe.wait_ge((q_ready, k_ready, ctx_split)[m], 8 * before)
                for i in part:
                    k = CONV_ORDER[i]
                    if before is None and m == 0 and i % 2 == 0:
                        pe.wait_ge(w_split, i // 2 + 1)
                    if m == 0 and i == KT:
                        pe.wait_ge(halo_done, 2 * gg + 2)
                    c = slice(CH[m] * P, (CH[m] + 1) * P)
                    t = slice(k // KT, k // KT + GT)
                    done = three(CONV_BANK[m][:, :], cw_hi[:, k, c], cw_lo[:, k, c], xt_hi[:, k % KT, t],
                                 xt_lo[:, k % KT, t], i == 0, i == NK - 1)
                if part[-1] == NK - 1:
                    done.then_inc(conv_full, 1)

            def project_qk(g, p):
                if p == 0:
                    pe.wait_ge(qkv_split, 3 * g + 3)
                else:
                    pe.wait_ge(q_ready, 8 * g + p)
                    pe.wait_ge(k_ready, 8 * g + p)
                c = slice(p * P, (p + 1) * P)
                three(Q_BANK[:, :], wq_hi[:, c], wq_lo[:, c], qkv_hi[:, 1, :], qkv_lo[:, 1, :], True, True).then_inc(q_full, 1)
                three(K_BANK[:, :], wk_hi[:, c], wk_lo[:, c], qkv_hi[:, 2, :], qkv_lo[:, 2, :], True, True).then_inc(k_full, 1)

            def scores(g, p, first):
                pe.wait_ge(q_ready, 8 * g + (p + 1))
                pe.wait_ge(k_ready, 8 * g + (p + 1))
                if p > 0:
                    pe.wait_ge(exp_done, 16 * g + 2 * p)
                elif not first:
                    pe.wait_ge(pj_evac, 4 * g)
                for h in range(2):
                    nc.tensor.matmul(S_BANK[h][:, :], ident16[:, :], mask16[:, :], start=True, stop=False)
                for b in range(GB):
                    t = slice(b * P, (b + 1) * P)
                    for h in range(2):
                        r = slice(E * h, E * h + E)
                        done = nc.tensor.matmul(S_BANK[h][:, t], qT[r, p % 2, t], kT[r, p % 2, t],
                                                start=False, stop=b == GB - 1)
                        if b == GB - 1:
                            done.then_inc(s_full, 1)

            def transpose_probs(g, p):
                for h in range(2):
                    pe.wait_ge(pn_ready, 16 * g + (2 * p + h + 1))
                    if h == 0 and p > 0:
                        pe.wait_ge(ptA_ready, 8 * g + p)
                    if h == 1 and p > 0:
                        pe.wait_ge(ptB_ready, 8 * g + p)
                    for j in range(4):
                        last = nc.tensor.transpose(T_BANK[h][:, j * P:(j + 1) * P], probs[:, p % 2, 4 * h + j, :], ident[:, :])
                    last.then_inc(t_full, 1)

            def context(g, p):
                if p > 0:
                    pe.wait_ge(ctx_split, 8 * g + p)
                pe.wait_ge(ptA_ready, 8 * g + (p + 1))
                pe.wait_ge(ptB_ready, 8 * g + (p + 1))
                for b in range(GB):
                    for h in range(2):
                        last = nc.tensor.matmul(V_BANK[E * h:E * h + E, b * P:(b + 1) * P],
                                                vh[:, b, (2 * p + h) * E:(2 * p + h + 1) * E],
                                                pT[:, 4 * h + b, :], start=True, stop=True)
                last.then_inc(pv_full, 1)

            def project_out(g, p, first):
                pe.wait_ge(ctx_split, 8 * g + (p + 1))
                if p == 0 and not first:
                    pe.wait_ge(o_split, g)
                last = three(O_BANK[:, :], wo_hi[:, p, :], wo_lo[:, p, :], ctx_hi[:, p % 2, :], ctx_lo[:, p % 2, :],
                             p == 0, p == NP - 1)
                last.then_inc(o_used if p < NP - 1 else oacc_full, 1)

            def values(g, u, first):
                if u == 2:
                    pe.wait_ge(qkv_split, 3 * g + 3)
                if u == 0:
                    pe.wait_ge(qkv_split, 3 * g + 1)
                    if not first:
                        pe.wait_ge(ptA_ready, 8 * g)
                        pe.wait_ge(ptB_ready, 8 * g)
                if u >= 3:
                    pe.wait_ge(vh_dve if u % 2 == 0 else vh_act, 4 * g + ((u - 3) // 2 + 1))
                t = slice((u // 2) * P, (u // 2 + 1) * P)
                c = slice((u % 2) * 512, (u % 2) * 512 + 512)
                three(VH_BANK[u % 3][:, :], qkv_hi[:, 0, t], qkv_lo[:, 0, t], wv_hi[:, c], wv_lo[:, c],
                      True, True).then_inc(v_full, 1)

            def x_block_transposes(g, p):
                for b in range(GB):
                    if X_SLOTS[b] == p:
                        pe.wait_ge(xn_ready, 4 * g + (GB + b + 1))
                        if b >= 2:
                            pe.wait_ge((q_ready, k_ready)[b - 2], 8 * g + 8)
                        x_transposes(X_BANK[b], b)

            def w_transposes(k):
                if k >= 2:
                    pe.wait_ge(base_free, k - 1)
                else:
                    pe.wait_ge((q_ready, k_ready)[k], 8 * NG)
                for t in range(KT):
                    done = nc.tensor.transpose(BASE_BANK[k % 2][:, t * P:(t + 1) * P], w_raw[:, t, k * P:(k + 1) * P], ident[:, :])
                done.then_inc(wT_full, 1)

            def x2_transposes(j):
                for b in range(2):
                    pe.wait_ge(x2_ready, 2 * j + (b + 1))
                    for k in range(KT):
                        last = nc.tensor.transpose(X2_BANK[b][:, k * P:(k + 1) * P], x2n[:, b, k * P:(k + 1) * P], ident[:, :])
                    last.then_inc(x2_full, 1)

            def lora_b_and_router_transposes():
                for t in range(KT):
                    done = nc.tensor.transpose(T_BANK[0][:, t * P:(t + 1) * P], b_raw[:, t, :, :].rearrange("p e r -> p (e r)"), ident[:, :])
                done.then_inc(bT_full, 1)
                for k in range(KT):
                    done = nc.tensor.transpose(T_BANK[1][:, k * NE:(k + 1) * NE], r_raw[:, k * P:(k + 1) * P], ident[0:NE, 0:NE])
                done.then_inc(rT_full, 1)

            def group(g, first, last):
                for u in range(2 * GB):
                    values(g, u, first)
                    after = [1, 2] if first else QK_AFTER
                    if u in after:
                        project_qk(g, after.index(u))
                    if u == S_AFTER:
                        scores(g, 0, first)
                project_qk(g, 2)
                for p in range(1, NP):
                    scores(g, p, first)
                    if p == 1:
                        pe.wait_ge(vh_act, 4 * g + 4)
                        pe.wait_ge(vh_dve, 4 * g + 4)
                    for b in range(GB):
                        if not last and X_SLOTS[b] == p - 1 and X_BANK[b] is T_BANK[0]:
                            pe.wait_ge(xt_split, 4 * g + (GB + b + 1))
                    transpose_probs(g, p - 1)
                    if p >= 2:
                        project_out(g, p - 2, first)
                    if p + 2 < NP:
                        project_qk(g, p + 2)
                    if not last and p == NP - 2:
                        x_block_transposes(g, p)
                    if not last and p == NP - 1:
                        convolve(0, g + 1, g + 1, CONV_PARTS[0])
                    context(g, p - 1)
                    if not last and p < NP - 2:
                        x_block_transposes(g, p)
                if not last:
                    convolve(0, g + 1, g + 1, CONV_PARTS[1])
                else:
                    pe.wait_ge(ffn_in, 16 * N_FFN)
                    w_transposes(0)
                    w_transposes(1)
                transpose_probs(g, NP - 1)
                if not last:
                    convolve(0, g + 1, g + 1, CONV_PARTS[2])
                project_out(g, NP - 2, first)
                if last:
                    w_transposes(2)
                    w_transposes(3)
                context(g, NP - 1)
                if not last:
                    convolve(1, g + 1, g + 1)
                else:
                    lora_b_and_router_transposes()
                project_out(g, NP - 1, first)
                if not last:
                    convolve(2, g + 1, g + 1)
                else:
                    for k in range(KT):
                        done = nc.tensor.transpose(TT_BANK[:, k * P:(k + 1) * P], a_raw[:, k * P:(k + 1) * P], ident[:, :])
                    done.then_inc(aT_full, 1)
                    pe.wait_ge(bT_ready, 1)
                    pe.wait_ge(rT_ready, 1)
                    x2_transposes(0)
                pe.wait_ge(exp_done, 16 * g + 16)
                pe.wait_ge(o_split, g + 1)
                for b in range(GB):
                    if b >= 3:
                        pe.wait_ge(pj_evac, 4 * g + (b - 2))
                    t = slice(b * P, (b + 1) * P)
                    three(PJ_BANK[b % 3][:, :], o_hi[:, t], o_lo[:, t], pj_hi[:, :], pj_lo[:, :], True, True).then_inc(pj_full, 1)

            convolve(0, 0, None)
            convolve(1, 0, None)
            pe.wait_ge(edge_split, 1)
            convolve(2, 0, None)
            pe.wait_ge(bias_done, 2)
            pe.wait_ge(dve_const, 1)
            pe.wait_ge(pool_const, 10)
            pe.wait_ge(w_split, NW)
            group(0, True, False)
            with pe.Fori(1, NG - 1) as g:
                group(g, False, False)
            group(NG - 1, False, True)

            def base_product(j, s, b):
                pe.wait_ge(base_free, 2 * j + (b + 3))
                for k in range(KT):
                    t = slice(b * P, (b + 1) * P)
                    last = three(BASE_BANK[b][:, :], x2T_hi[:, s, k, t], x2T_lo[:, s, k, t], wT_hi[:, k, :], wT_lo[:, k, :],
                                 k == 0, k == KT - 1)
                last.then_inc(base_full, 1)

            def tt_product(j, s):
                pe.wait_ge(tt_split, 1 * j + 1)
                for k in range(KT):
                    last = three(TT_BANK[:, 0:2 * P], aT_hi[:, k, :], aT_lo[:, k, :], x2T_hi[:, s, k, :], x2T_lo[:, s, k, :],
                                 k == 0, k == KT - 1)
                last.then_inc(tt_full, 1)

            def lora_product(n):
                if n == 0:
                    pe.wait_ge(bs_split, 1)
                else:
                    pe.wait_ge(tt_split, n // 2 + 2)
                if n >= 2:
                    pe.wait_ge(y_ready, n - 1)
                t = slice(n * P, (n + 1) * P)
                three(Y_BANK[n % 2][:, :], tT_hi[:, t], tT_lo[:, t], bS_hi, bS_lo, True, True).then_inc(y_full, 1)

            pe.wait_ge(base_free, KT)
            with pe.Fori(0, FREE // 2) as i:
                for s in range(2):
                    j = 2 * i + s
                    pe.wait_ge(x2_split, 2 * j + 2)
                    x2_transposes(j + 1)
                    base_product(j, s, 0)
                    base_product(j, s, 1)
                    tt_product(j, s)
            pe.wait_ge(avg_step, 3)
            for k in range(KT):
                last = nc.tensor.matmul(O_BANK[:, k * P:(k + 1) * P], acc[:, k * P:(k + 1) * P], ones[:, :], start=True, stop=True)
            last.then_inc(sum_full, 1)
            pe.wait_ge(pj_evac, 4 * NG)
            for j in range(FREE, NJ):
                pe.wait_ge(x2_split, 2 * j + 2)
                if j < NJ - 1:
                    x2_transposes(j + 1)
                if j == FREE:
                    pe.wait_ge(mean_ready, 1)
                    for k in range(KT):
                        last = nc.tensor.matmul(O_BANK[:, 0:NE], colmean[:, k, :], rT[:, k, :], start=k == 0, stop=k == KT - 1)
                    last.then_inc(logit_full, 1)
                for place in range(4):
                    if place in (1, 2):
                        base_product(j, j % 2, place - 1)
                    if place == 3:
                        tt_product(j, j % 2)
                    for n in finish(j, place):
                        lora_product(n)


_INS = ['L0_attn_inputs', 'L0_attn_conv_w', 'L0_attn_conv_b', 'L0_attn_wq', 'L0_attn_bq', 'L0_attn_wk', 'L0_attn_bk',
        'L0_attn_wv', 'L0_attn_bv', 'L0_attn_wo', 'L0_attn_bo', 'L0_attn_proj_w', 'L0_attn_proj_b', 'L0_ffn_W',
        'L0_ffn_b', 'L0_ffn_A', 'L0_ffn_B', 'L0_ffn_router_W', 'L0_ffn_router_b']
_OUTS = [((1, 2048, 512), 'float32')]


def kernel(**inputs):
    import numpy as _np
    import concourse.bacc as _bacc
    from concourse import mybir as _mybir
    from concourse.bass_utils import run_bass_kernel_spmd as _run

    nc = _bacc.Bacc("TRN2", target_bir_lowering=False, num_devices=1)
    arrays, args = {}, []
    for name in _INS:
        a = _np.ascontiguousarray(inputs[name])
        arrays[f"in_{name}_dram"] = a
        args.append(nc.dram_tensor(f"in_{name}_dram", a.shape, _mybir.dt.from_np(a.dtype), kind="ExternalInput").ap())
    for i, (shape, dtype) in enumerate(_OUTS):
        dt = _mybir.dt.from_np(_np.dtype(dtype))
        args.append(nc.dram_tensor(f"out_{i}_dram", shape, dt, kind="ExternalOutput").ap())
    attention_ffn_sandwich(nc, *args)
    r = _run(nc, [arrays], core_ids=[0])
    return r.results[0]["out_0_dram"]
```

```python
from contextlib import ExitStack

import concourse.bass as bass
from concourse import mybir

F32 = mybir.dt.float32
F32R = mybir.dt.float32r
BF16 = mybir.dt.bfloat16
ALU = mybir.AluOpType
ACT = mybir.ActivationFunctionType
AX_X = mybir.AxisListType.X

P = 128
EPS = 1e-5
MASKED = -1e9
LORA_SCALING = 2.0
Q_START, Q_END = 107, -1


def attention_ffn_sandwich(
    nc: bass.Bass, x: bass.AP, conv_w: bass.AP, conv_b: bass.AP,
    wq: bass.AP, bq: bass.AP, wk: bass.AP, bk: bass.AP, wv: bass.AP, bv: bass.AP,
    wo: bass.AP, bo: bass.AP, proj_w: bass.AP, proj_b: bass.AP,
    ffn_w: bass.AP, ffn_b: bass.AP, lora_a: bass.AP, lora_b: bass.AP,
    router_w: bass.AP, router_b: bass.AP, out: bass.AP,
):
    _, L, D = x.shape
    C, H, E = wq.shape
    TAPS = conv_w.shape[0]
    NE, R = lora_a.shape[:2]
    KT = D // P
    NBLK = L // P
    GB = 4
    GT = GB * P
    NG = NBLK // GB
    NP = H // 2
    NK = TAPS * KT
    NH = NK // 2
    SCALE = float(E) ** -0.5
    assert D == 512 and C == P and 2 * E == P and TAPS == 3 and NE * R == P and GT == 512

    xd = x.rearrange("a (g b p) d -> g p (a b) d", p=P, b=GB)
    xrow = x.rearrange("a l d -> (a l) d")
    outd = out.rearrange("a (n p) d -> n p (a d)", p=P)
    convd = conv_w.rearrange("j c n -> (j c) n").rearrange("(i t p) n -> i p t n", p=P, t=2)

    with ExitStack() as ctx:
        def sb(name, shape, dt=F32, scope=ctx):
            return scope.enter_context(nc.sbuf_tensor(name, shape, dt))

        def bank(name):
            return ctx.enter_context(nc.psum_tensor(name, [P, 512], F32))

        def sem(name):
            return ctx.enter_context(nc.semaphore(name))

        x1 = sb("x1", [P, NBLK, D])
        rows = sb("rows", [P, GB, D])
        ident = sb("ident", [P, P])
        stats2 = sb("stats2", [P, NBLK, 2])
        def norm_set(name, n=GB):
            return (sb(f"{name}_raw_sb", [P, n, 6]), sb(f"{name}_mv", [P, n, 2]), sb(f"{name}_ve", [P, n]),
                    sb(f"{name}_rs", [P, n]))

        raw_1, mv_1, ve_1, rs_1 = norm_set("in", NBLK)
        raw_o, mv_o, ve_o, rs_o = norm_set("attn")
        raw_2, mv_2, ve_2, rs_2 = norm_set("mid")
        neg_half, eps_sb = sb("neg_half", [P, NBLK]), sb("eps_sb", [P, NBLK])
        rowmask = sb("rowmask", [P, NBLK])
        avg_w = sb("avg_w", [P, NBLK])
        avg_m = sb("avg_m", [P, NBLK])
        avg_ms = sb("avg_ms", [P, 1])
        acc = sb("acc", [P, D])
        ones = sb("ones", [P, P])

        ph1 = ExitStack()
        cw_hi = sb("cw_hi", [P, NK, 3 * C], F32R, ph1)
        cw_lo = sb("cw_lo", [P, NK, 3 * C], F32R, ph1)
        ph1.close()
        ph2 = ExitStack()
        w_raw = sb("w_raw", [P, KT, D], F32, ph2)
        a_raw = sb("a_raw", [P, D], F32, ph2)
        b_raw = sb("b_raw", [P, KT, NE, R], F32, ph2)
        r_raw = sb("r_raw", [NE, D], F32, ph2)
        y_bias = sb("y_bias", [P, D], F32, ph2)
        wT_hi, wT_lo = sb("wT_hi", [P, KT, D], F32R, ph2), sb("wT_lo", [P, KT, D], F32R, ph2)
        bT = sb("bT", [P, D], F32, ph2)
        ph2.close()
        hold = sb("hold", [P, 2 * NK * 3 * C])

        r_bias = sb("r_bias", [P, NE])
        rT = sb("rT", [P, KT, NE])
        expert = sb("expert", [P, NE])
        logit, lexp, lpick = sb("logit", [P, NE]), sb("lexp", [P, NE]), sb("lpick", [P, NE])
        nlmax, lsum, lrec = sb("nlmax", [P, 1]), sb("lsum", [P, 1]), sb("lrec", [P, 1])
        route, route2 = sb("route", [P, 1]), sb("route2", [P, 1])
        y_nmr = sb("y_nmr", [P, GB])

        wqk = sb("wqk", [P, 4, H * E], F32R)
        wq_hi, wq_lo, wk_hi, wk_lo = wqk[:, 0, :], wqk[:, 1, :], wqk[:, 2, :], wqk[:, 3, :]
        wv_hi, wv_lo = sb("wv_hi", [P, H * E], F32R), sb("wv_lo", [P, H * E], F32R)
        wo_hi, wo_lo = sb("wo_hi", [P, NP, C], F32R), sb("wo_lo", [P, NP, C], F32R)
        pj_hi, pj_lo = sb("pj_hi", [P, D], F32R), sb("pj_lo", [P, D], F32R)
        NB = 3 * NP + 3 + 1
        bias_rows, biases, bq_sc = sb("bias_rows", [NB, P]), sb("biases", [P, NB]), sb("bq_sc", [P, NP])
        bk_sb, bv_sb = biases[:, NP:2 * NP], biases[:, 2 * NP:3 * NP]
        conv_bias, bo_sb = biases[:, 3 * NP:3 * NP + 3], biases[:, 3 * NP + 3:NB]
        pb_sb = sb("pb_sb", [P, D])
        ident16 = sb("ident16", [P, P], BF16)
        mask16 = sb("mask16", [P, 4 * P], BF16)
        NR = 2 * NG + 2
        edge = sb("edge", [NR, D])
        edge_bn, edge_mv = sb("edge_bn", [NR, 6]), sb("edge_mv", [NR, 2])
        edge_hi, edge_lo = sb("edge_hi", [P, KT, NR], F32R), sb("edge_lo", [P, KT, NR], F32R)
        xn = sb("xn", [P, 2, D])
        xt_hi, xt_lo = sb("xt_hi", [P, KT, GT + 2], F32R), sb("xt_lo", [P, KT, GT + 2], F32R)
        qkv_hi, qkv_lo = sb("qkv_hi", [P, 3, GT], F32R), sb("qkv_lo", [P, 3, GT], F32R)
        work = sb("work", [P, NBLK, D])
        vh = work[:, 0:8, :].rearrange("p (b u) n -> p b (u n)", u=2)
        probs = work[:, 8:12, :].rearrange("p a n -> p (a n)").rearrange("p (s c k) -> p s c k", s=2, k=P)
        qT, kT = work[:, 12:14, :], work[:, 14:16, :]
        nmax = sb("nmax", [P, 2, 8])
        rsum = sb("rsum", [P, 2, 8])
        rinv = sb("rinv", [P, 2, 8])
        pT = sb("pT", [P, 8, P])
        ctx_hi, ctx_lo = sb("ctx_hi", [P, 2, GT], F32R), sb("ctx_lo", [P, 2, GT], F32R)
        o_hi, o_lo = sb("o_hi", [P, GT], F32R), sb("o_lo", [P, GT], F32R)

        S_BANK = [bank("scores0"), bank("scores1")]
        Q_BANK, K_BANK = bank("proj_q"), bank("proj_k")
        T_BANK = [bank("trans0"), bank("trans1")]
        V_BANK = bank("context")
        O_BANK = bank("attn_out")
        CONV_BANK = [Q_BANK, K_BANK, V_BANK]
        VH_BANK = [T_BANK[0], T_BANK[1], V_BANK]
        PJ_BANK = [S_BANK[0], S_BANK[1], O_BANK]

        x_first = [sem(f"x_first{b}") for b in range(GB)]
        x_rest, edge_in, small_in, pb_in = [sem(f"x_rest{g}") for g in range(1, NG)], sem("edge_in"), sem("small_in"), sem("pb_in")
        w_in = [sem(f"w_in{i}") for i in range(NK // 2 + 5)]
        ffn_in = sem("ffn_in")
        out_done = sem("out_done")
        pool_const, dve_const, bias_done = sem("pool_const"), sem("dve_const"), sem("bias_done")
        bias_full = sem("bias_full")
        w_hi_done, w_split = sem("w_hi_done"), sem("w_split")
        edge_zero, edge_step, edge_n, edge_full = sem("edge_zero"), sem("edge_step"), sem("edge_n"), sem("edge_full")
        edge_hi_done, edge_split = sem("edge_hi_done"), sem("edge_split")
        edge_var, edge_rstd = sem("edge_var"), sem("edge_rstd")
        ln1_raw, ln1_stats, ln1_var, ln1_rstd = sem("ln1_raw"), sem("ln1_stats"), sem("ln1_var"), sem("ln1_rstd")
        xn_ready, xt_full, xt_hi_done, xt_split = sem("xn_ready"), sem("xt_full"), sem("xt_hi_done"), sem("xt_split")
        halo_done, conv_full, qkv_hi_done, qkv_split = sem("halo_done"), sem("conv_full"), sem("qkv_hi_done"), sem("qkv_split")
        v_full, vh_act, vh_dve = sem("v_full"), sem("vh_act"), sem("vh_dve")
        q_full, k_full, q_ready, k_ready = sem("q_full"), sem("k_full"), sem("q_ready"), sem("k_ready")
        s_full, nmax_ready, exp_done, rinv_ready = sem("s_full"), sem("nmax_ready"), sem("exp_done"), sem("rinv_ready")
        pn_ready, t_full = sem("pn_ready"), sem("t_full")
        ptA_ready, ptB_ready = sem("ptA_ready"), sem("ptB_ready")
        pv_full, ctx_hi_done, ctx_split, o_used = sem("pv_full"), sem("ctx_hi_done"), sem("ctx_split"), sem("o_used")
        oacc_full, o_hi_done, o_split, pj_full, pj_evac = sem("oacc_full"), sem("o_hi_done"), sem("o_split"), sem("pj_full"), sem("pj_evac")
        lno_raw, lno_stats, lno_var, lno_rstd = sem("lno_raw"), sem("lno_stats"), sem("lno_var"), sem("lno_rstd")
        on_ready, x1_ready = sem("on_ready"), sem("x1_ready")
        ln2_raw, ln2_stats, ln2_var, ln2_rstd, ln2_kept = sem("ln2_raw"), sem("ln2_stats"), sem("ln2_var"), sem("ln2_rstd"), sem("ln2_kept")
        acc_done = sem("acc_done")
        exp_mark, expert_ready = sem("exp_mark"), sem("expert_ready")
        wT_full, wT_hi_done = sem("wT_full"), sem("wT_hi_done")
        aT_full, aT_hi_done = sem("aT_full"), sem("aT_hi_done")
        bT_full, bT_ready, rT_full, rT_ready = sem("bT_full"), sem("bT_ready"), sem("rT_full"), sem("rT_ready")
        avg_step = sem("avg_step")
        sum_full, mean_ready, logit_full, route_step, lexp_ready = sem("sum_full"), sem("mean_ready"), sem("logit_full"), sem("route_step"), sem("lexp_ready")
        bs_ready, bs_hi_done, bs_split = sem("bs_ready"), sem("bs_hi_done"), sem("bs_split")
        x2_ready, x2_full, x2_hi_done, x2_split = sem("x2_ready"), sem("x2_full"), sem("x2_hi_done"), sem("x2_split")
        base_full, tt_full, tt_hi_done = sem("base_full"), sem("tt_full"), sem("tt_hi_done")
        base_free = sem("base_free")
        tt_split = sem("tt_split")
        y_scaled = sem("y_scaled")
        y_full, y_ready, y_raw, y_stats, y_var, y_rstd = sem("y_full"), sem("y_ready"), sem("y_raw"), sem("y_stats"), sem("y_var"), sem("y_rstd")
        last_yn, last_res = sem("last_yn"), sem("last_res")
        yn_ready, res_ready = sem("yn_ready"), sem("res_ready")

        x2T_hi = xt_hi[:, :, 0:GT].rearrange("p k (s t) -> p s k t", s=2)
        x2T_lo = xt_lo[:, :, 0:GT].rearrange("p k (s t) -> p s k t", s=2)
        x2n = xn
        base = work
        tT_hi = wqk[:, 0:2, :].rearrange("p a n -> p (a n)")
        tT_lo = wqk[:, 2:4, :].rearrange("p a n -> p (a n)")
        aT_hi = ctx_hi[:, 0, :].rearrange("p (k c) -> p k c", k=KT)
        aT_lo = ctx_lo[:, 0, :].rearrange("p (k c) -> p k c", k=KT)
        bS_hi, bS_lo = ctx_hi[:, 1, :], ctx_lo[:, 1, :]
        colmean = pT[:, 0:KT, :]
        AT_BANK, BT_BANK, RT_BANK = Q_BANK, K_BANK, S_BANK[0]
        X2_BANK, BASE_BANK, TT_BANK, Y_BANK = T_BANK, [Q_BANK, K_BANK], V_BANK, S_BANK
        NJ = NBLK // 2
        FREE = NJ // 2
        LATE = FREE + 1
        STEPS = {4: [("base", 0), ("base", 1), ("t", 0), ("finish", 0), ("finish", 1)],
                 5: [("finish", 2), ("t", 0), ("finish", 3), ("base", 0), ("finish", 4), ("base", 1)],
                 6: [("finish", 5), ("t", 0), ("finish", 6), ("base", 0), ("finish", 7), ("base", 1)],
                 7: [("finish", 8), ("t", 0), ("finish", 9), ("base", 0), ("base", 1)]}
        ORDER = [2 * j + i if what == "base" else i for j in range(FREE, NJ) for what, i in STEPS[j]
                 if what == "finish" or (what == "base" and j >= LATE)]
        NY = GB
        ON_POOL = NBLK - 2

        CHUNKS = [2, 3, 0, 1, 4, 5]
        CONV_ORDER = [k for i in CHUNKS for k in (2 * i, 2 * i + 1)]
        def flat(t):
            return t[:, :, :].rearrange("p a n -> p (a n)")

        splits = [(flat(cw_hi)[:, i * 768:(i + 1) * 768], flat(cw_lo)[:, i * 768:(i + 1) * 768], 768, 1.0)
                  for i in CHUNKS]
        splits += [(wq_hi[:, :], wq_lo[:, :], H * E, SCALE), (wk_hi[:, :], wk_lo[:, :], H * E, 1.0),
                   (wv_hi[:, :], wv_lo[:, :], H * E, 1.0), (flat(wo_hi), flat(wo_lo), NP * C, 1.0),
                   (pj_hi[:, :], pj_lo[:, :], D, 1.0)]
        sources = [(convd[i], "p t n") for i in CHUNKS]
        sources += [(wq.rearrange("c h e -> c (h e)"), ""), (wk.rearrange("c h e -> c (h e)"), ""),
                    (wv.rearrange("c h e -> c (h e)"), ""),
                    (wo.rearrange("(p two) e w -> (two e) p w", two=2), "p t n"), (proj_w, "")]
        NW = len(splits)
        LANDINGS = 8

        def landing(i):
            s = i % LANDINGS
            return work[:, 2 * s:2 * s + 2, :].rearrange("p a n -> p (a n)")[:, 0:splits[i][2]]

        CH = [2, 0, 1]
        X_SLOTS = [3, 4, 6, 6]
        X_BANK = [T_BANK[0], T_BANK[0], Q_BANK, K_BANK]
        QK_AFTER = [0, 2]
        VH_ACT, VH_DVE = [0, 2, 6], [1, 3, 4, 5, 7]
        S_AFTER = 3
        CONV_PARTS = [range(0, 4), range(4, 8), range(8, 12)]
        N_SMALL = 5
        N_FFN = KT + 5
        block = ctx.enter_context(nc.Block())

        @block.sync
        def _(sp):
            for b in range(GB):
                sp.dma_start(x1[:, b, :], xd[0, :, b, :]).then_inc(x_first[b], 16)
            for i in range(NW):
                if i == 2:
                    sp.wait_ge(edge_zero, 1)
                    beside = xrow[GT - 1:GT - 1 + (NG - 1) * GT, :].rearrange("(g t) d -> g t d", t=GT)[:, 0:2, :]
                    sp.dma_start(edge[2:2 * NG, :], beside).then_inc(edge_in, 16)
                if i >= LANDINGS:
                    sp.wait_ge(w_split, i - LANDINGS + 1)
                src, kind = sources[i]
                dst = landing(i)
                if kind:
                    dst = dst.rearrange("p (t n) -> p t n", n=src.shape[2])
                sp.dma_start(dst, src).then_inc(w_in[i], 16)
            sp.dma_start(pb_sb[:, :], proj_b.rearrange("(a e) -> a e", a=1).broadcast_to([P, D])).then_inc(pb_in, 16)
            for g in range(1, NG):
                sp.dma_start(x1[:, g * GB:(g + 1) * GB, :], xd[g]).then_inc(x_rest[g - 1], 16)
            sp.wait_ge(conv_full, 3 * NG)
            sp.dma_start(w_raw[:, :, :], ffn_w.rearrange("(t p) d -> p t d", p=P)).then_inc(ffn_in, 16)
            for t in range(KT):
                sp.dma_start(b_raw[:, t, :, :], lora_b[:, t * P:(t + 1) * P, :].rearrange("e p r -> p e r")).then_inc(ffn_in, 16)
            sp.dma_start(a_raw[:, :], lora_a.rearrange("e r d -> (e r) d")).then_inc(ffn_in, 16)
            sp.dma_start(r_raw[:, :], router_w).then_inc(ffn_in, 16)
            sp.dma_start(r_bias[:, :], router_b.rearrange("(a e) -> a e", a=1).broadcast_to([P, NE])).then_inc(ffn_in, 16)
            sp.dma_start(y_bias[:, :], ffn_b.rearrange("(a e) -> a e", a=1).broadcast_to([P, D])).then_inc(ffn_in, 16)

            def store(n):
                sp.dma_start(outd[ORDER[n]], base[:, ORDER[n], :]).then_inc(out_done, 16)

            for n in range(ON_POOL):
                sp.wait_ge(res_ready, n + 1)
                store(n)
            for n in range(ON_POOL, NBLK):
                sp.wait_ge(last_res, n - ON_POOL + 1)
                store(n)
            sp.wait_ge(out_done, 16 * NBLK)

        def rsqrt_chain(pool, n, stats_sem, var_sem, done_sem, count, mv, ve, rs, half):
            pool.wait_ge(stats_sem, count)
            nc.gpsimd.tensor_tensor(ve, mv, eps_sb[0:ve.shape[0], 0:n], ALU.add).then_inc(var_sem, 1)
            pool.wait_ge(var_sem, count)
            nc.gpsimd.tensor_tensor(rs, ve, half, ALU.pow).then_inc(done_sem, 1)

        @block.gpsimd
        def _(pool):
            nc.gpsimd.memset(edge[:, :], 0.0).then_inc(edge_zero, 1)
            nc.gpsimd.memset(ident[:, :], 0.0).then_inc(pool_const, 1)
            nc.gpsimd.memset(neg_half[:, :], -0.5).then_inc(pool_const, 1)
            nc.gpsimd.memset(eps_sb[:, :], EPS).then_inc(pool_const, 1)
            pool.wait_ge(pool_const, 3)
            nc.gpsimd.affine_select(out=ident[:, :], in_=ident[:, :], compare_op=ALU.not_equal, fill=1.0,
                                    base=0, pattern=[[-1, P]], channel_multiplier=1).then_inc(pool_const, 1)
            def x_scales(b0, b1, n):
                rsqrt_chain(pool, b1 - b0, ln1_stats, ln1_var, ln1_rstd, n, mv_1[:, b0:b1, 1], ve_1[:, b0:b1],
                            rs_1[:, b0:b1], neg_half[:, b0:b1])

            for b in range(GB):
                x_scales(b, b + 1, b + 1)
            rsqrt_chain(pool, 1, edge_n, edge_var, edge_rstd, 1, edge_mv[:, 1:2], edge_bn[:, 0:1], edge_bn[:, 1:2],
                        neg_half[0:NR, 0:1])
            pool.wait_ge(pool_const, 4)
            nc.gpsimd.tensor_copy(ident16[:, :], ident[:, :]).then_inc(pool_const, 1)
            nc.gpsimd.memset(mask16[:, :], 0.0).then_inc(pool_const, 1)
            nc.gpsimd.memset(rowmask[:, :], 1.0).then_inc(pool_const, 1)
            pool.wait_ge(pool_const, 7)
            nc.gpsimd.affine_select(out=mask16[:, :].rearrange("p (a k) -> p a k", k=P),
                                    in_=mask16[:, :].rearrange("p (a k) -> p a k", k=P),
                                    compare_op=ALU.is_ge, fill=MASKED, base=0,
                                    pattern=[[0, 4], [-1, P]], channel_multiplier=1).then_inc(pool_const, 1)
            nc.gpsimd.affine_select(out=rowmask[:, 0:1], in_=rowmask[:, 0:1], compare_op=ALU.is_ge, fill=0.0,
                                    base=-Q_START, pattern=[[0, 1]], channel_multiplier=1).then_inc(pool_const, 1)
            nc.gpsimd.affine_select(out=rowmask[:, NBLK - 1:NBLK], in_=rowmask[:, NBLK - 1:NBLK],
                                    compare_op=ALU.is_ge, fill=0.0, base=P - 1 + Q_END, pattern=[[0, 1]],
                                    channel_multiplier=-1).then_inc(pool_const, 1)

            def halo(g):
                pool.wait_ge(edge_split, 1)
                for dst, src in ((xt_hi, edge_hi), (xt_lo, edge_lo)):
                    nc.gpsimd.tensor_copy(dst[:, :, 0:GT + 2:GT + 1], src[:, :, bass.ds(2 * g, 2, step=3)]).then_inc(halo_done, 1)

            halo(0)

            x_scales(GB, NBLK, GB + 1)

            def x1_sums(g1, before, blocks=range(GB)):
                for b in blocks:
                    pool.wait_ge(on_ready, before + (b + 1))
                    xb = x1[:, bass.ds(4 * g1 + b, 1), :].rearrange("p a d -> p (a d)")
                    nc.gpsimd.tensor_tensor(xb, xb, rows[:, b, :], ALU.add).then_inc(x1_ready, 1)

            def x1_scales(g1, n):
                rsqrt_chain(pool, GB, ln2_stats, ln2_var, ln2_rstd, n, mv_2[:, :, 1], ve_2[:, :],
                            rs_2[:, :], neg_half[:, 0:GB])
                pool.wait_ge(ln2_rstd, n)
                nc.gpsimd.tensor_tensor(avg_w[:, bass.ds(4 * g1, 4)], rs_2[:, :], rowmask[:, bass.ds(4 * g1, 4)],
                                        ALU.mult).then_inc(ln2_kept, 1)
                nc.gpsimd.tensor_copy(stats2[:, bass.ds(4 * g1, 4), 0], mv_2[:, :, 0]).then_inc(ln2_kept, 1)
                nc.gpsimd.tensor_copy(stats2[:, bass.ds(4 * g1, 4), 1], rs_2[:, :]).then_inc(ln2_kept, 1)

            def attn_scales(n):
                rsqrt_chain(pool, GB, lno_stats, lno_var, lno_rstd, n, mv_o[:, :, 1], ve_o[:, :],
                            rs_o[:, :], neg_half[:, 0:GB])

            def group(g, first, last):
                if not last:
                    pool.wait_ge(conv_full, 3 * g + 3)
                    halo(g + 1)
                if not first:
                    attn_scales(g)
                for p in range(NP):
                    for h in range(2):
                        pool.wait_ge(rinv_ready, 16 * g + (2 * p + h + 1))
                        part = probs[:, p % 2, 4 * h:4 * h + 4, :]
                        nc.gpsimd.tensor_tensor(
                            part, part, rinv[:, p % 2, 4 * h:4 * h + 4].unsqueeze(2).broadcast_to([P, 4, P]),
                            ALU.mult).then_inc(pn_ready, 1)
                    if p == 0 and not first:
                        x1_sums(g - 1, 4 * g - 4, range(0, 2))
                    if p == 1 and not first:
                        x1_sums(g - 1, 4 * g - 4, range(2, 4))
                    if p == (3 if last else 4) and not first:
                        x1_scales(g - 1, g)

            group(0, True, False)
            with pool.Fori(1, NG - 1) as g:
                group(g, False, False)
            group(NG - 1, False, True)
            attn_scales(NG)
            x1_sums(NG - 1, 4 * NG - 4)
            x1_scales(NG - 1, NG)
            pool.wait_ge(ln2_kept, 3 * NG)
            nc.gpsimd.tensor_tensor(avg_m[:, :], avg_w[:, :], stats2[:, :, 0], ALU.mult).then_inc(avg_step, 1)

            nc.gpsimd.memset(expert[:, :], 1.0).then_inc(exp_mark, 1)
            pool.wait_ge(exp_mark, 1)
            nc.gpsimd.affine_select(out=expert[:, :], in_=expert[:, :], compare_op=ALU.is_ge, fill=0.0, base=0,
                                    pattern=[[-R, NE]], channel_multiplier=1).then_inc(exp_mark, 1)
            pool.wait_ge(exp_mark, 2)
            nc.gpsimd.affine_select(out=expert[:, :], in_=expert[:, :], compare_op=ALU.is_ge, fill=0.0, base=R - 1,
                                    pattern=[[R, NE]], channel_multiplier=-1).then_inc(expert_ready, 1)

            def residual(n):
                pool.wait_ge(yn_ready, n + 1)
                row = base[:, ORDER[n], :]
                nc.gpsimd.tensor_tensor(row, row, x1[:, ORDER[n], :], ALU.add).then_inc(res_ready, 1)

            for n in range(NBLK):
                s = n % NY
                pool.wait_ge(y_stats, n + 1)
                nc.gpsimd.tensor_tensor(ve_o[:, s:s + 1], mv_o[:, s, 1:2], eps_sb[:, 0:1], ALU.add).then_inc(y_var, 1)
                pool.wait_ge(y_var, n + 1)
                nc.gpsimd.tensor_tensor(rs_o[:, s:s + 1], ve_o[:, s:s + 1], neg_half[:, s:s + 1], ALU.pow).then_inc(y_rstd, 1)
                if 2 <= n < ON_POOL:
                    residual(n - 2)
            residual(ON_POOL - 2)
            residual(ON_POOL - 1)

        @block.scalar
        def _(act):
            for n, src in enumerate((bq, bk, bv)):
                act.dma_start(bias_rows[n * NP:(n + 1) * NP, :], src.rearrange("(p two) e -> p (two e)", two=2)).then_inc(small_in, 16)
            act.dma_start(bias_rows[3 * NP:3 * NP + 3, :], conv_b.rearrange("(m p) -> m p", p=P)).then_inc(small_in, 16)
            act.dma_start(bias_rows[3 * NP + 3:NB, :], bo.rearrange("(a p) -> a p", a=1)).then_inc(small_in, 16)

            def split_hi(i):
                act.wait_ge(w_in[i], 16)
                nc.scalar.activation(splits[i][0], landing(i), ACT.Copy, scale=splits[i][3]).then_inc(w_hi_done, 1)

            def xt_hi_part(n, b, bk):
                act.wait_ge(xt_full, n)
                nc.scalar.activation(xt_hi[:, :, 1 + b * P:1 + (b + 1) * P],
                                     bk[:, :].rearrange("p (k t) -> p k t", k=KT), ACT.Copy).then_inc(xt_hi_done, 1)

            for b in range(GB):
                xt_hi_part(b + 1, b, T_BANK[b % 2])
                if b == 1:
                    split_hi(0)
            split_hi(1)
            split_hi(2)
            act.wait_ge(edge_full, 1)
            nc.scalar.activation(edge_hi[:, :, :], V_BANK[:, 0:KT * NR].rearrange("p (k t) -> p k t", k=KT),
                                 ACT.Copy).then_inc(edge_hi_done, 1)
            split_hi(3)
            act.wait_ge(bias_full, 1)
            nc.scalar.activation(biases[:, :], S_BANK[0][:, 0:NB], ACT.Copy).then_inc(bias_done, 1)
            nc.scalar.activation(bq_sc[:, :], S_BANK[0][:, 0:NP], ACT.Copy, scale=SCALE).then_inc(bias_done, 1)
            for i in range(GB, NW):
                split_hi(i)
            act.wait_ge(bias_done, 2)

            def evac_qk(g, p):
                act.wait_ge(q_full, 8 * g + (p + 1))
                nc.scalar.activation(qT[:, p % 2, :], Q_BANK[:, :], ACT.Identity, bias=bq_sc[:, p:p + 1]).then_inc(q_ready, 1)
                act.wait_ge(k_full, 8 * g + (p + 1))
                nc.scalar.activation(kT[:, p % 2, :], K_BANK[:, :], ACT.Identity, bias=bk_sb[:, p:p + 1]).then_inc(k_ready, 1)

            def exps(g, p, h):
                act.wait_ge(nmax_ready, 16 * g + (2 * p + h + 1))
                if p >= 2:
                    act.wait_ge(t_full, 16 * g + (2 * (p - 2) + h + 1))
                for b in range(GB):
                    c = 4 * h + b
                    last = nc.scalar.activation(probs[:, p % 2, c, :], S_BANK[h][:, b * P:(b + 1) * P], ACT.Exp,
                                                bias=nmax[:, p % 2, c:c + 1], accum_out=rsum[:, p % 2, c:c + 1])
                last.then_inc(exp_done, 1)

            def conv_hi(m, n):
                act.wait_ge(conv_full, n)
                nc.scalar.activation(qkv_hi[:, m, :], CONV_BANK[m][:, :], ACT.Identity,
                                     bias=conv_bias[:, CH[m]:CH[m] + 1]).then_inc(qkv_hi_done, 1)

            def context_hi(g, p):
                act.wait_ge(pv_full, 8 * g + (p + 1))
                if p >= 2:
                    act.wait_ge(o_used, (NP - 1) * g + (p - 1))
                nc.scalar.activation(ctx_hi[:, p % 2, :], V_BANK[:, :], ACT.Identity,
                                     bias=bv_sb[:, p:p + 1]).then_inc(ctx_hi_done, 1)

            def x2_hi(j, b):
                act.wait_ge(x2_full, 2 * j + b + 1)
                nc.scalar.activation(x2T_hi[:, j % 2, :, b * P:(b + 1) * P],
                                     X2_BANK[b][:, :].rearrange("p (k t) -> p k t", k=KT), ACT.Copy).then_inc(x2_hi_done, 1)

            def x2_hi_pair(j):
                if j >= 2:
                    act.wait_ge(tt_full, j - 1)
                x2_hi(j, 0)
                x2_hi(j, 1)

            def wT_hi_part(k):
                act.wait_ge(wT_full, k + 1)
                nc.scalar.activation(wT_hi[:, k, :], BASE_BANK[k % 2][:, :], ACT.Copy).then_inc(wT_hi_done, 1)

            def group(g, last):
                for u in range(2 * GB):
                    if u == S_AFTER + 1:
                        exps(g, 0, 0)
                        exps(g, 0, 1)
                    if u in VH_ACT:
                        act.wait_ge(v_full, 8 * g + (u + 1))
                        nc.scalar.activation(vh[:, u // 2, (u % 2) * 512:(u % 2) * 512 + 512], VH_BANK[u % 3][:, :],
                                             ACT.Copy).then_inc(vh_act, 1)
                    if u in QK_AFTER:
                        evac_qk(g, QK_AFTER.index(u))
                for p in range(NP):
                    if p > 0:
                        exps(g, p, 0)
                        exps(g, p, 1)
                    if p + 2 < NP:
                        evac_qk(g, p + 2)
                    for b in range(0, 2):
                        if not last and X_SLOTS[b] == p:
                            xt_hi_part(4 * g + (GB + b + 1), b, X_BANK[b])
                    if p >= 1:
                        context_hi(g, p - 1)
                    for b in range(2, GB):
                        if not last and X_SLOTS[b] == p:
                            xt_hi_part(4 * g + (GB + b + 1), b, X_BANK[b])
                    if last and p >= NP - 2:
                        wT_hi_part(2 * (p - NP + 2))
                        wT_hi_part(2 * (p - NP + 2) + 1)
                if not last:
                    conv_hi(0, 3 * g + 4)
                else:
                    act.wait_ge(aT_full, 1)
                    nc.scalar.activation(aT_hi[:, :, :], AT_BANK[:, :].rearrange("p (k c) -> p k c", k=KT),
                                         ACT.Copy).then_inc(aT_hi_done, 1)
                context_hi(g, NP - 1)
                if not last:
                    conv_hi(1, 3 * g + 5)
                else:
                    act.wait_ge(rT_full, 1)
                    nc.scalar.activation(rT[:, :, :], RT_BANK[:, 0:KT * NE].rearrange("p (k e) -> p k e", k=KT),
                                         ACT.Copy).then_inc(rT_ready, 1)
                    act.wait_ge(bT_full, 1)
                    nc.scalar.activation(bT[:, :], BT_BANK[:, :], ACT.Copy).then_inc(bT_ready, 1)
                    x2_hi_pair(0)
                act.wait_ge(oacc_full, g + 1)
                nc.scalar.activation(o_hi[:, :], O_BANK[:, :], ACT.Identity, bias=bo_sb[:, 0:1]).then_inc(o_hi_done, 1)
                if not last:
                    conv_hi(2, 3 * g + 6)

            for m in range(3):
                conv_hi(m, m + 1)
            with act.Fori(0, NG - 1) as g:
                group(g, False)
            group(NG - 1, True)

            def tt_hi(j):
                act.wait_ge(tt_full, j + 1)
                nc.scalar.activation(tT_hi[:, 2 * j * P:2 * (j + 1) * P], TT_BANK[:, 0:2 * P], ACT.Copy).then_inc(tt_hi_done, 1)

            def y_norm(n):
                act.wait_ge(y_scaled, n + 1)
                nc.scalar.activation(base[:, ORDER[n], :], base[:, ORDER[n], :], ACT.Identity, bias=y_nmr[:, n % NY:n % NY + 1],
                                     scale=rs_o[:, n % NY:n % NY + 1]).then_inc(yn_ready, 1)

            for j in range(NJ):
                if j < NJ - 1:
                    x2_hi_pair(j + 1)
                if j == FREE - 1:
                    tt_hi(j)
                    act.wait_ge(sum_full, 1)
                    nc.scalar.activation(colmean, O_BANK[:, :].rearrange("p (k t) -> p k t", k=KT), ACT.Copy,
                                         scale=1.0 / (L + Q_END - Q_START)).then_inc(mean_ready, 1)
                if j == FREE:
                    act.wait_ge(route_step, 2)
                    nc.scalar.activation(lexp[:, :], logit[:, :], ACT.Exp, bias=nlmax[:, 0:1],
                                         accum_out=lsum[:, 0:1]).then_inc(lexp_ready, 1)
                    act.wait_ge(bs_ready, 1)
                    nc.scalar.activation(bS_hi, bT[:, :], ACT.Copy).then_inc(bs_hi_done, 1)
                if j < FREE - 1:
                    tt_hi(j)
                for what, i in STEPS.get(j, []):
                    if what == "t":
                        tt_hi(j)
                    elif what == "finish" or j >= LATE:
                        n = ORDER.index(i if what == "finish" else 2 * j + i)
                        if n >= 2:
                            y_norm(n - 2)

        @block.vector
        def _(dve):
            nc.vector.memset(acc[:, :], 0.0).then_inc(acc_done, 1)
            nc.vector.memset(ones[:, :], 1.0).then_inc(dve_const, 1)

            def raw_waited(raw, count):
                count = count if type(count) is int else dve.to_reg(count)
                dve.wait_ge(dve_const, 1)
                dve.wait_ge(raw, count)

            def x_block(n):
                if type(n) is int:
                    return x1[:, n, :]
                return x1[:, bass.ds(n, 1), :].rearrange("p a d -> p (a d)")

            def aggregate(raw, mv, raw_sem, count, done):
                raw_waited(raw_sem, count)
                for b in range(GB):
                    last = nc.vector.bn_aggr(mv[:, b, :], raw[:, b, :])
                last.then_inc(done, 1)

            def x_row_statistics(b):
                if b < GB:
                    dve.wait_ge(x_first[b], 16)
                nc.vector.bn_stats(raw_1[:, b, :], x1[:, b, :]).then_inc(ln1_raw, 1)

            def x_aggregate(b0, b1):
                raw_waited(ln1_raw, b1)
                for b in range(b0, b1):
                    last = nc.vector.bn_aggr(mv_1[:, b, :], raw_1[:, b, :])
                last.then_inc(ln1_stats, 1)

            def normed(gg, b, n_free):
                dve.wait_ge(ln1_rstd, b + 1 if type(gg) is int else GB + 1)
                n = 4 * gg + b
                if type(gg) is int:
                    mean, rstd = mv_1[:, n, 0:1], rs_1[:, n:n + 1]
                else:
                    mean, rstd = mv_1[:, bass.ds(n, 1), 0:1].rearrange("p a c -> p (a c)"), rs_1[:, bass.ds(n, 1)]
                if n_free is not None:
                    dve.wait_ge(xt_full, n_free)
                nc.vector.tensor_scalar(xn[:, b % 2, :], x_block(n), mean, rstd,
                                        ALU.subtract, ALU.mult).then_inc(xn_ready, 1)

            def xt_lo_part(n, b, bk):
                dve.wait_ge(xt_hi_done, n)
                nc.vector.tensor_tensor(xt_lo[:, :, 1 + b * P:1 + (b + 1) * P], bk[:, :].rearrange("p (k t) -> p k t", k=KT),
                                        xt_hi[:, :, 1 + b * P:1 + (b + 1) * P].bitcast(F32), ALU.subtract).then_inc(xt_split, 1)

            def split_lo(i):
                dve.wait_ge(w_hi_done, i + 1)
                nc.vector.scalar_tensor_tensor(out=splits[i][1], in0=landing(i), scalar=splits[i][3],
                                               in1=splits[i][0].bitcast(F32), op0=ALU.mult,
                                               op1=ALU.subtract).then_inc(w_split, 1)

            x_row_statistics(0)
            x_row_statistics(1)
            x_aggregate(0, 1)
            x_row_statistics(2)
            x_aggregate(1, 2)
            normed(0, 0, None)
            x_row_statistics(3)
            x_aggregate(2, 3)
            normed(0, 1, None)
            x_aggregate(3, 4)
            xt_lo_part(1, 0, T_BANK[0])
            normed(0, 2, 1)
            xt_lo_part(2, 1, T_BANK[1])
            normed(0, 3, 2)
            xt_lo_part(3, 2, T_BANK[0])
            split_lo(0)
            xt_lo_part(4, 3, T_BANK[1])
            dve.wait_ge(edge_in, 16)
            nc.vector.bn_stats(edge_bn[:, :], edge[:, :]).then_inc(edge_step, 1)
            dve.wait_ge(edge_step, 1)
            nc.vector.bn_aggr(edge_mv[:, :], edge_bn[:, :]).then_inc(edge_n, 1)
            split_lo(1)
            dve.wait_ge(edge_rstd, 1)
            nc.vector.tensor_scalar(edge[:, :], edge[:, :], edge_mv[:, 0:1], edge_bn[:, 1:2],
                                    ALU.subtract, ALU.mult).then_inc(edge_step, 1)
            split_lo(2)
            dve.wait_ge(edge_hi_done, 1)
            nc.vector.tensor_tensor(edge_lo[:, :, :], V_BANK[:, 0:KT * NR].rearrange("p (k t) -> p k t", k=KT),
                                    edge_hi[:, :, :].bitcast(F32), ALU.subtract).then_inc(edge_split, 1)
            split_lo(3)
            for i in range(GB, NW):
                split_lo(i)
            dve.wait_ge(pb_in, 16)
            dve.wait_ge(bias_done, 2)

            def conv_lo(m, n):
                dve.wait_ge(qkv_hi_done, n)
                nc.vector.scalar_tensor_tensor(
                    out=qkv_lo[:, m, :], in0=CONV_BANK[m][:, :], scalar=conv_bias[:, CH[m]:CH[m] + 1],
                    in1=qkv_hi[:, m, :].bitcast(F32), op0=ALU.add, op1=ALU.subtract).then_inc(qkv_split, 1)

            def row_max(g, p, h):
                dve.wait_ge(s_full, 16 * g + (2 * p + h + 1))
                nc.vector.tensor_reduce(nmax[:, p % 2, 4 * h:4 * h + 4], S_BANK[h][:, :].rearrange("p (a k) -> p a k", a=4),
                                        op=ALU.max, axis=AX_X, negate=True).then_inc(nmax_ready, 1)

            def values_out(g, u):
                dve.wait_ge(v_full, 8 * g + (u + 1))
                nc.vector.tensor_copy(vh[:, u // 2, (u % 2) * 512:(u % 2) * 512 + 512], VH_BANK[u % 3][:, :]).then_inc(vh_dve, 1)

            def row_inv(g, p, h):
                dve.wait_ge(exp_done, 16 * g + (2 * p + h + 1))
                nc.vector.reciprocal(rinv[:, p % 2, 4 * h:4 * h + 4], rsum[:, p % 2, 4 * h:4 * h + 4]).then_inc(rinv_ready, 1)

            def probs_back(g, p, h):
                dve.wait_ge(t_full, 16 * g + (2 * p + h + 1))
                nc.vector.tensor_copy(pT[:, 4 * h:4 * h + 4, :], T_BANK[h][:, :].rearrange("p (a k) -> p a k", a=4)
                                      ).then_inc(ptA_ready if h == 0 else ptB_ready, 1)

            def context_lo(g, p):
                dve.wait_ge(ctx_hi_done, 8 * g + (p + 1))
                nc.vector.scalar_tensor_tensor(out=ctx_lo[:, p % 2, :], in0=V_BANK[:, :], scalar=bv_sb[:, p:p + 1],
                                               in1=ctx_hi[:, p % 2, :].bitcast(F32), op0=ALU.add,
                                               op1=ALU.subtract).then_inc(ctx_split, 1)

            def attn_row_statistics(b):
                nc.vector.bn_stats(raw_o[:, b, :], rows[:, b, :]).then_inc(lno_raw, 1)

            def attn_statistics(n):
                for b in range(GB):
                    attn_row_statistics(b)
                aggregate(raw_o, mv_o, lno_raw, 4 * n, lno_stats)

            def attn_norm(n):
                dve.wait_ge(lno_rstd, n)
                for b in range(GB):
                    nc.vector.tensor_scalar(rows[:, b, :], rows[:, b, :], mv_o[:, b, 0:1], rs_o[:, b:b + 1],
                                            ALU.subtract, ALU.mult).then_inc(on_ready, 1)

            def x1_statistics(n, before, blocks=range(GB)):
                for b in blocks:
                    dve.wait_ge(x1_ready, before + (b + 1))
                    nc.vector.bn_stats(raw_2[:, b, :], x_block(before + b)).then_inc(ln2_raw, 1)
                if blocks[-1] == GB - 1:
                    aggregate(raw_2, mv_2, ln2_raw, 4 * n, ln2_stats)

            def x1_averaged(n, before, blocks=range(GB)):
                dve.wait_ge(ln2_kept, 3 * n)
                for b in blocks:
                    dve.wait_ge(acc_done, before + (b + 1))
                    nc.vector.scalar_tensor_tensor(out=acc[:, :], in0=x_block(before + b), scalar=row_weight(before + b),
                                                   in1=acc[:, :], op0=ALU.mult, op1=ALU.add).then_inc(acc_done, 1)

            def row_weight(n):
                if type(n) is int:
                    return avg_w[:, n:n + 1]
                return avg_w[:, bass.ds(n, 1)]

            def wT_lo_part(k):
                dve.wait_ge(wT_hi_done, k + 1)
                nc.vector.tensor_tensor(wT_lo[:, k, :], BASE_BANK[k % 2][:, :], wT_hi[:, k, :].bitcast(F32),
                                        ALU.subtract).then_inc(base_free, 1)

            def group(g, first, last):
                for p in range(NP):
                    if p >= 1:
                        row_inv(g, p - 1, 1)
                    for b in range(0, 2):
                        if not last and X_SLOTS[b] == p - 1:
                            xt_lo_part(4 * g + (GB + b + 1), b, X_BANK[b])
                    if p >= 2:
                        context_lo(g, p - 2)
                    for b in range(2, GB):
                        if not last and X_SLOTS[b] == p - 1:
                            xt_lo_part(4 * g + (GB + b + 1), b, X_BANK[b])
                    if p == 0:
                        values_out(g, 1)
                        if not first:
                            attn_statistics(g)
                        values_out(g, 3)
                    row_max(g, p, 0)
                    row_max(g, p, 1)
                    if p == 0:
                        values_out(g, 4)
                        values_out(g, 5)
                        values_out(g, 7)
                    if p >= 1:
                        probs_back(g, p - 1, 0)
                        probs_back(g, p - 1, 1)
                    row_inv(g, p, 0)
                    if p == 0 and not first:
                        attn_norm(g)
                    if p == 2 and not first:
                        x1_statistics(g, 4 * g - 4, range(0, 2))
                    if p == (3 if last else 4) and not first:
                        x1_statistics(g, 4 * g - 4, range(2, 4))
                    if last and p == NP - 1:
                        wT_lo_part(0)
                        wT_lo_part(1)
                    if last and p in (4, 5, 6):
                        x1_averaged(g, 4 * g - 4, range(p - 4, p - 3))
                    for b in range(GB):
                        if not last and X_SLOTS[b] == p + 1:
                            normed(g + 1, b, 4 * g + (b + 3))
                row_inv(g, NP - 1, 1)
                context_lo(g, NP - 2)
                if last:
                    wT_lo_part(2)
                probs_back(g, NP - 1, 0)
                probs_back(g, NP - 1, 1)
                if not last:
                    conv_lo(0, 3 * g + 4)
                else:
                    x2_norm(0)
                    wT_lo_part(3)
                    x2_norm(1)
                    dve.wait_ge(aT_hi_done, 1)
                    nc.vector.tensor_tensor(aT_lo[:, :, :], AT_BANK[:, :].rearrange("p (k c) -> p k c", k=KT),
                                            aT_hi[:, :, :].bitcast(F32), ALU.subtract).then_inc(tt_split, 1)
                    x1_averaged(g, 4 * g - 4, range(3, 4))
                context_lo(g, NP - 1)
                if not last:
                    if not first:
                        x1_averaged(g, 4 * g - 4)
                    conv_lo(1, 3 * g + 5)
                if last:
                    x2_lo(0, 0)
                    x2_lo(0, 1)
                dve.wait_ge(o_hi_done, g + 1)
                nc.vector.scalar_tensor_tensor(out=o_lo[:, :], in0=O_BANK[:, :], scalar=bo_sb[:, 0:1],
                                               in1=o_hi[:, :].bitcast(F32), op0=ALU.add, op1=ALU.subtract).then_inc(o_split, 1)
                if last:
                    x2_norm(2)
                    x2_norm(3)
                if not first:
                    dve.wait_ge(x1_ready, 4 * g)
                for b in range(GB):
                    dve.wait_ge(pj_full, 4 * g + (b + 1))
                    nc.vector.tensor_tensor(rows[:, b, :], PJ_BANK[b % 3][:, :], pb_sb[:, :], ALU.add).then_inc(pj_evac, 1)
                    if b == 0 and not last:
                        conv_lo(2, 3 * g + 6)
                dve.wait_ge(pj_evac, 4 * g + GB)

            def x2_lo(j, b):
                dve.wait_ge(x2_hi_done, 2 * j + b + 1)
                nc.vector.tensor_tensor(x2T_lo[:, j % 2, :, b * P:(b + 1) * P], X2_BANK[b][:, :].rearrange("p (k t) -> p k t", k=KT),
                                        x2T_hi[:, j % 2, :, b * P:(b + 1) * P].bitcast(F32), ALU.subtract).then_inc(x2_split, 1)

            def x2_norm(n):
                dve.wait_ge(ln2_kept, 3 * (n // GB + 1))
                if n >= 2:
                    dve.wait_ge(x2_full, n - 1)
                nc.vector.tensor_scalar(x2n[:, n % 2, :], x1[:, n, :], stats2[:, n, 0:1], stats2[:, n, 1:2],
                                        ALU.subtract, ALU.mult).then_inc(x2_ready, 1)

            conv_lo(0, 1)
            for g in range(1, NG):
                dve.wait_ge(x_rest[g - 1], 16)
                for b in range(g * GB, (g + 1) * GB):
                    x_row_statistics(b)
                if g == 1:
                    conv_lo(1, 2)
            x_aggregate(GB, NBLK)
            conv_lo(2, 3)
            group(0, True, False)
            with dve.Fori(1, NG - 1) as g:
                group(g, False, False)
            group(NG - 1, False, True)
            dve.wait_ge(ffn_in, 16 * N_FFN)

            def base_out(n):
                dve.wait_ge(base_full, n + 1)
                nc.vector.tensor_tensor(base[:, n, :], BASE_BANK[n % 2][:, :], y_bias[:, :], ALU.add).then_inc(base_free, 1)

            def tt_lo(j):
                dve.wait_ge(tt_hi_done, j + 1)
                t = slice(2 * j * P, 2 * (j + 1) * P)
                nc.vector.tensor_tensor(tT_lo[:, t], TT_BANK[:, 0:2 * P], tT_hi[:, t].bitcast(F32), ALU.subtract).then_inc(tt_split, 1)

            def y_sum(n):
                dve.wait_ge(y_full, n + 1)
                nc.vector.tensor_tensor(base[:, n, :], Y_BANK[n % 2][:, :], base[:, n, :], ALU.add).then_inc(y_ready, 1)

            def y_statistics(n):
                if ORDER[n] < 2 * LATE:
                    dve.wait_ge(y_ready, ORDER[n] + 1)
                else:
                    dve.wait_ge(base_free, KT + ORDER[n] + 1)
                nc.vector.bn_stats(raw_o[:, n % NY, :], base[:, ORDER[n], :]).then_inc(y_raw, 1)

            def y_aggregate(n):
                raw_waited(y_raw, n + 1)
                nc.vector.bn_aggr(mv_o[:, n % NY, :], raw_o[:, n % NY, :]).then_inc(y_stats, 1)

            def y_scale(n):
                s = n % NY
                dve.wait_ge(y_rstd, n + 1)
                nc.vector.scalar_tensor_tensor(out=y_nmr[:, s:s + 1], in0=mv_o[:, s, 0:1], scalar=-1.0, in1=rs_o[:, s:s + 1],
                                               op0=ALU.mult, op1=ALU.mult).then_inc(y_scaled, 1)

            def router_sum():
                dve.wait_ge(avg_step, 1)
                nc.vector.tensor_reduce(avg_ms[:, :], avg_m[:, :], op=ALU.add, axis=AX_X).then_inc(avg_step, 1)
                dve.wait_ge(avg_step, 2)
                dve.wait_ge(acc_done, NBLK + 1)
                nc.vector.tensor_scalar(acc[:, :], acc[:, :], avg_ms[:, 0:1], None, ALU.subtract).then_inc(avg_step, 1)

            def router_softmax():
                dve.wait_ge(logit_full, 1)
                nc.vector.tensor_tensor(logit[:, :], O_BANK[:, 0:NE], r_bias[:, :], ALU.add).then_inc(route_step, 1)
                dve.wait_ge(route_step, 1)
                nc.vector.tensor_reduce(nlmax[:, :], logit[:, :], op=ALU.max, axis=AX_X, negate=True).then_inc(route_step, 1)
                dve.wait_ge(lexp_ready, 1)
                nc.vector.reciprocal(lrec[:, :], lsum[:, :]).then_inc(route_step, 1)
                dve.wait_ge(expert_ready, 1)
                nc.vector.tensor_tensor(lpick[:, :], lexp[:, :], expert[:, :], ALU.mult).then_inc(route_step, 1)
                dve.wait_ge(route_step, 4)
                nc.vector.tensor_reduce(route[:, :], lpick[:, :], op=ALU.add, axis=AX_X).then_inc(route_step, 1)
                dve.wait_ge(route_step, 5)
                nc.vector.tensor_scalar(route2[:, :], route[:, :], lrec[:, 0:1], LORA_SCALING, ALU.mult, ALU.mult).then_inc(route_step, 1)
                dve.wait_ge(route_step, 6)
                dve.wait_ge(bT_ready, 1)
                nc.vector.tensor_scalar(bT[:, :], bT[:, :], route2[:, 0:1], None, ALU.mult).then_inc(bs_ready, 1)
                dve.wait_ge(bs_hi_done, 1)
                nc.vector.tensor_tensor(bS_lo, bT[:, :], bS_hi.bitcast(F32), ALU.subtract).then_inc(bs_split, 1)

            base_out(0)
            for j in range(NJ):
                if j < NJ - 1:
                    x2_lo(j + 1, 0)
                    x2_lo(j + 1, 1)
                if j < NJ - 2:
                    x2_norm(2 * j + 4)
                    x2_norm(2 * j + 5)
                if j == 0:
                    attn_statistics(NG)
                if j == 2:
                    x1_statistics(NG, 4 * NG - 4, range(2, 4))
                if j == 3:
                    x1_averaged(NG, 4 * NG - 4, range(0, 2))
                if j < FREE:
                    if j > 0:
                        base_out(2 * j)
                    base_out(2 * j + 1)
                    if j == 0:
                        attn_norm(NG)
                    if j == 1:
                        x1_statistics(NG, 4 * NG - 4, range(0, 2))
                    if j == 3:
                        x1_averaged(NG, 4 * NG - 4, range(2, 4))
                        router_sum()
                    tt_lo(j)
                for what, i in STEPS.get(j, []):
                    if what == "t":
                        tt_lo(j)
                    elif what == "base" and j < LATE:
                        base_out(2 * j + i)
                        if i == 0:
                            router_softmax()
                    else:
                        n = ORDER.index(i if what == "finish" else 2 * j + i)
                        if n >= 2:
                            y_scale(n - 2)
                        if what == "finish":
                            y_sum(i)
                        else:
                            base_out(2 * j + i)
                        if n >= 1:
                            y_aggregate(n - 1)
                        y_statistics(n)
            y_aggregate(NBLK - 1)
            for i, n in enumerate(range(ON_POOL, NBLK)):
                dve.wait_ge(y_rstd, n + 1)
                row = base[:, ORDER[n], :]
                nc.vector.tensor_scalar(row, row, mv_o[:, n % NY, 0:1], rs_o[:, n % NY:n % NY + 1],
                                        ALU.subtract, ALU.mult).then_inc(last_yn, 1)
                dve.wait_ge(last_yn, i + 1)
                nc.vector.tensor_tensor(row, row, x1[:, ORDER[n], :], ALU.add).then_inc(last_res, 1)

        @block.tensor
        def _(pe):
            def three(bank_ap, lhs_hi, lhs_lo, rhs_hi, rhs_lo, start, stop):
                nc.tensor.matmul(bank_ap, lhs_hi, rhs_hi, start=start, stop=False)
                nc.tensor.matmul(bank_ap, lhs_hi, rhs_lo, start=False, stop=False)
                return nc.tensor.matmul(bank_ap, lhs_lo, rhs_hi, start=False, stop=stop)

            def x_transposes(bk, b):
                for k in range(KT):
                    last = nc.tensor.transpose(bk[:, k * P:(k + 1) * P], xn[:, b % 2, k * P:(k + 1) * P], ident[:, :])
                last.then_inc(xt_full, 1)

            pe.wait_ge(pool_const, 4)
            for b in range(GB):
                pe.wait_ge(xn_ready, b + 1)
                if b >= 2:
                    pe.wait_ge(xt_split, b - 1)
                x_transposes(T_BANK[b % 2], b)

            def convolve(m, gg, before, part=range(NK)):
                if m == 0 and part[0] == 0:
                    pe.wait_ge(xt_split, 4 * gg + GB)
                if before is not None and part[0] == 0:
                    pe.wait_ge((q_ready, k_ready, ctx_split)[m], 8 * before)
                for i in part:
                    k = CONV_ORDER[i]
                    if before is None and m == 0 and i % 2 == 0:
                        pe.wait_ge(w_split, i // 2 + 1)
                    if m == 0 and i == KT:
                        pe.wait_ge(halo_done, 2 * gg + 2)
                    c = slice(CH[m] * P, (CH[m] + 1) * P)
                    t = slice(k // KT, k // KT + GT)
                    done = three(CONV_BANK[m][:, :], cw_hi[:, k, c], cw_lo[:, k, c], xt_hi[:, k % KT, t],
                                 xt_lo[:, k % KT, t], i == 0, i == NK - 1)
                if part[-1] == NK - 1:
                    done.then_inc(conv_full, 1)

            def project_qk(g, p):
                if p == 0:
                    pe.wait_ge(qkv_split, 3 * g + 3)
                else:
                    pe.wait_ge(q_ready, 8 * g + p)
                    pe.wait_ge(k_ready, 8 * g + p)
                c = slice(p * P, (p + 1) * P)
                three(Q_BANK[:, :], wq_hi[:, c], wq_lo[:, c], qkv_hi[:, 1, :], qkv_lo[:, 1, :], True, True).then_inc(q_full, 1)
                three(K_BANK[:, :], wk_hi[:, c], wk_lo[:, c], qkv_hi[:, 2, :], qkv_lo[:, 2, :], True, True).then_inc(k_full, 1)

            def scores(g, p, first):
                pe.wait_ge(q_ready, 8 * g + (p + 1))
                pe.wait_ge(k_ready, 8 * g + (p + 1))
                if p > 0:
                    pe.wait_ge(exp_done, 16 * g + 2 * p)
                elif not first:
                    pe.wait_ge(pj_evac, 4 * g)
                for h in range(2):
                    nc.tensor.matmul(S_BANK[h][:, :], ident16[:, :], mask16[:, :], start=True, stop=False)
                for b in range(GB):
                    t = slice(b * P, (b + 1) * P)
                    for h in range(2):
                        r = slice(E * h, E * h + E)
                        done = nc.tensor.matmul(S_BANK[h][:, t], qT[r, p % 2, t], kT[r, p % 2, t],
                                                start=False, stop=b == GB - 1)
                        if b == GB - 1:
                            done.then_inc(s_full, 1)

            def transpose_probs(g, p):
                for h in range(2):
                    pe.wait_ge(pn_ready, 16 * g + (2 * p + h + 1))
                    if h == 0 and p > 0:
                        pe.wait_ge(ptA_ready, 8 * g + p)
                    if h == 1 and p > 0:
                        pe.wait_ge(ptB_ready, 8 * g + p)
                    for j in range(4):
                        last = nc.tensor.transpose(T_BANK[h][:, j * P:(j + 1) * P], probs[:, p % 2, 4 * h + j, :], ident[:, :])
                    last.then_inc(t_full, 1)

            def context(g, p):
                if p > 0:
                    pe.wait_ge(ctx_split, 8 * g + p)
                pe.wait_ge(ptA_ready, 8 * g + (p + 1))
                pe.wait_ge(ptB_ready, 8 * g + (p + 1))
                for b in range(GB):
                    for h in range(2):
                        last = nc.tensor.matmul(V_BANK[E * h:E * h + E, b * P:(b + 1) * P],
                                                vh[:, b, (2 * p + h) * E:(2 * p + h + 1) * E],
                                                pT[:, 4 * h + b, :], start=True, stop=True)
                last.then_inc(pv_full, 1)

            def project_out(g, p, first):
                pe.wait_ge(ctx_split, 8 * g + (p + 1))
                if p == 0 and not first:
                    pe.wait_ge(o_split, g)
                last = three(O_BANK[:, :], wo_hi[:, p, :], wo_lo[:, p, :], ctx_hi[:, p % 2, :], ctx_lo[:, p % 2, :],
                             p == 0, p == NP - 1)
                last.then_inc(o_used if p < NP - 1 else oacc_full, 1)

            def values(g, u, first):
                if u == 2:
                    pe.wait_ge(qkv_split, 3 * g + 3)
                if u == 0:
                    pe.wait_ge(qkv_split, 3 * g + 1)
                    if not first:
                        pe.wait_ge(ptA_ready, 8 * g)
                        pe.wait_ge(ptB_ready, 8 * g)
                if u >= 3:
                    if u - 3 in VH_ACT:
                        pe.wait_ge(vh_act, len(VH_ACT) * g + (VH_ACT.index(u - 3) + 1))
                    else:
                        pe.wait_ge(vh_dve, len(VH_DVE) * g + (VH_DVE.index(u - 3) + 1))
                t = slice((u // 2) * P, (u // 2 + 1) * P)
                c = slice((u % 2) * 512, (u % 2) * 512 + 512)
                three(VH_BANK[u % 3][:, :], qkv_hi[:, 0, t], qkv_lo[:, 0, t], wv_hi[:, c], wv_lo[:, c],
                      True, True).then_inc(v_full, 1)

            def x_block_transposes(g, p):
                for b in range(GB):
                    if X_SLOTS[b] == p:
                        pe.wait_ge(xn_ready, 4 * g + (GB + b + 1))
                        if b >= 2:
                            pe.wait_ge((q_ready, k_ready)[b - 2], 8 * g + 8)
                        x_transposes(X_BANK[b], b)

            def w_transposes(k):
                if k >= 2:
                    pe.wait_ge(base_free, k - 1)
                else:
                    pe.wait_ge(ffn_in, 16 * N_FFN)
                    pe.wait_ge((q_ready, k_ready)[k], 8 * NG)
                for t in range(KT):
                    done = nc.tensor.transpose(BASE_BANK[k % 2][:, t * P:(t + 1) * P], w_raw[:, t, k * P:(k + 1) * P], ident[:, :])
                done.then_inc(wT_full, 1)

            def x2_transposes(j):
                for b in range(2):
                    pe.wait_ge(x2_ready, 2 * j + (b + 1))
                    for k in range(KT):
                        last = nc.tensor.transpose(X2_BANK[b][:, k * P:(k + 1) * P], x2n[:, b, k * P:(k + 1) * P], ident[:, :])
                    last.then_inc(x2_full, 1)

            def base_product(j, s, b, with_lora=False):
                pe.wait_ge(base_free, 2 * j + (b + 3))
                for k in range(KT):
                    t = slice(b * P, (b + 1) * P)
                    last = three(BASE_BANK[b][:, :], x2T_hi[:, s, k, t], x2T_lo[:, s, k, t], wT_hi[:, k, :], wT_lo[:, k, :],
                                 k == 0, k == KT - 1 and not with_lora)
                if with_lora:
                    pe.wait_ge(tt_split, j + 2)
                    t = slice((2 * j + b) * P, (2 * j + b + 1) * P)
                    last = three(BASE_BANK[b][:, :], tT_hi[:, t], tT_lo[:, t], bS_hi, bS_lo, False, True)
                last.then_inc(base_full, 1)

            def lora_b_transposes():
                pe.wait_ge(base_free, 4)
                for t in range(KT):
                    done = nc.tensor.transpose(BT_BANK[:, t * P:(t + 1) * P], b_raw[:, t, :, :].rearrange("p e r -> p (e r)"), ident[:, :])
                done.then_inc(bT_full, 1)

            def lora_a_and_router_transposes():
                pe.wait_ge(base_free, 3)
                for k in range(KT):
                    done = nc.tensor.transpose(AT_BANK[:, k * P:(k + 1) * P], a_raw[:, k * P:(k + 1) * P], ident[:, :])
                done.then_inc(aT_full, 1)
                pe.wait_ge(exp_done, 16 * NG)
                for k in range(KT):
                    done = nc.tensor.transpose(RT_BANK[:, k * NE:(k + 1) * NE], r_raw[:, k * P:(k + 1) * P], ident[0:NE, 0:NE])
                done.then_inc(rT_full, 1)

            def group(g, first, last):
                for u in range(2 * GB):
                    values(g, u, first)
                    after = [1, 2] if first else QK_AFTER
                    if u in after:
                        project_qk(g, after.index(u))
                    if u == S_AFTER:
                        scores(g, 0, first)
                project_qk(g, 2)
                for p in range(1, NP):
                    scores(g, p, first)
                    if p == 1:
                        pe.wait_ge(vh_act, len(VH_ACT) * (g + 1))
                        pe.wait_ge(vh_dve, len(VH_DVE) * (g + 1))
                    for b in range(GB):
                        if not last and X_SLOTS[b] == p - 1 and X_BANK[b] is T_BANK[0]:
                            pe.wait_ge(xt_split, 4 * g + (GB + b + 1))
                    transpose_probs(g, p - 1)
                    if p >= 2:
                        project_out(g, p - 2, first)
                    if p + 2 < NP:
                        project_qk(g, p + 2)
                    if not last and p == NP - 2:
                        x_block_transposes(g, p)
                    if not last and p == NP - 1:
                        convolve(0, g + 1, g + 1, CONV_PARTS[0])
                    if last and p == NP - 2:
                        w_transposes(0)
                        w_transposes(1)
                    context(g, p - 1)
                    if last and p == NP - 1:
                        w_transposes(2)
                        w_transposes(3)
                    if not last and p < NP - 2:
                        x_block_transposes(g, p)
                if not last:
                    convolve(0, g + 1, g + 1, CONV_PARTS[1])
                transpose_probs(g, NP - 1)
                if not last:
                    convolve(0, g + 1, g + 1, CONV_PARTS[2])
                project_out(g, NP - 2, first)
                if last:
                    lora_a_and_router_transposes()
                context(g, NP - 1)
                if not last:
                    convolve(1, g + 1, g + 1)
                else:
                    lora_b_transposes()
                    x2_transposes(0)
                project_out(g, NP - 1, first)
                if not last:
                    convolve(2, g + 1, g + 1)
                if last:
                    pe.wait_ge(base_free, KT)
                    pe.wait_ge(tt_split, 1)
                    pe.wait_ge(x2_split, 2)
                    base_product(0, 0, 0)
                    pe.wait_ge(rT_ready, 1)
                pe.wait_ge(exp_done, 16 * g + 16)
                pe.wait_ge(o_split, g + 1)
                for b in range(GB):
                    if b >= 3:
                        pe.wait_ge(pj_evac, 4 * g + (b - 2))
                    t = slice(b * P, (b + 1) * P)
                    three(PJ_BANK[b % 3][:, :], o_hi[:, t], o_lo[:, t], pj_hi[:, :], pj_lo[:, :], True, True).then_inc(pj_full, 1)

            convolve(0, 0, None, range(0, 2))
            pe.wait_ge(edge_step, 2)
            for k in range(KT):
                last = nc.tensor.transpose(V_BANK[:, k * NR:(k + 1) * NR], edge[:, k * P:(k + 1) * P],
                                           ident[0:NR, 0:NR])
            last.then_inc(edge_full, 1)
            pe.wait_ge(small_in, 16 * N_SMALL)
            nc.tensor.transpose(S_BANK[0][:, 0:NB], bias_rows[:, :], ident[0:NB, 0:NB]).then_inc(bias_full, 1)
            convolve(0, 0, None, range(2, NK))
            convolve(1, 0, None)
            pe.wait_ge(edge_split, 1)
            convolve(2, 0, None)
            pe.wait_ge(bias_done, 2)
            pe.wait_ge(dve_const, 1)
            pe.wait_ge(pool_const, 10)
            pe.wait_ge(w_split, NW)
            group(0, True, False)
            with pe.Fori(1, NG - 1) as g:
                group(g, False, False)
            group(NG - 1, False, True)

            def tt_product(j, s):
                pe.wait_ge(tt_split, j + 1)
                for k in range(KT):
                    last = three(TT_BANK[:, 0:2 * P], aT_hi[:, k, :], aT_lo[:, k, :], x2T_hi[:, s, k, :], x2T_lo[:, s, k, :],
                                 k == 0, k == KT - 1)
                last.then_inc(tt_full, 1)

            def lora_product(n):
                if n == 0:
                    pe.wait_ge(bs_split, 1)
                else:
                    pe.wait_ge(tt_split, n // 2 + 2)
                if n >= 2:
                    pe.wait_ge(y_ready, n - 1)
                t = slice(n * P, (n + 1) * P)
                three(Y_BANK[n % 2][:, :], tT_hi[:, t], tT_lo[:, t], bS_hi, bS_lo, True, True).then_inc(y_full, 1)

            pe.wait_ge(bT_ready, 1)
            for j in range(FREE):
                pe.wait_ge(x2_split, 2 * j + 2)
                x2_transposes(j + 1)
                if j > 0:
                    base_product(j, j % 2, 0)
                base_product(j, j % 2, 1)
                tt_product(j, j % 2)
            pe.wait_ge(pj_evac, 4 * NG)
            for j in range(FREE, NJ):
                pe.wait_ge(x2_split, 2 * j + 2)
                if j < NJ - 1:
                    x2_transposes(j + 1)
                if j == FREE:
                    pe.wait_ge(avg_step, 3)
                    for k in range(KT):
                        last = nc.tensor.matmul(O_BANK[:, k * P:(k + 1) * P], acc[:, k * P:(k + 1) * P], ones[:, :], start=True, stop=True)
                    last.then_inc(sum_full, 1)
                for what, i in STEPS[j]:
                    if what == "base":
                        base_product(j, j % 2, i, j >= LATE)
                        if j == FREE and i == 0:
                            pe.wait_ge(mean_ready, 1)
                            for k in range(KT):
                                last = nc.tensor.matmul(O_BANK[:, 0:NE], colmean[:, k, :], rT[:, k, :], start=k == 0, stop=k == KT - 1)
                            last.then_inc(logit_full, 1)
                    elif what == "t":
                        tt_product(j, j % 2)
                    else:
                        lora_product(i)


_INS = ['L0_attn_inputs', 'L0_attn_conv_w', 'L0_attn_conv_b', 'L0_attn_wq', 'L0_attn_bq', 'L0_attn_wk', 'L0_attn_bk',
        'L0_attn_wv', 'L0_attn_bv', 'L0_attn_wo', 'L0_attn_bo', 'L0_attn_proj_w', 'L0_attn_proj_b', 'L0_ffn_W',
        'L0_ffn_b', 'L0_ffn_A', 'L0_ffn_B', 'L0_ffn_router_W', 'L0_ffn_router_b']
_OUTS = [((1, 2048, 512), 'float32')]


def kernel(**inputs):
    import numpy as _np
    import concourse.bacc as _bacc
    from concourse import mybir as _mybir
    from concourse.bass_utils import run_bass_kernel_spmd as _run

    nc = _bacc.Bacc("TRN2", target_bir_lowering=False, num_devices=1)
    arrays, args = {}, []
    for name in _INS:
        a = _np.ascontiguousarray(inputs[name])
        arrays[f"in_{name}_dram"] = a
        args.append(nc.dram_tensor(f"in_{name}_dram", a.shape, _mybir.dt.from_np(a.dtype), kind="ExternalInput").ap())
    for i, (shape, dtype) in enumerate(_OUTS):
        dt = _mybir.dt.from_np(_np.dtype(dtype))
        args.append(nc.dram_tensor(f"out_{i}_dram", shape, dt, kind="ExternalOutput").ap())
    attention_ffn_sandwich(nc, *args)
    r = _run(nc, [arrays], core_ids=[0])
    return r.results[0]["out_0_dram"]
```
